# Optimizing a Trainium2 kernel written in Bass

```python
import numpy as np
import jax
import jax.numpy as jnp

def _softmax(x, axis=-1):
    return jax.nn.softmax(x, axis=axis)

def _gelu(x):
    return jax.nn.gelu(x, approximate=True)

def _silu(x):
    return jax.nn.silu(x)

def _sigmoid(x):
    return jax.nn.sigmoid(x)

def _layernorm(x, axis=-1, eps=1e-05):
    m = jnp.mean(x, axis=axis, keepdims=True)
    v = jnp.var(x, axis=axis, keepdims=True)
    return (x - m) / jnp.sqrt(v + eps)

def _scatter_add(tgt, idx, src, axis=0):
    return tgt.at[idx].add(src)

def _segment_sum(src, seg, n):
    return jax.ops.segment_sum(src, seg, n)
kernel_name = 'mk_vit_tower_d2_tok_img768_r4_309dd5'

def setup_inputs(seed: int=0):
    np.random.seed(seed)
    _w = jnp.asarray

    def _rec_inputs():
        import jax
        import jax.numpy as jnp
        _rk = jax.random.key(seed)
        x = -0.00016672 + 0.999947 * jax.random.normal(jax.random.fold_in(_rk, 1), (16, 3, 96, 96), jnp.float32)
        return x
    x = _rec_inputs()

    def _L0_tok_setup():
        import jax, jax.numpy as jnp
        import numpy as np
        IMG = 96
        PATCH = 16
        C = 3
        PROJ = 192
        NUM_PATCHES = (IMG // PATCH) ** 2
        FLAT = C * PATCH * PATCH
        BATCH = 64

        def _patchify(x):
            B, c, H, Wd = x.shape
            hp, wp = (H // PATCH, Wd // PATCH)
            x = x.reshape(B, c, hp, PATCH, wp, PATCH)
            x = x.transpose(0, 2, 4, 1, 3, 5)
            return x.reshape(B, hp * wp, c * PATCH * PATCH)
        key = jax.random.key(seed)
        k1, k2, k3, k4 = jax.random.split(key, 4)
        x = jax.random.normal(k1, (BATCH, C, IMG, IMG), dtype=jnp.float32)
        bound = 1.0 / np.sqrt(FLAT)
        W = jax.random.uniform(k2, (PROJ, FLAT), minval=-bound, maxval=bound, dtype=jnp.float32)
        b = jax.random.uniform(k3, (PROJ,), minval=-bound, maxval=bound, dtype=jnp.float32)
        pos_emb = jax.random.normal(k4, (NUM_PATCHES, PROJ), dtype=jnp.float32)
        return {'x': x, 'W': W, 'b': b, 'pos_emb': pos_emb}
    _L0_tok_all = _L0_tok_setup()
    _L0_tok_in = {k: v for k, v in _L0_tok_all.items() if k in ('W', 'b', 'pos_emb')}
    del _L0_tok_all

    def _L0_attn_setup():
        import jax, jax.numpy as jnp
        import numpy as np
        D_MODEL = 192
        NUM_HEADS = 3
        HEAD_DIM = D_MODEL // NUM_HEADS
        GN_EPS = 1e-05

        def _xavier(key, shape, gain=0.5):
            fan_in, fan_out = (shape[1], shape[0])
            a = gain * np.sqrt(6.0 / (fan_in + fan_out))
            return jax.random.uniform(key, shape, jnp.float32, -a, a)
        key = jax.random.key(seed)
        ks = jax.random.split(key, 5)
        x = jax.random.normal(ks[0], (4, 512, D_MODEL), jnp.float32)
        Wq = _xavier(ks[1], (D_MODEL, D_MODEL))
        Wk = _xavier(ks[2], (D_MODEL, D_MODEL))
        Wv = _xavier(ks[3], (D_MODEL, D_MODEL))
        Wo = _xavier(ks[4], (D_MODEL, D_MODEL))
        gammas = jnp.array([0.9, 0.95, 0.99], jnp.float32)
        gn_weight = jnp.ones((D_MODEL,), jnp.float32)
        gn_bias = jnp.zeros((D_MODEL,), jnp.float32)
        return {'x': x, 'Wq': Wq, 'Wk': Wk, 'Wv': Wv, 'Wo': Wo, 'gammas': gammas, 'gn_weight': gn_weight, 'gn_bias': gn_bias}
    _L0_attn_all = _L0_attn_setup()
    _L0_attn_in = {k: v for k, v in _L0_attn_all.items() if k in ('Wq', 'Wk', 'Wv', 'Wo', 'gammas', 'gn_weight', 'gn_bias')}
    del _L0_attn_all

    def _L0_ffn_setup():
        import jax, jax.numpy as jnp
        import numpy as np
        D_MODEL = 192
        D_FF = 768
        NUM_EXPERTS = 8
        EXPERT_CAPACITY = 256
        key = jax.random.key(seed)
        k0, k1, k2, k3 = jax.random.split(key, 4)
        hidden_states = jax.random.normal(k0, (2, 256, D_MODEL), dtype=jnp.float32)
        router_w = jax.random.normal(k1, (D_MODEL, NUM_EXPERTS), dtype=jnp.float32) * D_MODEL ** (-0.5)
        wi = jax.random.normal(k2, (NUM_EXPERTS, D_MODEL, D_FF), dtype=jnp.float32) * D_MODEL ** (-0.5)
        wo = jax.random.normal(k3, (NUM_EXPERTS, D_FF, D_MODEL), dtype=jnp.float32) * D_FF ** (-0.5)
        return {'hidden_states': hidden_states, 'router_w': router_w, 'wi': wi, 'wo': wo}
    _L0_ffn_all = _L0_ffn_setup()
    _L0_ffn_in = {k: v for k, v in _L0_ffn_all.items() if k in ('router_w', 'wi', 'wo')}
    del _L0_ffn_all

    def _L1_attn_setup():
        import jax, jax.numpy as jnp
        import numpy as np
        import math
        MAX_REL = 32
        key = jax.random.key(seed)
        ks = jax.random.split(key, 6)
        B, S, D = (2, 512, 192)
        H = 12
        dk = D // H
        s = 1.0 / math.sqrt(D)
        return {'x': jax.random.normal(ks[0], (B, S, D), jnp.float32), 'Wq': jax.random.normal(ks[1], (D, D), jnp.float32) * s, 'bq': jnp.zeros((D,), jnp.float32), 'Wk': jax.random.normal(ks[2], (D, D), jnp.float32) * s, 'bk': jnp.zeros((D,), jnp.float32), 'Wv': jax.random.normal(ks[3], (D, D), jnp.float32) * s, 'bv': jnp.zeros((D,), jnp.float32), 'Wo': jax.random.normal(ks[4], (D, D), jnp.float32) * s, 'bo': jnp.zeros((D,), jnp.float32), 'rel_emb': jax.random.normal(ks[5], (2 * MAX_REL + 1, dk), jnp.float32)}
    _L1_attn_all = _L1_attn_setup()
    _L1_attn_in = {k: v for k, v in _L1_attn_all.items() if k in ('Wq', 'bq', 'Wk', 'bk', 'Wv', 'bv', 'Wo', 'bo', 'rel_emb')}
    del _L1_attn_all

    def _L1_ffn_setup():
        import jax, jax.numpy as jnp
        import numpy as np
        G, E = (4, 8)
        KG, KE = (2, 2)
        D, M = (192, 768)
        SCALE = 0.02

        def _combine_weights(xf, Wg, bg, Wge, bge):
            N = xf.shape[0]
            glog = xf @ Wg + bg
            gtop, gidx = jax.lax.top_k(glog, KG)
            ggate = jax.nn.softmax(gtop, axis=-1)
            elog_all = jnp.einsum('nd,gde->nge', xf, Wge) + bge
            elog = jnp.take_along_axis(elog_all, gidx[:, :, None], axis=1)
            etop, eidx = jax.lax.top_k(elog, KE)
            egate = jax.nn.softmax(etop, axis=-1)
            w = ggate[:, :, None] * egate
            flat = gidx[:, :, None] * E + eidx
            comb = jnp.zeros((N, G * E), xf.dtype).at[jnp.arange(N)[:, None, None], flat].add(w)
            return comb
        key = jax.random.key(seed)
        ks = jax.random.split(key, 8)
        x = jax.random.normal(ks[0], (1, 128, D), jnp.float32)
        Wg = jax.random.normal(ks[1], (D, G), jnp.float32) * SCALE
        bg = jnp.zeros((G,), jnp.float32)
        Wge = jax.random.normal(ks[2], (G, D, E), jnp.float32) * SCALE
        bge = jnp.zeros((G, E), jnp.float32)
        W1 = jax.random.normal(ks[3], (G * E, D, M), jnp.float32) * SCALE
        b1 = jnp.zeros((G * E, M), jnp.float32)
        W2 = jax.random.normal(ks[4], (G * E, M, D), jnp.float32) * SCALE
        b2 = jnp.zeros((G * E, D), jnp.float32)
        return {'x': x, 'Wg': Wg, 'bg': bg, 'Wge': Wge, 'bge': bge, 'W1': W1, 'b1': b1, 'W2': W2, 'b2': b2}
    _L1_ffn_all = _L1_ffn_setup()
    _L1_ffn_in = {k: v for k, v in _L1_ffn_all.items() if k in ('Wg', 'bg', 'Wge', 'bge', 'W1', 'b1', 'W2', 'b2')}
    del _L1_ffn_all
    return {'x': x, 'L0_tok_W': _L0_tok_in['W'], 'L0_tok_b': _L0_tok_in['b'], 'L0_tok_pos_emb': _L0_tok_in['pos_emb'], 'L0_attn_Wq': _L0_attn_in['Wq'], 'L0_attn_Wk': _L0_attn_in['Wk'], 'L0_attn_Wv': _L0_attn_in['Wv'], 'L0_attn_Wo': _L0_attn_in['Wo'], 'L0_attn_gammas': _L0_attn_in['gammas'], 'L0_attn_gn_weight': _L0_attn_in['gn_weight'], 'L0_attn_gn_bias': _L0_attn_in['gn_bias'], 'L0_ffn_router_w': _L0_ffn_in['router_w'], 'L0_ffn_wi': _L0_ffn_in['wi'], 'L0_ffn_wo': _L0_ffn_in['wo'], 'L1_attn_Wq': _L1_attn_in['Wq'], 'L1_attn_bq': _L1_attn_in['bq'], 'L1_attn_Wk': _L1_attn_in['Wk'], 'L1_attn_bk': _L1_attn_in['bk'], 'L1_attn_Wv': _L1_attn_in['Wv'], 'L1_attn_bv': _L1_attn_in['bv'], 'L1_attn_Wo': _L1_attn_in['Wo'], 'L1_attn_bo': _L1_attn_in['bo'], 'L1_attn_rel_emb': _L1_attn_in['rel_emb'], 'L1_ffn_Wg': _L1_ffn_in['Wg'], 'L1_ffn_bg': _L1_ffn_in['bg'], 'L1_ffn_Wge': _L1_ffn_in['Wge'], 'L1_ffn_bge': _L1_ffn_in['bge'], 'L1_ffn_W1': _L1_ffn_in['W1'], 'L1_ffn_b1': _L1_ffn_in['b1'], 'L1_ffn_W2': _L1_ffn_in['W2'], 'L1_ffn_b2': _L1_ffn_in['b2']}

def reference(x, L0_tok_W, L0_tok_b, L0_tok_pos_emb, L0_attn_Wq, L0_attn_Wk, L0_attn_Wv, L0_attn_Wo, L0_attn_gammas, L0_attn_gn_weight, L0_attn_gn_bias, L0_ffn_router_w, L0_ffn_wi, L0_ffn_wo, L1_attn_Wq, L1_attn_bq, L1_attn_Wk, L1_attn_bk, L1_attn_Wv, L1_attn_bv, L1_attn_Wo, L1_attn_bo, L1_attn_rel_emb, L1_ffn_Wg, L1_ffn_bg, L1_ffn_Wge, L1_ffn_bge, L1_ffn_W1, L1_ffn_b1, L1_ffn_W2, L1_ffn_b2):
    import jax
    import jax.numpy as jnp

    def _L0_tok_ref(x, W, b, pos_emb):
        import jax, jax.numpy as jnp
        import numpy as np
        IMG = 96
        PATCH = 16
        C = 3
        PROJ = 192
        NUM_PATCHES = (IMG // PATCH) ** 2
        FLAT = C * PATCH * PATCH
        BATCH = 64

        def _patchify(x):
            B, c, H, Wd = x.shape
            hp, wp = (H // PATCH, Wd // PATCH)
            x = x.reshape(B, c, hp, PATCH, wp, PATCH)
            x = x.transpose(0, 2, 4, 1, 3, 5)
            return x.reshape(B, hp * wp, c * PATCH * PATCH)
        flat = _patchify(x)
        encoded = jnp.einsum('bnf,df->bnd', flat, W) + b + pos_emb[None, :, :]
        return encoded

    def _L0_attn_ref(x, Wq, Wk, Wv, Wo, gammas, gn_weight, gn_bias):
        import jax, jax.numpy as jnp
        import numpy as np
        D_MODEL = 192
        NUM_HEADS = 3
        HEAD_DIM = D_MODEL // NUM_HEADS
        GN_EPS = 1e-05

        def _xavier(key, shape, gain=0.5):
            fan_in, fan_out = (shape[1], shape[0])
            a = gain * np.sqrt(6.0 / (fan_in + fan_out))
            return jax.random.uniform(key, shape, jnp.float32, -a, a)
        B, L, D = x.shape
        H = gammas.shape[0]
        hd = D // H
        q = (x @ Wq.T).reshape(B, L, H, hd)
        k = (x @ Wk.T).reshape(B, L, H, hd)
        v = (x @ Wv.T).reshape(B, L, H, hd)
        scores = jnp.einsum('blhe,bmhe->bhlm', q, k) / jnp.sqrt(jnp.float32(hd))
        pos = jnp.arange(L)
        diff = pos[None, :] - pos[:, None]
        mask = diff >= 0
        dclip = jnp.maximum(diff, 0).astype(jnp.float32)
        decay = jnp.where(mask, gammas[:, None, None] ** dclip, 0.0)
        scores = scores * decay[None]
        weights = jax.nn.softmax(scores, axis=-1)
        o = jnp.einsum('bhlm,bmhe->blhe', weights, v)
        mean = o.mean(axis=(1, 3), keepdims=True)
        var = o.var(axis=(1, 3), keepdims=True)
        o = (o - mean) / jnp.sqrt(var + GN_EPS)
        y = o.reshape(B, L, D) * gn_weight + gn_bias
        return y @ Wo.T

    def _L0_ffn_ref(hidden_states, router_w, wi, wo):
        import jax, jax.numpy as jnp
        import numpy as np
        D_MODEL = 192
        D_FF = 768
        NUM_EXPERTS = 8
        EXPERT_CAPACITY = 256
        B, S, d = hidden_states.shape
        E = router_w.shape[1]
        x = hidden_states.reshape(-1, d)
        logits = x.astype(jnp.float32) @ router_w.astype(jnp.float32)
        probs = jax.nn.softmax(logits, axis=-1).astype(x.dtype)
        p = jnp.max(probs, axis=-1)
        e_idx = jnp.argmax(probs, axis=-1)
        mask = jax.nn.one_hot(e_idx, E, dtype=x.dtype)
        token_priority = jnp.cumsum(mask[:, None, :], axis=-2)[:, 0, :]
        mask = mask * (token_priority <= EXPERT_CAPACITY).astype(x.dtype)
        combine = mask * p[:, None]

        def body(acc, ew):
            Wi_e, Wo_e, w_e = ew
            h = jax.nn.relu(x @ Wi_e) @ Wo_e
            return (acc + w_e[:, None] * h, None)
        out, _ = jax.lax.scan(body, jnp.zeros_like(x), (wi, wo, combine.T))
        return out.reshape(B, S, d)

    def _L1_attn_ref(x, Wq, bq, Wk, bk, Wv, bv, Wo, bo, rel_emb):
        import jax, jax.numpy as jnp
        import numpy as np
        import math
        MAX_REL = 32
        B, S, D = x.shape
        dk = rel_emb.shape[-1]
        H = D // dk
        scale = 1.0 / math.sqrt(dk)

        def proj(W, b):
            return (x @ W + b).reshape(B, S, H, dk).transpose(0, 2, 1, 3)
        Q = proj(Wq, bq)
        K = proj(Wk, bk)
        V = proj(Wv, bv)
        pos = jnp.arange(S)
        rel_idx = jnp.clip(pos[:, None] - pos[None, :], -MAX_REL, MAX_REL) + MAX_REL
        rel = rel_emb[rel_idx]
        scores = jnp.einsum('bhqd,bhkd->bhqk', Q, K)
        scores = scores + jnp.einsum('bhqd,qkd->bhqk', Q, rel)
        scores = scores * scale
        attn = jax.nn.softmax(scores, axis=-1)
        ctx = jnp.einsum('bhqk,bhkd->bhqd', attn, V)
        ctx = ctx.transpose(0, 2, 1, 3).reshape(B, S, D)
        return ctx @ Wo + bo

    def _L1_ffn_ref(x, Wg, bg, Wge, bge, W1, b1, W2, b2):
        import jax, jax.numpy as jnp
        import numpy as np
        G, E = (4, 8)
        KG, KE = (2, 2)
        D, M = (192, 768)
        SCALE = 0.02

        def _combine_weights(xf, Wg, bg, Wge, bge):
            N = xf.shape[0]
            glog = xf @ Wg + bg
            gtop, gidx = jax.lax.top_k(glog, KG)
            ggate = jax.nn.softmax(gtop, axis=-1)
            elog_all = jnp.einsum('nd,gde->nge', xf, Wge) + bge
            elog = jnp.take_along_axis(elog_all, gidx[:, :, None], axis=1)
            etop, eidx = jax.lax.top_k(elog, KE)
            egate = jax.nn.softmax(etop, axis=-1)
            w = ggate[:, :, None] * egate
            flat = gidx[:, :, None] * E + eidx
            comb = jnp.zeros((N, G * E), xf.dtype).at[jnp.arange(N)[:, None, None], flat].add(w)
            return comb
        shp = x.shape
        xf = x.reshape(-1, D)
        comb = _combine_weights(xf, Wg, bg, Wge, bge)
        h = jax.nn.gelu(jnp.einsum('nd,edm->nem', xf, W1) + b1, approximate=False)
        y = jnp.einsum('nem,emd->ned', h, W2) + b2
        out = jnp.einsum('ne,ned->nd', comb, y)
        return out.reshape(shp)
    h = _L0_tok_ref(x, L0_tok_W, L0_tok_b, L0_tok_pos_emb)
    h = h + _L0_attn_ref(_layernorm(h, axis=-1), L0_attn_Wq, L0_attn_Wk, L0_attn_Wv, L0_attn_Wo, L0_attn_gammas, L0_attn_gn_weight, L0_attn_gn_bias)
    h = h + _L0_ffn_ref(_layernorm(h, axis=-1), L0_ffn_router_w, L0_ffn_wi, L0_ffn_wo)
    h = h + _L1_attn_ref(_layernorm(h, axis=-1), L1_attn_Wq, L1_attn_bq, L1_attn_Wk, L1_attn_bk, L1_attn_Wv, L1_attn_bv, L1_attn_Wo, L1_attn_bo, L1_attn_rel_emb)
    h = h + _L1_ffn_ref(_layernorm(h, axis=-1), L1_ffn_Wg, L1_ffn_bg, L1_ffn_Wge, L1_ffn_bge, L1_ffn_W1, L1_ffn_b1, L1_ffn_W2, L1_ffn_b2)
    return h

_drawn_inputs = setup_inputs


def setup_inputs(seed=0):
    import zlib

    import numpy as np

    out = dict(_drawn_inputs(seed))
    spreads = {'L0_attn_gn_weight': (1.0, 0.2),
     'L0_attn_gn_bias': (0.0, 0.1),
     'L1_attn_bq': (0.0, 0.304),
     'L1_attn_bk': (0.0, 0.8),
     'L1_attn_bv': (0.0, 0.1),
     'L1_attn_bo': (0.0, 0.1),
     'L1_ffn_bg': (0.0, 0.369),
     'L1_ffn_bge': (0.0, 0.285),
     'L1_ffn_b1': (0.0, 0.704),
     'L1_ffn_b2': (0.0, 0.1)}
    factors = {}
    for name, (base, spread) in spreads.items():
        noise = np.random.default_rng([zlib.crc32(name.encode()), seed]).standard_normal(out[name].shape)
        drawn = base * np.exp(spread * noise) if base else spread * noise
        out[name] = jnp.asarray(drawn.astype(out[name].dtype))
    for name, factor in factors.items():
        out[name] = (out[name] * factor).astype(out[name].dtype)
    return out
```

```python
from contextlib import ExitStack

import numpy as np

import concourse.bass as bass
from concourse import mybir

F32 = mybir.dt.float32
F32R = mybir.dt.float32r
BF16 = mybir.dt.bfloat16
I32 = mybir.dt.int32
U32 = mybir.dt.uint32
ALU = mybir.AluOpType
ACT = mybir.ActivationFunctionType
AX_X = mybir.AxisListType.X

NI, NCH, IMG, PATCH = 16, 3, 96, 16
L = (IMG // PATCH) ** 2
FLAT = NCH * PATCH * PATCH
KF = FLAT // 128
TOK = NI * L
NT = -(-TOK // 128)
NP = NT * 128
LAST = TOK - (NT - 1) * 128
D = 192
CC, CP = 2, 96
M = 768
MC = M // 128
H = (3, 12)
E = (8, 32)
G, GE = 4, 8
NPAIR = NI // 2
TR = 3 * L
UW = 4 * TR
U = (2, 8)
HALF = TOK // 2
W_REL = 2 * L - 1
MAX_REL = 32
NCHUNK = NT
LN_EPS = 1e-5
GN_EPS = 1e-5
LOWEST = -3.0e38


def constants():
    p = np.arange(128)
    parts = {
        "ident": np.eye(128),
        "upto": (p[:, None] <= p[None, :]),
        "ones": np.ones((128, 128)),
        "count": np.broadcast_to(np.arange(1, NP + 129), (128, NP + 128)),
        "row": p[:, None],
        "row1": p[:, None] + 1,
        "eight": np.broadcast_to(np.arange(8), (128, 8)),
        "tile": np.broadcast_to(128 * np.arange(NT), (128, NT)),
    }
    ch = np.arange(CC)[None, :, None] * CP + p[:, None, None]
    parts["khead0"] = (ch // 64 == np.arange(3)).reshape(128, -1)
    parts["khead1"] = (p[:, None, None] // 16 == np.arange(6)) & (np.arange(CC)[None, :, None] >= 0)
    col = np.arange(D)
    parts["vhead0"] = p[:, None] // L == col // 64
    parts["vhead1"] = p[:, None] // L == (col // 16) % 3
    to = np.arange(CC)[:, None] * CP + np.arange(CP)[None, :]
    parts["same"] = (ch[:, :, :, None] // 64 == to[None, None] // 64).reshape(128, -1)
    where, cols, at = {}, [], 0
    for name, a in parts.items():
        a = np.asarray(a, np.float32).reshape(128, -1)
        where[name] = (at, a.shape[1])
        cols.append(a)
        at += a.shape[1]
    return where, np.concatenate(cols, 1)


WHERE, TABLE = constants()


def vit_tower(nc, A, out):
    with ExitStack() as ctx:
        def sb(name, shape, dt=F32):
            return ctx.enter_context(nc.sbuf_tensor(name, shape, dt))

        def sem(name):
            return ctx.enter_context(nc.semaphore(name))

        rows_dram = [nc.dram_tensor(f"rows{l}", (NP, D), F32).ap() for l in range(2)]
        rel_dram = nc.dram_tensor("reltab", (NP, H[1] * W_REL), F32)
        decay_dram = nc.dram_tensor("decaytab", (L, H[0] * W_REL), F32)

        table = sb("table", [128, TABLE.shape[1]])
        early = sb("early", [128, KF * (NP + D)])
        patches = early[:, 0:KF * NP].rearrange("p (k n) -> p k n", k=KF)
        tok_w = early[:, KF * NP:].rearrange("p (k n) -> p k n", k=KF)
        qrel = early[:, 0:NT * 12 * W_REL].rearrange("p (t w) -> p t w", t=NT)
        posb = sb("posb", [128, NT, D])
        tok_b = sb("tok_b", [128, D])
        h = sb("h", [128, NT, D])
        stats = sb("stats", [128, NT, 6])
        mv = sb("mv", [128, NT, 2])
        vare = sb("vare", [128, NT])
        std = sb("std", [128, NT])
        rstd = sb("rstd", [128, NT])
        xn = sb("xn", [128, NT, D])
        xT = sb("xT", [CP, CC, NP])
        wq, wk, wv, wo = [[sb(f"w{n}{l}", [CP, CC, D]) for l in range(2)] for n in "qkvo"]
        bq = sb("bq", [CP, CC])
        bk = sb("bk", [CP, CC])
        bv = sb("bv", [CP, CC])
        bkm = sb("bkm", [CP, CC, 6])
        bo = sb("bo", [128, D])
        gnw = sb("gnw", [CP, CC])
        gnb = sb("gnb", [CP, CC])
        zero_col = sb("zero_col", [128, 1])
        spare = sb("spare", [128, 16])
        qT = sb("qT", [CP, CC, NP])
        kblk = sb("kblk", [CP, CC, NI * 6 * L])
        xT3 = sb("xT3", [CP, 2, CC, 2, TR])
        vblk = sb("vblk", [TR, NI, D])
        score = sb("score", [128, 2, UW])
        prob = sb("prob", [128, 2, UW])
        top = sb("top", [128, 2, 12])
        psumm = sb("psumm", [128, 8, 12])
        pinv = sb("pinv", [128, 8, 12])
        probT = sb("probT", [TR, 2, 512])
        ctxr = sb("ctxr", [128, NPAIR, D])
        ctxT = sb("ctxT", [CP, CC, NP])
        gam = sb("gam", [L, 3])
        powers = sb("powers", [L, 3, W_REL])
        decay = sb("decay", [128, 3, L])
        gsum = sb("gsum", [CP, CC, NI])
        gvar = sb("gvar", [CP, CC, NI])
        gstd = sb("gstd", [CP, CC, NI])
        grs = sb("grs", [CP, CC, NI])
        gscale = sb("gscale", [CP, CC, NI])
        emb_rev = sb("emb_rev", [CP, 6, W_REL])
        rel = sb("rel", [128, NPAIR, UW])
        ones_bf = sb("ones_bf", [128, 128], BF16)
        upto_bf = sb("upto_bf", [128, 128], BF16)
        zero_bf = sb("zero_bf", [128, 512], BF16)
        wr = [sb("wr0", [CP, CC, E[0]]), sb("wr1", [CP, CC, G + E[1]])]
        rbias = sb("rbias", [128, G + E[1]])
        RW = 5
        logit = sb("logit", [128, NT * RW, 8])
        pick = [sb(f"pick{n}", [128, NT * RW, 8]) for n in range(2)]
        rank8 = sb("rank8", [128, NT * RW, 8])
        best = [sb(f"best{n}", [128, NT * RW]) for n in range(2)]
        first = sb("first", [128, NT * RW])
        gate = [sb(f"gate{n}", [128, NT * RW]) for n in range(4)]
        gated = sb("gated", [128, NT * RW, 8])
        comb = sb("comb", [128, NT, 32])
        crest = sb("crest", [128, NT, 32])
        mask_bf = sb("mask_bf", [128, NT, 32], BF16)
        wparts = sb("wparts", [128, NT, 32, 3], BF16)
        pos = sb("pos", [128, NT, 32])
        count = sb("count", [128, 32])
        nchunk = sb("nchunk", [128, 32])
        ends = sb("ends", [128, 32])
        before = sb("before", [128, 32])
        begun = sb("begun", [128, 32])
        job_e = sb("job_e", [128, 2])
        job_t = sb("job_t", [128, 2])
        jobs = sb("jobs", [1, 256], I32)
        njobs = sb("njobs", [1, 1], I32)
        combT = sb("combT", [32, NP])
        b1all = sb("b1all", [128, 32, MC])
        b2all = sb("b2all", [32, D])
        w1 = sb("w1", [CP, 2, CC, M])
        w2 = sb("w2", [128, 2, MC, D])
        sel = sb("sel", [128, 2, NT, 128], BF16)
        info = sb("info", [128, 2, NT, 5], BF16)
        nxt = sb("nxt", [128, 2, 2])
        cur = sb("cur", [128, 2, 2])
        idx = sb("idx", [128, 2], U32)
        xg = sb("xg", [128, 2, D])
        xgT = sb("xgT", [CP, 2, CC, 128])
        hid = sb("hid", [128, MC, 128])
        yw = sb("yw", [128, 2, 2, D], F32R)
        selT = sb("selT", [128, 2, NP], F32R)

        ps = ctx.enter_context(nc.psum_tensor("ps", [128, 8, 512], F32))

        def cst(name, rows=128):
            at, n = WHERE[name]
            return table[0:rows, at:at + n]

        ident = cst("ident")

        def view(ap, dims, offset=0):
            return bass.AP(ap.tensor, ap.offset + offset, [list(ap.ap[0])] + [list(d) for d in dims])

        s_table = sem("table_loaded")
        s_patch = sem("patches_loaded")
        s_posld = sem("pos_loaded")
        s_attw = [sem("attn0_weights_loaded"), sem("attn1_weights_loaded")]
        s_rtw = [sem("router0_loaded"), sem("router1_loaded")]
        s_pad = sem("pads_zeroed")
        s_posb = sem("pos_plus_bias")
        s_emb = sem("embedding_in_psum")
        s_hemb = sem("embedding_read")
        s_step = [sem(f"vector_step{n}") for n in range(5)]
        s_lnvar = sem("ln_variance")
        s_lnstd = sem("ln_deviation")
        s_xn = sem("normed_rows")
        s_xtp = sem("normed_in_psum")
        s_xt = sem("normed_columns")
        s_gam = sem("gammas_loaded")
        s_pow = sem("powers_ready")
        s_powst = sem("powers_stored")
        s_decay = sem("decay_loaded")
        s_qp, s_q, s_kp, s_kv, s_ka, s_vp, s_vv, s_sp, s_sr, s_sh, s_ex, s_sum, s_ptp, s_pt, s_cp, s_cn, s_ctp, s_ct, s_op, s_or = [
            [sem(f"{n}{l}") for l in range(2)] for n in (
                "queries_in_psum", "queries_ready", "keys_in_psum", "keys_by_vector", "keys_by_scalar",
                "values_in_psum", "values_ready", "scores_in_psum", "scores_read", "scores_shifted",
                "exp_ready", "sums_ready", "probsT_in_psum", "probsT_ready", "context_in_psum",
                "context_ready", "contextT_in_psum", "contextT_ready", "projected", "projected_read")]
        s_tri = [sem(f"columns_tripled{l}") for l in range(2)]
        s_gs = sem("group_sums")
        s_gp = sem("group_sums_in_psum")
        s_gc = sem("centred")
        s_gq = sem("squared")
        s_gv = sem("group_variance")
        s_gd = sem("group_deviation")
        s_gn = sem("group_normed")
        s_rp = sem("rel_in_psum")
        s_rs = sem("rel_rows_ready")
        s_rst = sem("rel_rows_stored")
        s_rel = sem("rel_loaded")
        s_hbo = sem("bias_added")
        s_bkm = sem("key_bias_masked")
        (s_rows, s_lp, s_rx, s_re, s_mask, s_rank, s_jcol, s_jrow, s_jobs, s_cbp, s_cbt, s_acc, s_hp, s_hd,
         s_sel, s_inf, s_idx, s_xgp, s_xg, s_yp, s_yw, s_done) = [
            [sem(f"{n}{l}") for l in range(2)] for n in (
                "rows_stored", "logits_in_psum", "router_shifted", "router_exp", "mask_ready",
                "ranks_in_psum", "job_columns", "job_rows_in_psum", "jobs_ready", "combineT_in_psum",
                "combineT_ready", "sums_begun", "hidden_in_psum", "hidden_ready", "selection_ready",
                "slots_in_psum", "slots_ready", "gatheredT_in_psum", "gatheredT_ready", "outputs_in_psum",
                "outputs_ready", "sums_complete")]
        s_w1, s_w2, s_gat = [[[sem(f"{n}{l}_{s}") for s in range(2)] for l in range(2)]
                             for n in ("w1_loaded", "w2_loaded", "rows_gathered")]
        s_asked = [sem(f"gather_asked{l}") for l in range(2)]
        s_out = sem("output_ready")
        s_stored = sem("output_stored")

        W1d = [A["L0_ffn_wi"], A["L1_ffn_W1"]]
        W2d = [A["L0_ffn_wo"], A["L1_ffn_W2"]]
        chunked = "(c p) n -> p c n"

        def key_slot(l, co, n, hh):
            hk = 6 if l else 3
            return view(kblk[:, co, 0:1], [[hk * L, NI // 2], [1, L]], (n * NI // 2 * hk + hh) * L)

        def job_count(eng, l):
            eng.wait_ge(s_jobs[l], 1)
            return eng.snap((eng.value_load(njobs[0:1, 0:1], min_val=1, max_val=64) + 1) // 2)

        def job_expert(eng, l, j):
            return eng.value_load(jobs[0:1, bass.ds(j, 1)], min_val=0, max_val=E[l] - 1)

        block = ctx.enter_context(nc.Block())

        @block.sync
        def _(sp):
            for half in range(2):
                k = slice(half * KF // 2, (half + 1) * KF // 2)
                sp.dma_start(patches[:, k, 0:TOK], A["patchesT"].rearrange("(k p) n -> p k n", p=128)[:, k]).then_inc(s_patch, 16)
                sp.dma_start(tok_w[:, k, :], A["tok_WT"].rearrange("(k p) n -> p k n", p=128)[:, k]).then_inc(s_patch, 16)
            sp.dma_start(posb[:, 0:NT - 1, :], A["pos"][0:(NT - 1) * 128].rearrange("(t p) n -> p t n", p=128)).then_inc(s_posld, 16)
            sp.dma_start(posb[0:LAST, NT - 1, :], A["pos"][(NT - 1) * 128:TOK]).then_inc(s_posld, 16)
            sp.dma_start(tok_b[:], A["L0_tok_b"].partition_broadcast(128)).then_inc(s_posld, 16)
            sp.dma_start(table[:], A["table"]).then_inc(s_table, 16)
            sp.dma_start(gam[:], A["L0_attn_gammas"].partition_broadcast(L)).then_inc(s_gam, 16)
            for w, n in ((wq, "WqT0"), (wk, "WkT0"), (wv, "WvT0"), (wo, "WoT0")):
                sp.dma_start(w[0][:], A[n].rearrange(chunked, p=CP)).then_inc(s_attw[0], 16)
            for b, n in ((gnw, "L0_attn_gn_weight"), (gnb, "L0_attn_gn_bias")):
                sp.dma_start(b[:], A[n]).then_inc(s_attw[0], 16)
            sp.dma_start(wr[0][:], A["L0_ffn_router_w"].rearrange(chunked, p=CP)).then_inc(s_rtw[0], 16)
            sp.wait_ge(s_pow, 1)
            sp.dma_start(decay_dram.ap(), powers[:].rearrange("q h w -> q (h w)")).then_inc(s_powst, 16)
            sp.wait_ge(s_powst, 16)
            sp.wait_ge(s_pad, 1)
            sheared = bass.AP(decay_dram, L - 1, [[3 * W_REL - 1, L], [W_REL, 3], [1, L]])
            for i in range(2):
                sp.dma_start(decay[64 * i:64 * i + L], sheared).then_inc(s_decay, 16)
            for w, n in ((wq, "Wq"), (wk, "Wk"), (wv, "Wv"), (wo, "Wo")):
                sp.dma_start(w[1][:], A["L1_attn_" + n].rearrange(chunked, p=CP)).then_inc(s_attw[1], 16)
            for b, n in ((bq, "bq"), (bk, "bk"), (bv, "bv")):
                sp.dma_start(b[:], A["L1_attn_" + n]).then_inc(s_attw[1], 16)
            sp.dma_start(bo[:], A["L1_attn_bo"].partition_broadcast(128)).then_inc(s_attw[1], 16)
            sp.wait_ge(s_pad, 8)
            for k in range(6):
                sp.dma_start(emb_rev[16 * k:16 * k + 16, k, :], A["emb_rev"]).then_inc(s_attw[1], 16)
            sp.dma_start(wr[1][:, :, 0:G], A["L1_ffn_Wg"].rearrange(chunked, p=CP)).then_inc(s_rtw[1], 16)
            for g in range(G):
                sp.dma_start(wr[1][:, :, G + GE * g:G + GE * (g + 1)], A["L1_ffn_Wge"][g].rearrange(chunked, p=CP)).then_inc(s_rtw[1], 16)
            sp.dma_start(rbias[:, 0:G], A["L1_ffn_bg"].partition_broadcast(128)).then_inc(s_rtw[1], 16)
            sp.dma_start(rbias[:, G:], A["L1_ffn_bge"].rearrange("g e -> (g e)").partition_broadcast(128)).then_inc(s_rtw[1], 16)
            sp.dma_start(b1all[:], A["b1T"]).then_inc(s_rtw[1], 16)
            sp.dma_start(b2all[:], A["L1_ffn_b2"]).then_inc(s_rtw[1], 16)

            def experts(l):
                sp.wait_ge(s_xn, NT * (2 * l + 2))
                sp.dma_start(rows_dram[l].rearrange("(t p) n -> p t n", p=128), xn[:]).then_inc(s_rows[l], 16)

                def load(j, s, e, first=False):
                    if not first:
                        sp.wait_ge(s_hp[l], j * 2 - 2)
                    sp.dma_start(w1[:, s], W1d[l][bass.ds(e, 1)].rearrange("e (c p) m -> p (e c) m", p=CP)).then_inc(s_w1[l][s], 16)
                    if not first:
                        sp.wait_ge(s_yp[l], j - 1)
                    sp.dma_start(w2[:, s], W2d[l][bass.ds(e, 1)].rearrange("e (c p) m -> p (e c) m", p=128)).then_inc(s_w2[l][s], 16)

                pairs = job_count(sp, l)
                for s in range(2):
                    load(s, s, job_expert(sp, l, s), first=True)
                with sp.Fori(0, pairs) as i:
                    for s in range(2):
                        load(i * 2 + s + 2, s, job_expert(sp, l, i * 2 + s + 2))

            experts(0)
            for t in range(NT):
                sp.wait_ge(s_rs, 2 * t + 2)
                sp.dma_start(rel_dram.ap()[t * 128:(t + 1) * 128], qrel[:, t, :]).then_inc(s_rst, 16)
            sp.wait_ge(s_rst, 16 * NT)
            for b in range(NI):
                sheared = bass.AP(rel_dram, L * b * 12 * W_REL + L - 1, [[12 * W_REL - 1, L], [W_REL, 12], [1, L]])
                sp.dma_start(rel[64 * (b % 2):64 * (b % 2) + L, b // 2, :].rearrange("p (h k) -> p h k", k=L),
                             sheared).then_inc(s_rel, 16)
            experts(1)
            sp.wait_ge(s_out, 1)
            sp.dma_start(out[0:(NT - 1) * 128].rearrange("(t p) n -> p t n", p=128), h[:, 0:NT - 1, :]).then_inc(s_stored, 16)
            sp.dma_start(out[(NT - 1) * 128:TOK], h[0:LAST, NT - 1, :]).then_inc(s_stored, 16)
            sp.wait_ge(s_stored, 32)
            sp.wait_ge(s_powst, 16)
            for l in range(2):
                sp.wait_ge(s_rows[l], 16)

        @block.gpsimd
        def _(pool):
            for n, pad in enumerate((
                    decay[:],
                    patches[:, :, TOK:NP],
                    posb[64:128, NT - 1, :],
                    zero_col[:],
                    qT[:, :, TOK:NP],
                    ctxT[:, :, TOK:NP],
                    rel[:],
                    emb_rev[:],
                    selT[:].bitcast(F32),
                    zero_bf[:],
            )):
                if n:
                    pool.wait_ge(s_pad, n)
                pool.memset(pad, 0.0).then_inc(s_pad, 1)
            pool.wait_ge(s_pad, 10)
            pool.wait_ge(s_posld, 48)
            pool.tensor_tensor(posb[:], posb[:], view(tok_b[:], [[0, NT], [1, D]]), ALU.add).then_inc(s_posb, 1)
            pool.wait_ge(s_table, 16)
            pool.tensor_copy(ones_bf[:], cst("ones")).then_inc(s_pad, 1)
            pool.tensor_copy(upto_bf[:], cst("upto")).then_inc(s_pad, 1)
            for s in range(2):
                pool.tensor_copy(info[:, s, :, 0], view(cst("row1"), [[0, NT]])).then_inc(s_pad, 1)
                pool.tensor_copy(info[:, s, :, 1], cst("tile")).then_inc(s_pad, 1)

            def gathers(l):
                pool.wait_ge(s_rows[l], 16)
                def gather(j, s):
                    pool.wait_ge(s_idx[l], j + 1)
                    pool.sem_inc(s_asked[l], 1)
                    pool.indirect_dma_start(xg[:, s, :], None, rows_dram[l],
                                            bass.IndirectOffsetOnAxis(idx[:, s:s + 1], 0)).then_inc(s_gat[l][s], 16)

                pairs = job_count(pool, l)
                for s in range(2):
                    gather(s, s)
                with pool.Fori(0, pairs) as i:
                    for s in range(2):
                        gather(i * 2 + s + 2, s)

            def triple(l):
                pool.wait_ge(s_xt, NT * (2 * l + 1))
                for p in range(NPAIR):
                    if p >= 2:
                        pool.wait_ge(s_vp[l], p - 1)
                    for i in range(2):
                        b = 2 * p + i
                        pool.tensor_copy(xT3[:, p % 2, :, i, :].rearrange("p c (r k) -> p c r k", r=3),
                                         view(xT[:, 0, L * b:L * b + L], [[NP, CC], [0, 3], [1, L]])).then_inc(s_tri[l], 1)

            triple(0)
            gathers(0)
            triple(1)
            pool.wait_ge(s_attw[1], 16 * 14)
            pool.wait_ge(s_xn, NT * 3)
            pool.tensor_tensor(h[:], h[:], view(bo[:], [[0, NT], [1, D]]), ALU.add).then_inc(s_hbo, 1)
            gathers(1)

        @block.scalar
        def _(act):
            spares = iter(range(16))

            def table_for(func):
                n = next(spares)
                act.activation(spare[:, n:n + 1], zero_col[:], func)

            def norm(k):
                act.wait_ge(s_lnvar, k + 1)
                act.activation(std[:], vare[:], ACT.Sqrt).then_inc(s_lnstd, 1)
                for t in range(NT):
                    n = NT * k + t
                    act.wait_ge(s_xtp, n + 1)
                    act.activation(xT[:, :, t * 128:(t + 1) * 128],
                                   ps[0:CP, 6 + t % 2, 0:256].rearrange("p (c n) -> p c n", c=CC),
                                   ACT.Identity).then_inc(s_xt, 1)

            def attention(l):
                act.wait_ge(s_pad, 6)
                if l:
                    act.wait_ge(s_attw[1], 16 * 14)
                for m in range(4):
                    co, n = m // 2, m % 2
                    act.wait_ge(s_qp[l], m + 1)
                    act.activation(qT[:, co, n * HALF:(n + 1) * HALF], ps[0:CP, m, 0:HALF], ACT.Identity,
                                   bias=bq[:, co:co + 1] if l else zero_col[0:CP]).then_inc(s_q[l], 1)
                if l:
                    for t in range(NT):
                        for c in range(CC):
                            r = 2 * t + c
                            act.wait_ge(s_rp, r + 1)
                            act.activation(qrel[:, t, c * 6 * W_REL:(c + 1) * 6 * W_REL], ps[:, 4 + r % 2, 0:6 * W_REL],
                                           ACT.Identity).then_inc(s_rs, 1)
                    act.wait_ge(s_bkm, 1)
                hk = H[l] // 2 if l else 3
                for m in (1, 3):
                    co, n = m // 2, m % 2
                    act.wait_ge(s_kp[l], m + 1)
                    for hh in range(hk):
                        mcol = WHERE[f"khead{l}"][0] + co * hk + hh
                        act.activation(key_slot(l, co, n, hh), ps[0:CP, m, 0:HALF].rearrange("p (b k) -> p b k", k=L),
                                       ACT.Identity, scale=table[0:CP, mcol:mcol + 1],
                                       bias=bkm[:, co, hh:hh + 1] if l else zero_col[0:CP]).then_inc(s_ka[l], 1)
                table_for(ACT.Exp)
                per = NPAIR // U[l]
                for u in range(U[l] + 3):
                    if u < U[l]:
                        act.wait_ge(s_sh[l], u + 1)
                        if u >= 2:
                            act.wait_ge(s_ptp[l], u - 1)
                            act.wait_ge(s_sum[l], u - 1)
                        act.activation(prob[:, u % 2], score[:, u % 2], ACT.Exp, scale=0.25 if l else 1.0).then_inc(s_ex[l], 1)
                    if 1 <= u <= U[l]:
                        v = u - 1
                        act.wait_ge(s_ptp[l], v + 1)
                        if v >= 2:
                            act.wait_ge(s_cp[l], v - 1)
                        act.activation(probT[:, v % 2], ps[0:TR, 2 + v % 2, :], ACT.Identity).then_inc(s_pt[l], 1)
                    if u >= 3:
                        for p in range((u - 3) * per, (u - 2) * per):
                            act.wait_ge(s_ctp[l], p + 1)
                            for c in range(CC):
                                src = view(ps[0:CP, 6 + p % 2, 128 * c:128 * c + 1], [[64, 2], [1, L]])
                                act.activation(ctxT[:, c, 72 * p:72 * p + 72].rearrange("p (i k) -> p i k", k=L), src,
                                               ACT.Identity, bias=bv[:, c:c + 1] if l else zero_col[0:CP]).then_inc(s_ct[l], 1)
                if l == 0:
                    table_for(ACT.Sqrt)
                    act.wait_ge(s_gc, 1)
                    act.activation(kblk[:, :, 0:TOK], ctxT[:, :, 0:TOK], ACT.Square).then_inc(s_gq, 1)
                    act.wait_ge(s_gv, 1)
                    act.activation(gstd[:], gvar[:], ACT.Sqrt).then_inc(s_gd, 1)

            def experts(l):
                if l == 0:
                    act.wait_ge(s_rx[0], 1)
                    act.activation(pick[1][:, 0:NT, :], pick[0][:, 0:NT, :], ACT.Exp).then_inc(s_re[0], 1)
                else:
                    act.wait_ge(s_rx[1], 1)
                    act.activation(gate[1][:], gate[0][:], ACT.Exp).then_inc(s_re[1], 1)
                    act.wait_ge(s_cbp[1], 1)
                    act.activation(combT[:, 0:512], ps[0:32, 5, :], ACT.Identity).then_inc(s_cbt[1], 1)
                    act.activation(combT[:, 512:NP], ps[0:32, 4, 0:128], ACT.Identity).then_inc(s_cbt[1], 1)

                def columns(j, s):
                    act.wait_ge(s_xgp[l], j + 1)
                    act.activation(xgT[:, s], ps[0:CP, 6, 256 * s:256 * s + 256].rearrange("p (c n) -> p c n", c=CC),
                                   ACT.Identity).then_inc(s_xg[l], 1)

                def hidden(j, s):
                    if l:
                        e = job_expert(act, l, j)
                    for b in range(2):
                        act.wait_ge(s_hp[l], j * 2 + b + 1)
                        if l == 0:
                            ins = act.activation(hid[:, 3 * b:3 * b + 3, :].rearrange("p m n -> p (m n)"),
                                                 ps[:, 3 + b, 0:384], ACT.Relu)
                        else:
                            for m in range(3):
                                ins = act.activation(hid[:, 3 * b + m, :], ps[:, 3 + b, 128 * m:128 * m + 128], ACT.Gelu,
                                                     bias=b1all[:, bass.ds(e, 1), 3 * b + m])
                        ins.then_inc(s_hd[l], 1)

                table_for(ACT.Gelu if l else ACT.Relu)
                pairs = job_count(act, l)
                columns(0, 0)
                with act.Fori(0, pairs) as i:
                    for s in range(2):
                        hidden(i * 2 + s, s)
                        columns(i * 2 + s + 1, 1 - s)

            act.wait_ge(s_pad, 4)
            table_for(ACT.Sqrt)
            norm(0)
            attention(0)
            norm(1)
            table_for(ACT.Exp)
            experts(0)
            table_for(ACT.Sqrt)
            norm(2)
            attention(1)
            table_for(ACT.Sqrt)
            norm(3)
            table_for(ACT.Exp)
            experts(1)

        @block.vector
        def _(dve):
            stretch, steps = 0, 0

            def step(ins, before=0):
                nonlocal steps
                steps += 1
                ins.then_inc(s_step[stretch], 1)
                dve.wait_ge(s_step[stretch], before + steps)

            def next_stretch():
                nonlocal stretch, steps
                stretch, steps = stretch + 1, 0

            for bank in (0, 1, 4, 5):
                ins = dve.memset(ps[:, bank, :], 0.0)
            step(ins)

            step(dve.memset(powers[:], 0.0))
            dve.wait_ge(s_gam, 16)
            at = L - 1
            step(dve.memset(powers[:, :, at:at + 1], 1.0))
            step(dve.tensor_copy(powers[:, :, at + 1:at + 2], gam[:].rearrange("p (h o) -> p h o", o=1)))
            n = 1
            while n < L - 1:
                m = min(n, L - 1 - n)
                step(dve.tensor_tensor(powers[:, :, at + n + 1:at + n + m + 1], powers[:, :, at + 1:at + m + 1],
                                       view(powers[:, :, at + n:at + n + 1], [[W_REL, 3], [0, m]]), ALU.mult))
                n += m
            dve.tensor_scalar(powers[:], powers[:], 0.125, None, ALU.mult).then_inc(s_pow, 1)

            dve.wait_ge(s_posb, 1)
            for t in range(NT):
                dve.wait_ge(s_emb, t + 1)
                dve.tensor_tensor(h[:, t, :], ps[:, t % 2, 0:D], posb[:, t, :], ALU.add).then_inc(s_hemb, 1)
            dve.wait_ge(s_hemb, NT)

            def norm(k):
                for t in range(NT):
                    ins = dve.bn_stats(stats[:, t, :], h[:, t, :])
                step(ins)
                for t in range(NT):
                    ins = dve.bn_aggr(mv[:, t, :], stats[:, t, :])
                step(ins)
                dve.tensor_scalar(vare[:], mv[:, :, 1], LN_EPS, None, ALU.add).then_inc(s_lnvar, 1)
                dve.wait_ge(s_lnstd, k + 1)
                step(dve.reciprocal(rstd[:], std[:]))
                for t in range(NT):
                    dve.tensor_scalar(xn[:, t, :], h[:, t, :], mv[:, t, 0:1], rstd[:, t:t + 1], ALU.subtract, ALU.mult).then_inc(s_xn, 1)

            def attention(l):
                nu, per = U[l], NPAIR // U[l]
                hk = 6 if l else 3
                if l:
                    dve.wait_ge(s_attw[1], 16 * 14)
                    dve.tensor_tensor(bkm[:], view(bk[:], [[1, CC], [0, 6]]),
                                      cst("khead1", CP).rearrange("p (c h) -> p c h", c=CC), ALU.mult).then_inc(s_bkm, 1)
                for m in (0, 2):
                    co, n = m // 2, m % 2
                    dve.wait_ge(s_kp[l], m + 1)
                    for hh in range(hk):
                        mcol = WHERE[f"khead{l}"][0] + co * hk + hh
                        src = ps[0:CP, m, 0:HALF].rearrange("p (b k) -> p b k", k=L)
                        dve.tensor_scalar(key_slot(l, co, n, hh), src, bk[:, co:co + 1] if l else 0.0,
                                          table[0:CP, mcol:mcol + 1], ALU.add, ALU.mult).then_inc(s_kv[l], 1)
                for p in range(NPAIR):
                    dve.wait_ge(s_vp[l], p + 1)
                    dve.tensor_tensor(vblk[:, 2 * p:2 * p + 2, :], ps[0:TR, 4 + p % 2, 0:2 * D].rearrange("p (i n) -> p i n", i=2),
                                      view(cst(f"vhead{l}", TR), [[0, 2], [1, D]]), ALU.mult).then_inc(s_vv[l], 1)
                if l:
                    dve.wait_ge(s_rel, 16 * NI)
                else:
                    dve.wait_ge(s_decay, 32)
                hw = D // H[l]
                for u in range(nu + 2):
                    if u < nu:
                        dve.wait_ge(s_sp[l], u + 1)
                        if u >= 2:
                            dve.wait_ge(s_ex[l], u - 1)
                        if l:
                            ins = dve.tensor_tensor(score[:, u % 2], ps[:, u % 2, 0:UW], rel[:, u, :], ALU.add)
                        else:
                            ins = dve.tensor_tensor(score[:, u % 2].rearrange("p (g k) -> p g k", g=4),
                                                    ps[:, u % 2, 0:UW].rearrange("p (g k) -> p g k", g=4),
                                                    view(decay[:], [[0, 4], [1, TR]]), ALU.mult)
                        ins.then_inc(s_sr[l], 1)
                        dve.wait_ge(s_sr[l], u + 1)
                        s3 = score[:, u % 2].rearrange("p (h k) -> p h k", k=L)
                        step(dve.tensor_reduce(top[:, u % 2], s3, AX_X, ALU.max))
                        dve.tensor_tensor(s3, s3, view(top[:, u % 2], [[1, 12], [0, L]]), ALU.subtract).then_inc(s_sh[l], 1)
                    if 1 <= u <= nu:
                        v = u - 1
                        dve.wait_ge(s_ex[l], v + 1)
                        dve.tensor_reduce(psumm[:, v], prob[:, v % 2].rearrange("p (h k) -> p h k", k=L), AX_X, ALU.add).then_inc(s_sum[l], 1)
                        dve.wait_ge(s_sum[l], v + 1)
                        step(dve.reciprocal(pinv[:, v], psumm[:, v]))
                    if u >= 2:
                        v = u - 2
                        dve.wait_ge(s_cp[l], v + 1)
                        if l:
                            dve.tensor_tensor(ctxr[:, v, :].rearrange("p (h n) -> p h n", n=hw),
                                              ps[:, 4 + v % 2, 0:D].rearrange("p (h n) -> p h n", n=hw),
                                              view(pinv[:, v], [[1, 12], [0, hw]]), ALU.mult).then_inc(s_cn[l], 1)
                        else:
                            for b in range(2):
                                ins = dve.tensor_tensor(
                                    ctxr[:, 4 * v + 2 * b:4 * v + 2 * b + 2, :].rearrange("p g (h n) -> p (g h) n", n=hw),
                                    ps[:, 4 + b, 0:2 * D].rearrange("p (h n) -> p h n", n=hw),
                                    view(pinv[:, v], [[1, 6], [0, hw]], 6 * b), ALU.mult)
                            ins.then_inc(s_cn[l], 1)
                if l == 0:
                    dve.wait_ge(s_ct[0], 2 * NPAIR)
                    c4 = ctxT[:, :, 0:TOK].rearrange("p c (b k) -> p c b k", k=L)
                    spread = [[NI, CC], [1, NI], [0, L]]
                    dve.tensor_reduce(gsum[:], c4, AX_X, ALU.add).then_inc(s_gs, 1)
                    dve.wait_ge(s_gp, 1)
                    step(dve.tensor_scalar(gvar[:], ps[0:CP, 7, 0:CC * NI].rearrange("p (c b) -> p c b", c=CC),
                                           1.0 / (64 * L), None, ALU.mult))
                    dve.tensor_tensor(c4, c4, view(gvar[:], spread), ALU.subtract).then_inc(s_gc, 1)
                    dve.wait_ge(s_gq, 1)
                    dve.tensor_reduce(gsum[:], kblk[:, :, 0:TOK].rearrange("p c (b k) -> p c b k", k=L), AX_X, ALU.add).then_inc(s_gs, 1)
                    dve.wait_ge(s_gp, 2)
                    dve.tensor_scalar(gvar[:], ps[0:CP, 7, 0:CC * NI].rearrange("p (c b) -> p c b", c=CC),
                                      1.0 / (64 * L), GN_EPS, ALU.mult, ALU.add).then_inc(s_gv, 1)
                    dve.wait_ge(s_gd, 1)
                    step(dve.reciprocal(grs[:], gstd[:]))
                    step(dve.tensor_tensor(gscale[:], grs[:], view(gnw[:], [[1, CC], [0, NI]]), ALU.mult))
                    step(dve.tensor_tensor(c4, c4, view(gscale[:], spread), ALU.mult))
                    for c in range(CC):
                        dve.tensor_scalar(ctxT[:, c, 0:TOK], ctxT[:, c, 0:TOK], gnb[:, c:c + 1], None, ALU.add).then_inc(s_gn, 1)
                else:
                    dve.wait_ge(s_hbo, 1)
                for t in range(NT):
                    dve.wait_ge(s_op[l], t + 1)
                    dve.tensor_tensor(h[:, t, :], ps[:, t % 2, 0:D], h[:, t, :], ALU.add).then_inc(s_or[l], 1)
                dve.wait_ge(s_or[l], NT)

            def choose(x, n, rows, which):
                step(dve.tensor_reduce(best[which][:, 0:rows], x, AX_X, ALU.max))
                b = view(best[which][:], [[1, rows], [0, 8]])
                step(dve.tensor_tensor(rank8[:, 0:rows], x, b, ALU.is_equal))
                step(dve.tensor_scalar(rank8[:, 0:rows], rank8[:, 0:rows], -8.0, None, ALU.mult))
                step(dve.tensor_tensor(rank8[:, 0:rows], rank8[:, 0:rows], view(cst("eight"), [[0, rows], [1, 8]]), ALU.add))
                step(dve.tensor_reduce(first[:, 0:rows], rank8[:, 0:rows], AX_X, ALU.min))
                step(dve.tensor_tensor(pick[which][:, 0:rows], rank8[:, 0:rows], view(first[:], [[1, rows], [0, 8]]), ALU.is_equal))

            def route(l):
                ne = E[l]
                dve.wait_ge(s_lp[l], 1)
                if l == 0:
                    rows = NT
                    step(dve.tensor_copy(logit[:, 0:rows, :], ps[:, 7, 0:8 * NT].rearrange("p (t e) -> p t e", e=8)))
                    step(dve.tensor_reduce(best[0][:, 0:rows], logit[:, 0:rows, :], AX_X, ALU.max))
                    dve.tensor_tensor(pick[0][:, 0:rows], logit[:, 0:rows], view(best[0][:], [[1, rows], [0, 8]]), ALU.subtract).then_inc(s_rx[0], 1)
                    dve.wait_ge(s_re[0], 1)
                    step(dve.tensor_reduce(gate[0][:, 0:rows], pick[1][:, 0:rows], AX_X, ALU.add))
                    step(dve.reciprocal(gate[1][:, 0:rows], gate[0][:, 0:rows]))
                    step(dve.tensor_tensor(logit[:, 0:rows], pick[1][:, 0:rows], view(gate[1][:], [[1, rows], [0, 8]]), ALU.mult))
                    choose(logit[:, 0:rows], 8, rows, 0)
                    step(dve.tensor_tensor(comb[:, :, 0:ne], pick[0][:, 0:rows], view(best[0][:], [[1, rows], [0, 8]]), ALU.mult))
                else:
                    rows = NT * RW
                    dve.wait_ge(s_rtw[1], 16 * 9)
                    step(dve.memset(logit[:], LOWEST))
                    l4 = logit[:].rearrange("p (t r) e -> p t r e", r=RW)
                    step(dve.tensor_tensor(l4[:, :, 0, 0:G], ps[:, 7, 0:36 * NT].rearrange("p (t e) -> p t e", t=NT)[:, :, 0:G],
                                           view(rbias[:], [[0, NT], [1, G]]), ALU.add))
                    for t in range(NT):
                        ins = dve.tensor_tensor(l4[:, t, 1:RW, :], ps[:, 7, 36 * t + G:36 * t + 36].rearrange("p (g e) -> p g e", e=GE),
                                                rbias[:, G:].rearrange("p (g e) -> p g e", e=GE), ALU.add)
                    step(ins)
                    choose(logit[:], 8, rows, 0)
                    step(dve.scalar_tensor_tensor(out=logit[:].rearrange("p r e -> p (r e)"), in0=pick[0][:].rearrange("p r e -> p (r e)"),
                                                  scalar=LOWEST, in1=logit[:].rearrange("p r e -> p (r e)"), op0=ALU.mult, op1=ALU.add))
                    choose(logit[:], 8, rows, 1)
                    dve.tensor_tensor(gate[0][:], best[1][:], best[0][:], ALU.subtract).then_inc(s_rx[1], 1)
                    dve.wait_ge(s_re[1], 1)
                    step(dve.tensor_scalar(gate[2][:], gate[1][:], 1.0, None, ALU.add))
                    step(dve.reciprocal(gate[3][:], gate[2][:]))
                    step(dve.tensor_tensor(gate[2][:], gate[1][:], gate[3][:], ALU.mult))
                    step(dve.tensor_tensor(pick[0][:], pick[0][:], view(gate[3][:], [[1, rows], [0, 8]]), ALU.mult))
                    step(dve.tensor_tensor(pick[1][:], pick[1][:], view(gate[2][:], [[1, rows], [0, 8]]), ALU.mult))
                    step(dve.tensor_tensor(gated[:], pick[0][:], pick[1][:], ALU.add))
                    for t in range(NT):
                        ins = dve.tensor_tensor(comb[:, t, :].rearrange("p (g e) -> p g e", e=GE), gated[:, RW * t + 1:RW * t + RW, :],
                                                view(gated[:, RW * t], [[1, G], [0, GE]]), ALU.mult)
                    step(ins)
                step(dve.memset(comb[LAST:128, NT - 1, 0:ne], 0.0))
                dve.tensor_scalar(mask_bf[:, :, 0:ne], comb[:, :, 0:ne], 0.0, None, ALU.is_gt).then_inc(s_mask[l], 1)
                step(dve.tensor_copy(wparts[:, :, 0:ne, 0], comb[:, :, 0:ne]))
                step(dve.tensor_tensor(crest[:, :, 0:ne], comb[:, :, 0:ne], wparts[:, :, 0:ne, 0], ALU.subtract))
                step(dve.tensor_copy(wparts[:, :, 0:ne, 1], crest[:, :, 0:ne]))
                step(dve.tensor_tensor(crest[:, :, 0:ne], crest[:, :, 0:ne], wparts[:, :, 0:ne, 1], ALU.subtract))
                step(dve.tensor_copy(wparts[:, :, 0:ne, 2], crest[:, :, 0:ne]))

            def list_jobs(l):
                ne = E[l]
                dve.wait_ge(s_rank[l], 1)
                step(dve.tensor_tensor(pos[:, :, 0:ne], ps[:, 6, 0:NT * ne].rearrange("p (t e) -> p t e", t=NT), mask_bf[:, :, 0:ne], ALU.mult))
                step(dve.tensor_copy(count[:, 0:ne], ps[:, 6, NT * ne:(NT + 1) * ne]))
                step(dve.tensor_scalar(nchunk[:, 0:ne], count[:, 0:ne], 0.0, None, ALU.is_gt))
                for c in range(1, NCHUNK):
                    step(dve.scalar_tensor_tensor(out=nchunk[:, 0:ne], in0=count[:, 0:ne], scalar=128.0 * c, in1=nchunk[:, 0:ne],
                                                  op0=ALU.is_gt, op1=ALU.add))
                step(dve.tensor_tensor_scan(ends[:, 0:ne], cst("ones")[:, 0:ne], nchunk[:, 0:ne], 0.0, ALU.mult, ALU.add))
                step(dve.tensor_scalar(before[:, 0:ne], ends[:, 0:ne], cst("row"), None, ALU.is_le))
                step(dve.tensor_tensor(begun[:, 0:ne], before[:, 0:ne], nchunk[:, 0:ne], ALU.mult))
                step(dve.tensor_reduce(job_t[:, 0:1], before[:, 0:ne], AX_X, ALU.add))
                step(dve.tensor_reduce(job_t[:, 1:2], begun[:, 0:ne], AX_X, ALU.add))
                step(dve.tensor_scalar(job_e[:, 0:1], job_t[:, 0:1], float(ne - 1), None, ALU.min))
                step(dve.tensor_tensor(job_t[:, 1:2], cst("row"), job_t[:, 1:2], ALU.subtract))
                step(dve.scalar_tensor_tensor(out=job_t[:, 1:2], in0=before[:, ne - 1:ne], scalar=float(NCHUNK), in1=job_t[:, 1:2],
                                              op0=ALU.mult, op1=ALU.add))
                dve.tensor_scalar(job_e[:, 1:2], job_t[:, 1:2], float(NCHUNK), 128.0, ALU.min, ALU.mult).then_inc(s_jcol[l], 1)
                dve.wait_ge(s_jrow[l], 1)
                step(dve.tensor_copy(njobs[:], ends[0:1, ne - 1:ne]))
                dve.tensor_copy(jobs[:], ps[0:1, 7, 256:512]).then_inc(s_jobs[l], 1)

            def experts(l):
                ne = E[l]
                dve.wait_ge(s_pad, 16)
                route(l)
                list_jobs(l)
                dve.memset(yw[:, 1].bitcast(F32), 0.0).then_inc(s_yw[l], 1)
                pairs = job_count(dve, l)

                def select(j, s):
                    e = job_expert(dve, l, j)
                    c = dve.value_load(jobs[0:1, bass.ds(j + 128, 1)], min_val=0, max_val=128 * NCHUNK)
                    dve.tensor_copy(info[:, s, :, 2:5], wparts[:, :, bass.ds(e, 1), :].rearrange("p t e w -> p t (e w)"))
                    mine = pos[:, :, bass.ds(e, 1)].rearrange("p t e -> p (t e)")
                    slots = table[:, bass.ds(c + WHERE["count"][0], 128)]
                    dve.tensor_tensor(sel[:, s], view(mine, [[32, NT], [0, 128]]), view(slots, [[0, NT], [1, 128]]),
                                      ALU.is_equal).then_inc(s_sel[l], 1)

                def slots_of(j, s, extra=0):
                    dve.wait_ge(s_inf[l], j + 1)
                    dve.tensor_reduce(nxt[:, s, 1:2], ps[:, 7, 8 * s + 2:8 * s + 5], AX_X, ALU.add)
                    step(dve.tensor_reduce(nxt[:, s, 0:1], ps[:, 7, 8 * s:8 * s + 2], AX_X, ALU.add), extra)
                    dve.tensor_scalar(idx[:, s:s + 1], nxt[:, s, 0:1], -1.0, 0.0, ALU.add, ALU.max).then_inc(s_idx[l], 1)

                for s in range(2):
                    select(s, s)
                    slots_of(s, s)
                select(2, 0)
                next_stretch()
                per = 2 * 3
                with dve.Fori(0, pairs) as i:
                    for s in range(2):
                        j = i * 2 + s
                        step(dve.tensor_copy(cur[:, s, :], nxt[:, s, :]), i * per)
                        dve.tensor_scalar(selT[:, s, :], cst("count")[:, 0:NP], cur[:, s, 0:1], None, ALU.is_equal)
                        slots_of(j + 2, s, i * per)
                        select(j + 3, 1 - s)
                        dve.wait_ge(s_yp[l], j + 1)
                        y, w = ps[:, 5, D * s:D * s + D], cur[:, s, 1:2]
                        step(dve.tensor_scalar(yw[:, s, 0], y, w, None, ALU.mult), i * per)
                        dve.scalar_tensor_tensor(out=yw[:, s, 1], in0=y, scalar=w, in1=yw[:, s, 0].bitcast(F32),
                                                 op0=ALU.mult, op1=ALU.subtract).then_inc(s_yw[l], 1)
                assert steps == per
                next_stretch()
                dve.wait_ge(s_done[l], 1)
                if l == 0:
                    for b in range(3):
                        n = 2 if b < 2 else 1
                        ins = dve.tensor_tensor(h[:, 2 * b:2 * b + n, :], ps[:, b, 0:n * D].rearrange("p (t n) -> p t n", t=n),
                                                h[:, 2 * b:2 * b + n, :], ALU.add)
                    ins.then_inc(s_hemb, 1)
                    dve.wait_ge(s_hemb, NT + 1)
                else:
                    for b in range(3):
                        n = 2 if b < 2 else 1
                        ins = dve.tensor_tensor(h[:, 2 * b:2 * b + n, :], ps[:, b, 0:n * D].rearrange("p (t n) -> p t n", t=n),
                                                h[:, 2 * b:2 * b + n, :], ALU.add)
                    ins.then_inc(s_out, 1)

            norm(0)
            attention(0)
            norm(1)
            experts(0)
            norm(2)
            attention(1)
            norm(3)
            experts(1)

        @block.tensor
        def _(pe):
            def mm(o, a, b, start=True, stop=True):
                return pe.matmul(o, a, b, start=start, stop=stop, skip_group_check=True)

            def norm(k):
                for t in range(NT):
                    n = NT * k + t
                    pe.wait_ge(s_xn, n + 1)
                    if t >= 2:
                        pe.wait_ge(s_xt, n - 1)
                    for c in range(CC):
                        ins = pe.transpose(ps[0:CP, 6 + t % 2, 128 * c:128 * c + 128], xn[:, t, CP * c:CP * c + CP], ident)
                    ins.then_inc(s_xtp, 1)
                pe.wait_ge(s_xt, NT * (k + 1))

            def attention(l):
                nu, per = U[l], NPAIR // U[l]
                hk = 6 if l else 3
                pe.wait_ge(s_attw[l], 16 * (14 if l else 6))

                def project(w, bank, co, n):
                    for ci in range(CC):
                        ins = mm(ps[0:CP, bank, 0:HALF], w[l][:, ci, CP * co:CP * co + CP], xT[:, ci, n * HALF:(n + 1) * HALF],
                                 ci == 0, ci == CC - 1)
                    return ins

                for m in range(4):
                    project(wq, m, m // 2, m % 2).then_inc(s_qp[l], 1)
                if l:
                    pe.wait_ge(s_q[l], 4)
                    pe.wait_ge(s_pad, 5)
                    for r in range(CC * NT):
                        t, c = r // CC, r % CC
                        if r >= 2:
                            pe.wait_ge(s_rs, r - 1)
                        mm(ps[:, 4 + r % 2, 0:6 * W_REL], qT[:, c, t * 128:(t + 1) * 128],
                           emb_rev[:].rearrange("p h w -> p (h w)")).then_inc(s_rp, 1)
                for m in range(4):
                    pe.wait_ge(s_q[l], m + 1)
                    project(wk, m, m // 2, m % 2).then_inc(s_kp[l], 1)
                if l:
                    pe.wait_ge(s_rs, CC * NT)
                for p in range(NPAIR):
                    if p >= 2:
                        pe.wait_ge(s_vv[l], p - 1)
                    pe.wait_ge(s_tri[l], 2 * (p + 1))
                    for i in range(2):
                        for ci in range(CC):
                            ins = mm(ps[0:TR, 4 + p % 2, D * i:D * i + D], xT3[:, p % 2, ci, i, :], wv[l][:, ci, :], ci == 0, ci == CC - 1)
                    ins.then_inc(s_vp[l], 1)
                pe.wait_ge(s_kv[l], 2 * hk)
                pe.wait_ge(s_ka[l], 2 * hk)

                def scores(u):
                    if u >= 2:
                        pe.wait_ge(s_sr[l], u - 1)
                    for g in range(per):
                        for i in range(2):
                            b = 2 * (u * per + g) + i
                            for c in range(CC):
                                q = qT[:, c, L * b:L * b + L]
                                k = kblk[:, c, b * hk * L:(b + 1) * hk * L]
                                if l:
                                    ins = mm(ps[64 * i:64 * i + L, u % 2, hk * L * c:hk * L * (c + 1)], q, k)
                                else:
                                    ins = mm(ps[64 * i:64 * i + L, u % 2, TR * g:TR * g + TR], q, k, c == 0, c == CC - 1)
                    ins.then_inc(s_sp[l], 1)

                def turn_probs(u):
                    pe.wait_ge(s_ex[l], u + 1)
                    if u >= 2:
                        pe.wait_ge(s_pt[l], u - 1)
                    for g in range(4):
                        ins = pe.transpose(ps[0:TR, 2 + u % 2, 128 * g:128 * g + 128], prob[:, u % 2, TR * g:TR * g + TR], ident)
                    ins.then_inc(s_ptp[l], 1)

                def context(u):
                    pe.wait_ge(s_pt[l], u + 1)
                    if l and u >= 2:
                        pe.wait_ge(s_cn[l], u - 1)
                    if not l and u >= 1:
                        pe.wait_ge(s_cn[l], u)
                    for g in range(4):
                        for i in range(2):
                            p = probT[:, u % 2, 128 * g + 64 * i:128 * g + 64 * i + L]
                            if l:
                                ins = mm(ps[64 * i:64 * i + L, 4 + u % 2, 48 * g:48 * g + 48], p, vblk[:, 2 * u + i, 48 * g:48 * g + 48])
                            else:
                                ins = mm(ps[64 * i:64 * i + L, 4 + g // 2, D * (g % 2):D * (g % 2) + D], p, vblk[:, 2 * (4 * u + g) + i, :])
                    ins.then_inc(s_cp[l], 1)

                def turn_context(u):
                    pe.wait_ge(s_cn[l], u + 1)
                    for p in range(u * per, (u + 1) * per):
                        if p >= 2:
                            pe.wait_ge(s_ct[l], 2 * (p - 1))
                        for c in range(CC):
                            ins = pe.transpose(ps[0:CP, 6 + p % 2, 128 * c:128 * c + 128], ctxr[:, p, CP * c:CP * c + CP], ident)
                        ins.then_inc(s_ctp[l], 1)

                pe.wait_ge(s_vv[l], NPAIR)
                for u in range(nu + 3):
                    if u < nu:
                        scores(u)
                    if 1 <= u <= nu:
                        turn_probs(u - 1)
                    if 2 <= u <= nu + 1:
                        context(u - 2)
                    if u >= 3:
                        turn_context(u - 3)
                if l == 0:
                    for r in range(2):
                        pe.wait_ge(s_gs, r + 1)
                        same = cst("same", CP).rearrange("p (c d n) -> p c d n", c=CC, d=CC)
                        for d in range(CC):
                            for c in range(CC):
                                ins = mm(ps[0:CP, 7, NI * d:NI * d + NI], same[:, c, d, :], gsum[:, c, :], c == 0, c == CC - 1)
                        ins.then_inc(s_gp, 1)
                    pe.wait_ge(s_gn, CC)
                else:
                    pe.wait_ge(s_ct[l], CC * NPAIR)
                for t in range(NT):
                    if t >= 2:
                        pe.wait_ge(s_or[l], t - 1)
                    for ci in range(CC):
                        ins = mm(ps[:, t % 2, 0:D], ctxT[:, ci, t * 128:(t + 1) * 128], wo[l][:, ci, :], ci == 0, ci == CC - 1)
                    ins.then_inc(s_op[l], 1)

            def experts(l):
                ne = E[l]
                nl = G + ne if l else ne
                pe.wait_ge(s_pad, 16)
                pe.wait_ge(s_rtw[l], 16 * (9 if l else 1))
                for t in range(NT):
                    for ci in range(CC):
                        ins = mm(ps[:, 7, nl * t:nl * t + nl], xT[:, ci, t * 128:(t + 1) * 128], wr[l][:, ci, :], ci == 0, ci == CC - 1)
                ins.then_inc(s_lp[l], 1)
                pe.wait_ge(s_mask[l], 1)
                for t in range(NT):
                    for r in range(t + 1):
                        mm(ps[:, 6, ne * t:ne * t + ne], upto_bf[:] if r == t else ones_bf[:], mask_bf[:, r, 0:ne], r == 0, r == t)
                for r in range(NT):
                    ins = mm(ps[:, 6, NT * ne:(NT + 1) * ne], ones_bf[:], mask_bf[:, r, 0:ne], r == 0, r == NT - 1)
                ins.then_inc(s_rank[l], 1)
                if l:
                    for t in range(NT):
                        ins = pe.transpose(ps[0:32, 5 if t < 4 else 4, 128 * (t % 4):128 * (t % 4) + 128], comb[:, t, :], ident)
                    ins.then_inc(s_cbp[l], 1)
                    pe.wait_ge(s_cbt[l], 2)
                for t in range(NT):
                    o = ps[:, t // 2, D * (t % 2):D * (t % 2) + D]
                    if l:
                        ins = mm(o, combT[:, 128 * t:128 * t + 128], b2all[:], t % 2 == 0, False)
                    else:
                        ins = mm(o, zero_bf[:, 0:128], zero_bf[:, 0:D], t % 2 == 0, False)
                pe.wait_ge(s_jcol[l], 1)
                for c in range(2):
                    ins = mm(ps[0:1, 7, 256 + 128 * c:384 + 128 * c], job_e[:, c:c + 1], ident)
                ins.then_inc(s_jrow[l], 1)

                def slots(j, s):
                    pe.wait_ge(s_sel[l], j + 1)
                    for t in range(NT):
                        ins = mm(ps[:, 7, 8 * s:8 * s + 5], sel[:, s, t, :], info[:, s, t, :], t == 0, t == NT - 1)
                    ins.then_inc(s_inf[l], 1)

                def turn(i, s):
                    pe.wait_ge(s_gat[l][s], i * 16 + 16)
                    for c in range(CC):
                        o = 256 * s + 128 * c
                        ins = pe.transpose(ps[0:CP, 6, o:o + 128], xg[:, s, CP * c:CP * c + CP], ident)
                    ins.then_inc(s_xgp[l], 1)

                def first(i, j, s):
                    pe.wait_ge(s_xg[l], j + 1)
                    pe.wait_ge(s_w1[l][s], i * 16 + 16)
                    for m in range(MC):
                        for ci in range(CC):
                            ins = mm(ps[:, 3 + m // 3, 128 * (m % 3):128 * (m % 3) + 128], w1[:, s, ci, 128 * m:128 * m + 128],
                                     xgT[:, s, ci, :], ci == 0, ci == CC - 1)
                        if m % 3 == 2:
                            ins.then_inc(s_hp[l], 1)

                def second(i, j, s):
                    pe.wait_ge(s_w2[l][s], i * 16 + 16)
                    for m in range(MC):
                        if m % 3 == 0:
                            pe.wait_ge(s_hd[l], j * 2 + 1 + m // 3)
                        ins = mm(ps[:, 5, D * s:D * s + D], hid[:, m, :], w2[:, s, m, :], m == 0, m == MC - 1)
                    ins.then_inc(s_yp[l], 1)

                def scatter(j, s):
                    pe.wait_ge(s_yw[l], j + 2)
                    for t in range(NT):
                        for part in range(2):
                            ins = mm(ps[:, t // 2, D * (t % 2):D * (t % 2) + D], selT[:, s, 128 * t:128 * t + 128],
                                     yw[:, s, part], False, False)
                    return ins

                pairs = job_count(pe, l)
                for s in range(2):
                    slots(s, s)
                turn(0, 0)
                with pe.Fori(0, pairs) as i:
                    for s in range(2):
                        j = i * 2 + s
                        first(i, j, s)
                        scatter(j - 1, 1 - s)
                        slots(j + 2, s)
                        turn(i + s, 1 - s)
                        second(i, j, s)
                scatter(pairs * 2 - 1, 1).then_inc(s_done[l], 1)
                pe.wait_ge(s_gat[l][1], pairs * 16 + 16)
                for q in (s_w1[l], s_w2[l]):
                    for s in range(2):
                        pe.wait_ge(q[s], pairs * 16 + 16)

            pe.wait_ge(s_patch, 64)
            pe.wait_ge(s_pad, 2)
            pe.wait_ge(s_step[0], 1)
            for t in range(NT):
                if t >= 2:
                    pe.wait_ge(s_hemb, t - 1)
                for k in range(KF):
                    ins = mm(ps[:, t % 2, 0:D], patches[:, k, t * 128:(t + 1) * 128], tok_w[:, k, :], k == 0, k == KF - 1)
                ins.then_inc(s_emb, 1)
            pe.wait_ge(s_table, 16)
            norm(0)
            attention(0)
            norm(1)
            experts(0)
            norm(2)
            attention(1)
            norm(3)
            experts(1)


def kernel(**inputs):
    import concourse.bacc as bacc
    from concourse.bass_utils import run_bass_kernel_spmd

    a = {k: np.ascontiguousarray(v) for k, v in inputs.items()}
    n = IMG // PATCH
    x = a.pop("x").reshape(NI, NCH, n, PATCH, n, PATCH)
    a["patchesT"] = x.transpose(1, 3, 5, 0, 2, 4).reshape(FLAT, TOK)
    a["tok_WT"] = a.pop("L0_tok_W").T
    a["pos"] = np.tile(a.pop("L0_tok_pos_emb"), (NI, 1))
    for w in ("Wq", "Wk", "Wv", "Wo"):
        a[w + "T0"] = a.pop("L0_attn_" + w).T
    distance = np.clip(L - 1 - np.arange(W_REL), -MAX_REL, MAX_REL) + MAX_REL
    a["emb_rev"] = a.pop("L1_attn_rel_emb")[distance].T
    a["b1T"] = a.pop("L1_ffn_b1").reshape(E[1], MC, 128).transpose(2, 0, 1)
    for name in ("L0_attn_gn_weight", "L0_attn_gn_bias", "L1_attn_bq", "L1_attn_bk", "L1_attn_bv"):
        a[name] = a[name].reshape(CC, CP).T
    a["table"] = TABLE
    nc = bacc.Bacc("TRN2", target_bir_lowering=False, num_devices=1)
    arrays, aps = {}, {}
    for name, v in a.items():
        arrays["in_" + name] = v = np.ascontiguousarray(v)
        aps[name] = nc.dram_tensor("in_" + name, v.shape, mybir.dt.from_np(v.dtype), kind="ExternalInput").ap()
    out = nc.dram_tensor("tower_out", (TOK, D), F32, kind="ExternalOutput").ap()
    vit_tower(nc, aps, out)
    r = run_bass_kernel_spmd(nc, [arrays], core_ids=[0])
    return r.results[0]["tower_out"].reshape(NI, L, D)
```

```python
from contextlib import ExitStack

import numpy as np

import concourse.bass as bass
from concourse import mybir

F32 = mybir.dt.float32
F32R = mybir.dt.float32r
BF16 = mybir.dt.bfloat16
I32 = mybir.dt.int32
U32 = mybir.dt.uint32
ALU = mybir.AluOpType
ACT = mybir.ActivationFunctionType
AX_X = mybir.AxisListType.X

NI, NCH, IMG, PATCH = 16, 3, 96, 16
L = (IMG // PATCH) ** 2
FLAT = NCH * PATCH * PATCH
KF = FLAT // 128
TOK = NI * L
NT = -(-TOK // 128)
NP = NT * 128
LAST = TOK - (NT - 1) * 128
D = 192
CC, CP = 2, 96
M = 768
MC = M // 128
H = (3, 12)
E = (8, 32)
G, GE = 4, 8
NPAIR = NI // 2
TR = 3 * L
UW = 4 * TR
U = (2, 8)
HALF = TOK // 2
W_REL = 2 * L - 1
MAX_REL = 32
NCHUNK = NT
MOST_JOBS = 50
JOBS = 64
LN_EPS = 1e-5
GN_EPS = 1e-5
LOWEST = -3.0e38


def constants():
    p = np.arange(128)
    parts = {
        "ident": np.eye(128),
        "upto": (p[:, None] <= p[None, :]),
        "ones": np.ones((128, 128)),
        "count": np.broadcast_to(np.arange(1, NP + 129), (128, NP + 128)),
        "row": p[:, None],
        "row1": p[:, None] + 1,
        "eight": np.broadcast_to(np.arange(8), (128, 8)),
        "tile": np.broadcast_to(128 * np.arange(NT), (128, NT)),
    }
    ch = np.arange(CC)[None, :, None] * CP + p[:, None, None]
    parts["khead0"] = (ch // 64 == np.arange(3)).reshape(128, -1)
    parts["khead1"] = (p[:, None, None] // 16 == np.arange(6)) & (np.arange(CC)[None, :, None] >= 0)
    col = np.arange(D)
    parts["vhead0"] = p[:, None] // L == col // 64
    parts["vhead1"] = p[:, None] // L == (col // 16) % 3
    to = np.arange(CC)[:, None] * CP + np.arange(CP)[None, :]
    parts["same"] = (ch[:, :, :, None] // 64 == to[None, None] // 64).reshape(128, -1)
    where, cols, at = {}, [], 0
    for name, a in parts.items():
        a = np.asarray(a, np.float32).reshape(128, -1)
        where[name] = (at, a.shape[1])
        cols.append(a)
        at += a.shape[1]
    return where, np.concatenate(cols, 1)


WHERE, TABLE = constants()


def vit_tower(nc, A, out):
    with ExitStack() as ctx:
        def sb(name, shape, dt=F32):
            return ctx.enter_context(nc.sbuf_tensor(name, shape, dt))

        def sem(name):
            return ctx.enter_context(nc.semaphore(name))

        rows_dram = [nc.dram_tensor(f"rows{l}", (NP, D), F32).ap() for l in range(2)]
        rel_dram = nc.dram_tensor("reltab", (NP, H[1] * W_REL), F32)
        value_dram = [nc.dram_tensor(f"values{l}", (NP, D), F32) for l in range(2)]
        decay_dram = nc.dram_tensor("decaytab", (L, H[0] * W_REL), F32)

        table = sb("table", [128, TABLE.shape[1]])
        early = sb("early", [128, KF * (NP + D)])
        patches = early[:, 0:KF * NP].rearrange("p (k n) -> p k n", k=KF)
        tok_w = early[:, KF * NP:].rearrange("p (k n) -> p k n", k=KF)
        qrel = early[:, 0:NT * 12 * W_REL].rearrange("p (t w) -> p t w", t=NT)
        posb = sb("posb", [128, NT, D])
        tok_b = sb("tok_b", [128, D])
        h = sb("h", [128, NT, D])
        stats = sb("stats", [128, NT, 6])
        mv = sb("mv", [128, NT, 2])
        vare = sb("vare", [128, NT])
        std = sb("std", [128, NT])
        rstd = sb("rstd", [128, NT])
        xn = sb("xn", [128, NT, D])
        xT = sb("xT", [CP, CC, NP])
        wq, wk, wv, wo = [[sb(f"w{n}{l}", [CP, CC, D]) for l in range(2)] for n in "qkvo"]
        bq = sb("bq", [CP, CC])
        bk = sb("bk", [CP, CC])
        bv = sb("bv", [CP, CC])
        bkm = sb("bkm", [CP, CC, 6])
        bo = sb("bo", [128, D])
        gnw = sb("gnw", [CP, CC])
        gnb = sb("gnb", [CP, CC])
        zero_col = sb("zero_col", [128, 1])
        spare = sb("spare", [128, 16])
        qT = sb("qT", [CP, CC, NP])
        kblk = sb("kblk", [CP, CC, NI * 6 * L])
        vrow = sb("vrow", [128, NT, D])
        vblk = sb("vblk", [TR, NI, D])
        score = sb("score", [128, 2, UW])
        prob = sb("prob", [128, 2, UW])
        top = sb("top", [128, 2, 12])
        psumm = sb("psumm", [128, 8, 12])
        pinv = sb("pinv", [128, 8, 12])
        probT = sb("probT", [TR, 2, 512])
        ctxr = sb("ctxr", [128, NPAIR, D])
        ctxT = sb("ctxT", [CP, CC, NP])
        gam = sb("gam", [L, 3])
        powers = sb("powers", [L, 3, W_REL])
        decay = sb("decay", [128, 3, L])
        gsum = sb("gsum", [CP, CC, NI])
        gvar = sb("gvar", [CP, CC, NI])
        gstd = sb("gstd", [CP, CC, NI])
        grs = sb("grs", [CP, CC, NI])
        gscale = sb("gscale", [CP, CC, NI])
        emb_rev = sb("emb_rev", [CP, 6, W_REL])
        rel = sb("rel", [128, NPAIR, UW])
        ones_bf = sb("ones_bf", [128, 128], BF16)
        upto_bf = sb("upto_bf", [128, 128], BF16)
        ident_bf = sb("ident_bf", [128, JOBS], BF16)
        zero_bf = sb("zero_bf", [128, 512], BF16)
        wr = [sb("wr0", [CP, CC, E[0]]), sb("wr1", [CP, CC, G + E[1]])]
        rbias = sb("rbias", [128, G + E[1]])
        RW = 5
        logit = sb("logit", [128, NT * RW, 8])
        pick = [sb(f"pick{n}", [128, NT * RW, 8]) for n in range(2)]
        rank8 = sb("rank8", [128, NT * RW, 8])
        best = [sb(f"best{n}", [128, NT * RW]) for n in range(2)]
        first = sb("first", [128, NT * RW])
        gate = [sb(f"gate{n}", [128, NT * RW]) for n in range(4)]
        gated = sb("gated", [128, NT * RW, 8])
        comb = sb("comb", [128, NT, 32])
        crest = sb("crest", [128, NT, 32])
        mask_bf = sb("mask_bf", [128, NT, 32], BF16)
        wparts = sb("wparts", [128, NT, 32, 3], BF16)
        pos = sb("pos", [128, NT, 32])
        over = sb("over", [128, 32, NCHUNK])
        nchunk = sb("nchunk", [128, 32])
        ends = sb("ends", [128, 32])
        before = sb("before", [128, 2, 32])
        job_e = sb("job_e", [128, 2], BF16)
        job_t = sb("job_t", [128, 2])
        jobs = sb("jobs", [1, 2 * JOBS], I32)
        njobs = sb("njobs", [1, 1], I32)
        combT = sb("combT", [32, NP])
        b1all = sb("b1all", [128, 32, MC])
        b2all = sb("b2all", [32, D])
        w1 = sb("w1", [CP, 2, CC, M])
        w2 = sb("w2", [128, 2, MC, D])
        sel = sb("sel", [128, 2, NT, 128], BF16)
        info = sb("info", [128, 2, NT, 5], BF16)
        nxt = sb("nxt", [128, 2, 2])
        cur = sb("cur", [128, 2, 2])
        idx = sb("idx", [128, 2], U32)
        xg = sb("xg", [128, 2, D])
        xgT = sb("xgT", [CP, 2, CC, 128])
        hid = sb("hid", [128, MC, 128])
        yw = sb("yw", [128, 2, 2, D], F32R)
        selT = sb("selT", [128, 2, NP], F32R)

        ps = ctx.enter_context(nc.psum_tensor("ps", [128, 8, 512], F32))

        def cst(name, rows=128):
            at, n = WHERE[name]
            return table[0:rows, at:at + n]

        ident = cst("ident")

        def view(ap, dims, offset=0):
            return bass.AP(ap.tensor, ap.offset + offset, [list(ap.ap[0])] + [list(d) for d in dims])

        s_table = sem("table_loaded")
        s_patch = [sem(f"patches_loaded{k}") for k in range(KF)]
        s_posld = sem("pos_loaded")
        s_attw = [sem("attn0_weights_loaded"), sem("attn1_weights_loaded")]
        s_rtw = [sem("router0_loaded"), sem("router1_loaded")]
        s_pad = sem("pads_zeroed")
        s_posb = sem("pos_plus_bias")
        s_emb = sem("embedding_in_psum")
        s_hemb = sem("embedding_read")
        s_step = [sem(f"vector_step{n}") for n in range(5)]
        s_lnvar = sem("ln_variance")
        s_lnstd = sem("ln_deviation")
        s_xn = sem("normed_rows")
        s_xtp = sem("normed_in_psum")
        s_xt = sem("normed_columns")
        s_gam = sem("gammas_loaded")
        s_pow = sem("powers_ready")
        s_powst = sem("powers_stored")
        s_decay = sem("decay_loaded")
        s_qp, s_q, s_kp, s_kv, s_ka, s_vp, s_vv, s_sp, s_sr, s_sh, s_ex, s_sum, s_ptp, s_pt, s_cp, s_cn, s_ctp, s_ct, s_op, s_or = [
            [sem(f"{n}{l}") for l in range(2)] for n in (
                "queries_in_psum", "queries_ready", "keys_in_psum", "keys_by_vector", "keys_by_scalar",
                "values_masked_pool", "values_masked", "scores_in_psum", "scores_read", "scores_shifted",
                "exp_ready", "sums_ready", "probsT_in_psum", "probsT_ready", "context_in_psum",
                "context_ready", "contextT_in_psum", "contextT_ready", "projected", "projected_read")]
        s_vtp, s_vtr = [[sem(f"{n}{l}") for l in range(2)] for n in ("value_rows_in_psum", "value_rows_ready")]
        s_vst, s_vld = [[sem(f"{n}{l}") for l in range(2)] for n in ("values_stored", "values_loaded")]
        s_gs = sem("group_sums")
        s_gp = sem("group_sums_in_psum")
        s_gc = sem("centred")
        s_gq = sem("squared")
        s_gv = sem("group_variance")
        s_gd = sem("group_deviation")
        s_gn = sem("group_normed")
        s_rp = sem("rel_in_psum")
        s_rs = sem("rel_rows_ready")
        s_rst = sem("rel_rows_stored")
        s_rel = sem("rel_loaded")
        s_hbo = sem("bias_added")
        s_bkm = sem("key_bias_masked")
        (s_rows, s_lp, s_rx, s_re, s_mask, s_rank, s_jcol, s_jrow, s_jobs, s_cbp, s_cbt, s_acc, s_hp, s_hd,
         s_sel, s_inf, s_idx, s_xgp, s_xg, s_yp, s_yw, s_done) = [
            [sem(f"{n}{l}") for l in range(2)] for n in (
                "rows_stored", "logits_in_psum", "router_shifted", "router_exp", "mask_ready",
                "ranks_in_psum", "job_columns", "job_rows_in_psum", "jobs_ready", "combineT_in_psum",
                "combineT_ready", "sums_begun", "hidden_in_psum", "hidden_ready", "selection_ready",
                "slots_in_psum", "slots_ready", "gatheredT_in_psum", "gatheredT_ready", "outputs_in_psum",
                "outputs_ready", "sums_complete")]
        s_w1, s_w2, s_gat = [[[sem(f"{n}{l}_{s}") for s in range(2)] for l in range(2)]
                             for n in ("w1_loaded", "w2_loaded", "rows_gathered")]
        s_asked = [sem(f"gather_asked{l}") for l in range(2)]
        s_hmoe = [sem(f"experts_added{l}") for l in range(2)]
        s_stored = sem("output_stored")

        W1d = [A["L0_ffn_wi"], A["L1_ffn_W1"]]
        W2d = [A["L0_ffn_wo"], A["L1_ffn_W2"]]
        chunked = "(c p) n -> p c n"

        def key_slot(l, co, n, hh):
            hk = 6 if l else 3
            return view(kblk[:, co, 0:1], [[hk * L, NI // 2], [1, L]], (n * NI // 2 * hk + hh) * L)

        def job_count(eng, l):
            eng.wait_ge(s_jobs[l], 1)
            return eng.snap((eng.value_load(njobs[0:1, 0:1], min_val=1, max_val=MOST_JOBS) + 1) // 2)

        def job_expert(eng, l, j):
            return eng.value_load(jobs[0:1, bass.ds(j, 1)], min_val=0, max_val=E[l] - 1)

        block = ctx.enter_context(nc.Block())

        @block.sync
        def _(sp):
            for k in range(KF):
                sp.dma_start(patches[:, k, 0:TOK], A["patchesT"][128 * k:128 * k + 128]).then_inc(s_patch[k], 16)
                sp.dma_start(tok_w[:, k, :], A["tok_WT"][128 * k:128 * k + 128]).then_inc(s_patch[k], 16)
            sp.dma_start(posb[:, 0:NT - 1, :], A["pos"][0:(NT - 1) * 128].rearrange("(t p) n -> p t n", p=128)).then_inc(s_posld, 16)
            sp.dma_start(posb[0:LAST, NT - 1, :], A["pos"][(NT - 1) * 128:TOK]).then_inc(s_posld, 16)
            sp.dma_start(tok_b[:], A["L0_tok_b"].partition_broadcast(128)).then_inc(s_posld, 16)
            sp.dma_start(table[:], A["table"]).then_inc(s_table, 16)
            sp.dma_start(gam[:], A["L0_attn_gammas"].partition_broadcast(L)).then_inc(s_gam, 16)
            for w, n in ((wq, "WqT0"), (wk, "WkT0"), (wv, "WvT0"), (wo, "WoT0")):
                sp.dma_start(w[0][:], A[n].rearrange(chunked, p=CP)).then_inc(s_attw[0], 16)
            for b, n in ((gnw, "L0_attn_gn_weight"), (gnb, "L0_attn_gn_bias")):
                sp.dma_start(b[:], A[n]).then_inc(s_attw[0], 16)
            sp.dma_start(wr[0][:], A["L0_ffn_router_w"].rearrange(chunked, p=CP)).then_inc(s_rtw[0], 16)
            sp.wait_ge(s_pow, 1)
            sp.dma_start(decay_dram.ap(), powers[:].rearrange("q h w -> q (h w)")).then_inc(s_powst, 16)
            sp.wait_ge(s_powst, 16)
            sp.wait_ge(s_pad, 1)
            sheared = bass.AP(decay_dram, L - 1, [[3 * W_REL - 1, L], [W_REL, 3], [1, L]])
            for i in range(2):
                sp.dma_start(decay[64 * i:64 * i + L], sheared).then_inc(s_decay, 16)
            for w, n in ((wq, "Wq"), (wk, "Wk"), (wv, "Wv"), (wo, "Wo")):
                sp.dma_start(w[1][:], A["L1_attn_" + n].rearrange(chunked, p=CP)).then_inc(s_attw[1], 16)
            for b, n in ((bq, "bq"), (bk, "bk"), (bv, "bv")):
                sp.dma_start(b[:], A["L1_attn_" + n]).then_inc(s_attw[1], 16)
            sp.dma_start(bo[:], A["L1_attn_bo"].partition_broadcast(128)).then_inc(s_attw[1], 16)
            sp.wait_ge(s_pad, 8)
            for k in range(6):
                sp.dma_start(emb_rev[16 * k:16 * k + 16, k, :], A["emb_rev"]).then_inc(s_attw[1], 16)
            sp.dma_start(wr[1][:, :, 0:G], A["L1_ffn_Wg"].rearrange(chunked, p=CP)).then_inc(s_rtw[1], 16)
            for g in range(G):
                sp.dma_start(wr[1][:, :, G + GE * g:G + GE * (g + 1)], A["L1_ffn_Wge"][g].rearrange(chunked, p=CP)).then_inc(s_rtw[1], 16)
            sp.dma_start(rbias[:, 0:G], A["L1_ffn_bg"].partition_broadcast(128)).then_inc(s_rtw[1], 16)
            sp.dma_start(rbias[:, G:], A["L1_ffn_bge"].rearrange("g e -> (g e)").partition_broadcast(128)).then_inc(s_rtw[1], 16)
            sp.dma_start(b1all[:], A["b1T"]).then_inc(s_rtw[1], 16)
            sp.dma_start(b2all[:], A["L1_ffn_b2"]).then_inc(s_rtw[1], 16)

            def values(l):
                sp.wait_ge(s_vtr[l], NT)
                sp.dma_start(value_dram[l].ap().rearrange("(t p) n -> p t n", p=128), vrow[:]).then_inc(s_vst[l], 16)
                sp.wait_ge(s_vst[l], 16)
                for r in range(3):
                    by_image = bass.AP(value_dram[l], 0, [[D, L], [L * D, NI], [1, D]])
                    sp.dma_start(vblk[r * L:(r + 1) * L], by_image).then_inc(s_vld[l], 16)

            def experts(l):
                sp.wait_ge(s_xn, NT * (2 * l + 2))
                sp.dma_start(rows_dram[l].rearrange("(t p) n -> p t n", p=128), xn[:]).then_inc(s_rows[l], 16)

                def load(j, s, e, first=False):
                    if not first:
                        sp.wait_ge(s_hp[l], j * 2 - 2)
                    sp.dma_start(w1[:, s], W1d[l][bass.ds(e, 1)].rearrange("e (c p) m -> p (e c) m", p=CP)).then_inc(s_w1[l][s], 16)
                    if not first:
                        sp.wait_ge(s_yp[l], j - 1)
                    sp.dma_start(w2[:, s], W2d[l][bass.ds(e, 1)].rearrange("e (c p) m -> p (e c) m", p=128)).then_inc(s_w2[l][s], 16)

                sp.wait_ge(s_jobs[l], 1)
                load(0, 0, job_expert(sp, l, 0), first=True)
                e = job_expert(sp, l, 1)
                sp.wait_ge(s_gat[l][0], 16)
                load(1, 1, e, first=True)
                pairs = job_count(sp, l)
                with sp.Fori(0, pairs) as i:
                    for s in range(2):
                        load(i * 2 + s + 2, s, job_expert(sp, l, i * 2 + s + 2))

            values(0)
            experts(0)
            values(1)
            for t in range(NT):
                sp.wait_ge(s_rs, 2 * t + 2)
                sp.dma_start(rel_dram.ap()[t * 128:(t + 1) * 128], qrel[:, t, :]).then_inc(s_rst, 16)
            sp.wait_ge(s_rst, 16 * NT)
            for b in range(NI):
                sheared = bass.AP(rel_dram, L * b * 12 * W_REL + L - 1, [[12 * W_REL - 1, L], [W_REL, 12], [1, L]])
                sp.dma_start(rel[64 * (b % 2):64 * (b % 2) + L, b // 2, :].rearrange("p (h k) -> p h k", k=L),
                             sheared).then_inc(s_rel, 16)
            experts(1)
            sp.wait_ge(s_hmoe[1], 3)
            sp.dma_start(out[0:(NT - 1) * 128].rearrange("(t p) n -> p t n", p=128), h[:, 0:NT - 1, :]).then_inc(s_stored, 16)
            sp.dma_start(out[(NT - 1) * 128:TOK], h[0:LAST, NT - 1, :]).then_inc(s_stored, 16)
            sp.wait_ge(s_stored, 32)
            sp.wait_ge(s_powst, 16)
            for l in range(2):
                sp.wait_ge(s_rows[l], 16)

        @block.gpsimd
        def _(pool):
            for n, pad in enumerate((
                    decay[:],
                    patches[:, :, TOK:NP],
                    posb[64:128, NT - 1, :],
                    zero_col[:],
                    qT[:, :, TOK:NP],
                    ctxT[:, :, TOK:NP],
                    rel[:],
                    emb_rev[:],
                    selT[:].bitcast(F32),
                    zero_bf[:],
            )):
                if n:
                    pool.wait_ge(s_pad, n)
                pool.memset(pad, 0.0).then_inc(s_pad, 1)
            pool.wait_ge(s_pad, 10)
            pool.wait_ge(s_posld, 48)
            pool.tensor_tensor(posb[:], posb[:], view(tok_b[:], [[0, NT], [1, D]]), ALU.add).then_inc(s_posb, 1)
            pool.wait_ge(s_table, 16)
            pool.tensor_copy(ones_bf[:], cst("ones")).then_inc(s_pad, 1)
            pool.tensor_copy(upto_bf[:], cst("upto")).then_inc(s_pad, 1)
            pool.tensor_copy(ident_bf[:], ident[:, 0:JOBS]).then_inc(s_pad, 1)
            for s in range(2):
                pool.tensor_copy(info[:, s, :, 0], view(cst("row1"), [[0, NT]])).then_inc(s_pad, 1)
                pool.tensor_copy(info[:, s, :, 1], cst("tile")).then_inc(s_pad, 1)

            def gathers(l):
                pool.wait_ge(s_rows[l], 16)
                def gather(j, s):
                    pool.wait_ge(s_idx[l], j + 1)
                    pool.sem_inc(s_asked[l], 1)
                    pool.indirect_dma_start(xg[:, s, :], None, rows_dram[l],
                                            bass.IndirectOffsetOnAxis(idx[:, s:s + 1], 0)).then_inc(s_gat[l][s], 16)

                pairs = job_count(pool, l)
                for s in range(2):
                    gather(s, s)
                with pool.Fori(0, pairs) as i:
                    for s in range(2):
                        gather(i * 2 + s + 2, s)

            def mask_values(l):
                pool.wait_ge(s_vld[l], 16 * 3)
                pool.wait_ge(s_table, 16)
                half = vblk[:, NI // 2:NI, :]
                pool.tensor_tensor(half, half, view(cst(f"vhead{l}", TR), [[0, NI // 2], [1, D]]), ALU.mult).then_inc(s_vp[l], 1)

            mask_values(0)
            gathers(0)
            mask_values(1)
            pool.wait_ge(s_attw[1], 16 * 14)
            pool.wait_ge(s_xn, NT * 3)
            pool.tensor_tensor(h[:], h[:], view(bo[:], [[0, NT], [1, D]]), ALU.add).then_inc(s_hbo, 1)
            gathers(1)

        @block.scalar
        def _(act):
            spares = iter(range(16))

            def table_for(func):
                n = next(spares)
                act.activation(spare[:, n:n + 1], zero_col[:], func)

            def norm(k):
                act.wait_ge(s_lnvar, k + 1)
                act.activation(std[:], vare[:], ACT.Sqrt).then_inc(s_lnstd, 1)
                for t in range(NT):
                    n = NT * k + t
                    act.wait_ge(s_xtp, n + 1)
                    act.activation(xT[:, :, t * 128:(t + 1) * 128],
                                   ps[0:CP, 6 + t % 2, 0:256].rearrange("p (c n) -> p c n", c=CC),
                                   ACT.Identity).then_inc(s_xt, 1)

            def attention(l):
                act.wait_ge(s_pad, 6)
                if l:
                    act.wait_ge(s_attw[1], 16 * 14)
                for t in range(NT):
                    act.wait_ge(s_vtp[l], t + 1)
                    act.activation(vrow[:, t, :], ps[:, 4 + t % 2, 0:D], ACT.Identity).then_inc(s_vtr[l], 1)
                for m in range(4):
                    co, n = m // 2, m % 2
                    act.wait_ge(s_qp[l], m + 1)
                    act.activation(qT[:, co, n * HALF:(n + 1) * HALF], ps[0:CP, m, 0:HALF], ACT.Identity,
                                   bias=bq[:, co:co + 1] if l else zero_col[0:CP]).then_inc(s_q[l], 1)
                if l:
                    for t in range(NT):
                        for c in range(CC):
                            r = 2 * t + c
                            act.wait_ge(s_rp, r + 1)
                            act.activation(qrel[:, t, c * 6 * W_REL:(c + 1) * 6 * W_REL], ps[:, 4 + r % 2, 0:6 * W_REL],
                                           ACT.Identity).then_inc(s_rs, 1)
                    act.wait_ge(s_bkm, 1)
                hk = H[l] // 2 if l else 3
                for m in (1, 3):
                    co, n = m // 2, m % 2
                    act.wait_ge(s_kp[l], m + 1)
                    for hh in range(hk):
                        mcol = WHERE[f"khead{l}"][0] + co * hk + hh
                        act.activation(key_slot(l, co, n, hh), ps[0:CP, m, 0:HALF].rearrange("p (b k) -> p b k", k=L),
                                       ACT.Identity, scale=table[0:CP, mcol:mcol + 1],
                                       bias=bkm[:, co, hh:hh + 1] if l else zero_col[0:CP]).then_inc(s_ka[l], 1)
                table_for(ACT.Exp)
                per = NPAIR // U[l]
                for u in range(U[l] + 3):
                    if u < U[l]:
                        act.wait_ge(s_sh[l], u + 1)
                        if u >= 2:
                            act.wait_ge(s_ptp[l], u - 1)
                            act.wait_ge(s_sum[l], u - 1)
                        act.activation(prob[:, u % 2], score[:, u % 2], ACT.Exp, scale=0.25 if l else 1.0).then_inc(s_ex[l], 1)
                    if 1 <= u <= U[l]:
                        v = u - 1
                        act.wait_ge(s_ptp[l], v + 1)
                        if v >= 2:
                            act.wait_ge(s_cp[l], v - 1)
                        act.activation(probT[:, v % 2], ps[0:TR, 2 + v % 2, :], ACT.Identity).then_inc(s_pt[l], 1)
                    if u >= 3:
                        for p in range((u - 3) * per, (u - 2) * per):
                            act.wait_ge(s_ctp[l], p + 1)
                            for c in range(CC):
                                src = view(ps[0:CP, 6 + p % 2, 128 * c:128 * c + 1], [[64, 2], [1, L]])
                                act.activation(ctxT[:, c, 72 * p:72 * p + 72].rearrange("p (i k) -> p i k", k=L), src,
                                               ACT.Identity, bias=bv[:, c:c + 1] if l else zero_col[0:CP]).then_inc(s_ct[l], 1)
                if l == 0:
                    table_for(ACT.Sqrt)
                    for c in range(CC):
                        act.wait_ge(s_gc, c + 1)
                        act.activation(kblk[:, c, 0:TOK], ctxT[:, c, 0:TOK], ACT.Square).then_inc(s_gq, 1)
                    act.wait_ge(s_gv, 1)
                    act.activation(gstd[:], gvar[:], ACT.Sqrt).then_inc(s_gd, 1)

            def experts(l):
                if l == 0:
                    act.wait_ge(s_rx[0], 1)
                    act.activation(pick[1][:, 0:NT, :], pick[0][:, 0:NT, :], ACT.Exp).then_inc(s_re[0], 1)
                else:
                    act.wait_ge(s_rx[1], 1)
                    act.activation(gate[1][:], gate[0][:], ACT.Exp).then_inc(s_re[1], 1)
                    act.wait_ge(s_cbp[1], 1)
                    act.activation(combT[:, 0:512], ps[0:32, 5, :], ACT.Identity).then_inc(s_cbt[1], 1)
                    act.activation(combT[:, 512:NP], ps[0:32, 4, 0:128], ACT.Identity).then_inc(s_cbt[1], 1)

                def columns(j, s):
                    act.wait_ge(s_xgp[l], j + 1)
                    act.activation(xgT[:, s], ps[0:CP, 6, 256 * s:256 * s + 256].rearrange("p (c n) -> p c n", c=CC),
                                   ACT.Identity).then_inc(s_xg[l], 1)

                def hidden(j, s):
                    if l:
                        e = job_expert(act, l, j)
                    for b in range(2):
                        act.wait_ge(s_hp[l], j * 2 + b + 1)
                        if l == 0:
                            ins = act.activation(hid[:, 3 * b:3 * b + 3, :].rearrange("p m n -> p (m n)"),
                                                 ps[:, 3 + b, 0:384], ACT.Relu)
                        else:
                            for m in range(3):
                                ins = act.activation(hid[:, 3 * b + m, :], ps[:, 3 + b, 128 * m:128 * m + 128], ACT.Gelu,
                                                     bias=b1all[:, bass.ds(e, 1), 3 * b + m])
                        ins.then_inc(s_hd[l], 1)

                table_for(ACT.Gelu if l else ACT.Relu)
                pairs = job_count(act, l)
                columns(0, 0)
                with act.Fori(0, pairs) as i:
                    for s in range(2):
                        hidden(i * 2 + s, s)
                        columns(i * 2 + s + 1, 1 - s)

            act.wait_ge(s_pad, 4)
            table_for(ACT.Sqrt)
            norm(0)
            attention(0)
            norm(1)
            table_for(ACT.Exp)
            experts(0)
            table_for(ACT.Sqrt)
            norm(2)
            attention(1)
            table_for(ACT.Sqrt)
            norm(3)
            table_for(ACT.Exp)
            experts(1)

        @block.vector
        def _(dve):
            stretch, steps = 0, 0

            def step(ins, before=0):
                nonlocal steps
                steps += 1
                ins.then_inc(s_step[stretch], 1)
                dve.wait_ge(s_step[stretch], before + steps)

            def next_stretch():
                nonlocal stretch, steps
                stretch, steps = stretch + 1, 0

            for bank in (0, 1, 4, 5):
                ins = dve.memset(ps[:, bank, :], 0.0)
            step(ins)

            step(dve.memset(powers[:], 0.0))
            dve.wait_ge(s_gam, 16)
            at = L - 1
            step(dve.memset(powers[:, :, at:at + 1], 1.0))
            step(dve.tensor_copy(powers[:, :, at + 1:at + 2], gam[:].rearrange("p (h o) -> p h o", o=1)))
            n = 1
            while n < L - 1:
                m = min(n, L - 1 - n)
                step(dve.tensor_tensor(powers[:, :, at + n + 1:at + n + m + 1], powers[:, :, at + 1:at + m + 1],
                                       view(powers[:, :, at + n:at + n + 1], [[W_REL, 3], [0, m]]), ALU.mult))
                n += m
            dve.tensor_scalar(powers[:], powers[:], 0.125, None, ALU.mult).then_inc(s_pow, 1)

            dve.wait_ge(s_posb, 1)

            def embed():
                for t in range(NT + 1):
                    if t < NT:
                        dve.wait_ge(s_emb, t + 1)
                        dve.tensor_tensor(h[:, t, :], ps[:, t, 0:D], posb[:, t, :], ALU.add).then_inc(s_hemb, 1)
                    if t:
                        dve.wait_ge(s_hemb, t)
                        ins = dve.bn_stats(stats[:, t - 1, :], h[:, t - 1, :])
                step(ins)

            def norm(k):
                for t in range(NT):
                    ins = dve.bn_aggr(mv[:, t, :], stats[:, t, :])
                step(ins)
                dve.tensor_scalar(vare[:], mv[:, :, 1], LN_EPS, None, ALU.add).then_inc(s_lnvar, 1)
                dve.wait_ge(s_lnstd, k + 1)
                step(dve.reciprocal(rstd[:], std[:]))
                for t in range(NT):
                    dve.tensor_scalar(xn[:, t, :], h[:, t, :], mv[:, t, 0:1], rstd[:, t:t + 1], ALU.subtract, ALU.mult).then_inc(s_xn, 1)

            def attention(l):
                nu, per = U[l], NPAIR // U[l]
                hk = 6 if l else 3
                if l:
                    dve.wait_ge(s_attw[1], 16 * 14)
                    dve.tensor_tensor(bkm[:], view(bk[:], [[1, CC], [0, 6]]),
                                      cst("khead1", CP).rearrange("p (c h) -> p c h", c=CC), ALU.mult).then_inc(s_bkm, 1)
                for m in (0, 2):
                    co, n = m // 2, m % 2
                    dve.wait_ge(s_kp[l], m + 1)
                    for hh in range(hk):
                        mcol = WHERE[f"khead{l}"][0] + co * hk + hh
                        src = ps[0:CP, m, 0:HALF].rearrange("p (b k) -> p b k", k=L)
                        dve.tensor_scalar(key_slot(l, co, n, hh), src, bk[:, co:co + 1] if l else 0.0,
                                          table[0:CP, mcol:mcol + 1], ALU.add, ALU.mult).then_inc(s_kv[l], 1)
                dve.wait_ge(s_vld[l], 16 * 3)
                half = vblk[:, 0:NI // 2, :]
                dve.tensor_tensor(half, half, view(cst(f"vhead{l}", TR), [[0, NI // 2], [1, D]]), ALU.mult).then_inc(s_vv[l], 1)
                if l:
                    dve.wait_ge(s_rel, 16 * NI)
                else:
                    dve.wait_ge(s_decay, 32)
                hw = D // H[l]
                for u in range(nu + 2):
                    if u < nu:
                        dve.wait_ge(s_sp[l], u + 1)
                        if u >= 2:
                            dve.wait_ge(s_ex[l], u - 1)
                        if l:
                            ins = dve.tensor_tensor(score[:, u % 2], ps[:, u % 2, 0:UW], rel[:, u, :], ALU.add)
                        else:
                            ins = dve.tensor_tensor(score[:, u % 2].rearrange("p (g k) -> p g k", g=4),
                                                    ps[:, u % 2, 0:UW].rearrange("p (g k) -> p g k", g=4),
                                                    view(decay[:], [[0, 4], [1, TR]]), ALU.mult)
                        ins.then_inc(s_sr[l], 1)
                        dve.wait_ge(s_sr[l], u + 1)
                        s3 = score[:, u % 2].rearrange("p (h k) -> p h k", k=L)
                        step(dve.tensor_reduce(top[:, u % 2], s3, AX_X, ALU.max))
                        dve.tensor_tensor(s3, s3, view(top[:, u % 2], [[1, 12], [0, L]]), ALU.subtract).then_inc(s_sh[l], 1)
                    if 1 <= u <= nu:
                        v = u - 1
                        dve.wait_ge(s_ex[l], v + 1)
                        dve.tensor_reduce(psumm[:, v], prob[:, v % 2].rearrange("p (h k) -> p h k", k=L), AX_X, ALU.add).then_inc(s_sum[l], 1)
                        dve.wait_ge(s_sum[l], v + 1)
                        step(dve.reciprocal(pinv[:, v], psumm[:, v]))
                    if u >= 2:
                        v = u - 2
                        dve.wait_ge(s_cp[l], v + 1)
                        if l:
                            dve.tensor_tensor(ctxr[:, v, :].rearrange("p (h n) -> p h n", n=hw),
                                              ps[:, 4 + v % 2, 0:D].rearrange("p (h n) -> p h n", n=hw),
                                              view(pinv[:, v], [[1, 12], [0, hw]]), ALU.mult).then_inc(s_cn[l], 1)
                        else:
                            for b in range(2):
                                ins = dve.tensor_tensor(
                                    ctxr[:, 4 * v + 2 * b:4 * v + 2 * b + 2, :].rearrange("p g (h n) -> p (g h) n", n=hw),
                                    ps[:, 4 + b, 0:2 * D].rearrange("p (h n) -> p h n", n=hw),
                                    view(pinv[:, v], [[1, 6], [0, hw]], 6 * b), ALU.mult)
                            ins.then_inc(s_cn[l], 1)
                if l == 0:
                    c4 = ctxT[:, :, 0:TOK].rearrange("p c (b k) -> p c b k", k=L)
                    q4 = kblk[:, :, 0:TOK].rearrange("p c (b k) -> p c b k", k=L)
                    spread = [[1, NI], [0, L]]
                    for half in range(2):
                        dve.wait_ge(s_ct[0], NPAIR * (half + 1))
                        b = slice(half * NI // 2, (half + 1) * NI // 2)
                        dve.tensor_reduce(gsum[:, :, b], c4[:, :, b], AX_X, ALU.add).then_inc(s_gs, 1)
                    dve.wait_ge(s_gp, 1)
                    step(dve.tensor_scalar(gvar[:], ps[0:CP, 7, 0:CC * NI].rearrange("p (c b) -> p c b", c=CC),
                                           1.0 / (64 * L), None, ALU.mult))
                    for c in range(CC):
                        dve.tensor_tensor(c4[:, c], c4[:, c], view(gvar[:, c], spread), ALU.subtract).then_inc(s_gc, 1)
                    for c in range(CC):
                        dve.wait_ge(s_gq, c + 1)
                        dve.tensor_reduce(gsum[:, c], q4[:, c], AX_X, ALU.add).then_inc(s_gs, 1)
                    dve.wait_ge(s_gp, 2)
                    dve.tensor_scalar(gvar[:], ps[0:CP, 7, 0:CC * NI].rearrange("p (c b) -> p c b", c=CC),
                                      1.0 / (64 * L), GN_EPS, ALU.mult, ALU.add).then_inc(s_gv, 1)
                    dve.wait_ge(s_gd, 1)
                    step(dve.reciprocal(grs[:], gstd[:]))
                    step(dve.tensor_tensor(gscale[:], grs[:], view(gnw[:], [[1, CC], [0, NI]]), ALU.mult))
                    for c in range(CC):
                        ins = dve.tensor_tensor(c4[:, c], c4[:, c], view(gscale[:, c], spread), ALU.mult)
                    step(ins)
                    for c in range(CC):
                        dve.tensor_scalar(ctxT[:, c, 0:TOK], ctxT[:, c, 0:TOK], gnb[:, c:c + 1], None, ALU.add).then_inc(s_gn, 1)
                else:
                    dve.wait_ge(s_hbo, 1)
                for t in range(NT + 1):
                    if t < NT:
                        dve.wait_ge(s_op[l], t + 1)
                        dve.tensor_tensor(h[:, t, :], ps[:, t % 2, 0:D], h[:, t, :], ALU.add).then_inc(s_or[l], 1)
                    if t:
                        dve.wait_ge(s_or[l], t)
                        ins = dve.bn_stats(stats[:, t - 1, :], h[:, t - 1, :])
                step(ins)

            def choose(x, n, rows, which):
                step(dve.tensor_reduce(best[which][:, 0:rows], x, AX_X, ALU.max))
                b = view(best[which][:], [[1, rows], [0, 8]])
                step(dve.tensor_tensor(rank8[:, 0:rows], x, b, ALU.is_equal))
                step(dve.scalar_tensor_tensor(out=rank8[:, 0:rows], in0=rank8[:, 0:rows], scalar=-8.0,
                                              in1=view(cst("eight"), [[0, rows], [1, 8]]), op0=ALU.mult, op1=ALU.add))
                step(dve.tensor_reduce(first[:, 0:rows], rank8[:, 0:rows], AX_X, ALU.min))
                step(dve.tensor_tensor(pick[which][:, 0:rows], rank8[:, 0:rows], view(first[:], [[1, rows], [0, 8]]), ALU.is_equal))

            def route(l):
                ne = E[l]
                dve.wait_ge(s_lp[l], 1)
                if l == 0:
                    rows = NT
                    step(dve.tensor_copy(logit[:, 0:rows, :], ps[:, 5, 0:8 * NT].rearrange("p (t e) -> p t e", e=8)))
                    step(dve.tensor_reduce(best[0][:, 0:rows], logit[:, 0:rows, :], AX_X, ALU.max))
                    dve.tensor_tensor(pick[0][:, 0:rows], logit[:, 0:rows], view(best[0][:], [[1, rows], [0, 8]]), ALU.subtract).then_inc(s_rx[0], 1)
                    dve.wait_ge(s_re[0], 1)
                    step(dve.tensor_reduce(gate[0][:, 0:rows], pick[1][:, 0:rows], AX_X, ALU.add))
                    step(dve.reciprocal(gate[1][:, 0:rows], gate[0][:, 0:rows]))
                    step(dve.tensor_tensor(logit[:, 0:rows], pick[1][:, 0:rows], view(gate[1][:], [[1, rows], [0, 8]]), ALU.mult))
                    choose(logit[:, 0:rows], 8, rows, 0)
                    step(dve.tensor_tensor(comb[:, :, 0:ne], pick[0][:, 0:rows], view(best[0][:], [[1, rows], [0, 8]]), ALU.mult))
                else:
                    rows = NT * RW
                    dve.wait_ge(s_rtw[1], 16 * 9)
                    step(dve.memset(logit[:], LOWEST))
                    l4 = logit[:].rearrange("p (t r) e -> p t r e", r=RW)
                    step(dve.tensor_tensor(l4[:, :, 0, 0:G], ps[:, 5, 0:36 * NT].rearrange("p (t e) -> p t e", t=NT)[:, :, 0:G],
                                           view(rbias[:], [[0, NT], [1, G]]), ALU.add))
                    for t in range(NT):
                        ins = dve.tensor_tensor(l4[:, t, 1:RW, :], ps[:, 5, 36 * t + G:36 * t + 36].rearrange("p (g e) -> p g e", e=GE),
                                                rbias[:, G:].rearrange("p (g e) -> p g e", e=GE), ALU.add)
                    step(ins)
                    choose(logit[:], 8, rows, 0)
                    step(dve.scalar_tensor_tensor(out=logit[:].rearrange("p r e -> p (r e)"), in0=pick[0][:].rearrange("p r e -> p (r e)"),
                                                  scalar=LOWEST, in1=logit[:].rearrange("p r e -> p (r e)"), op0=ALU.mult, op1=ALU.add))
                    choose(logit[:], 8, rows, 1)
                    dve.tensor_tensor(gate[0][:], best[1][:], best[0][:], ALU.subtract).then_inc(s_rx[1], 1)
                    dve.wait_ge(s_re[1], 1)
                    step(dve.tensor_scalar(gate[2][:], gate[1][:], 1.0, None, ALU.add))
                    step(dve.reciprocal(gate[3][:], gate[2][:]))
                    step(dve.tensor_tensor(gate[2][:], gate[1][:], gate[3][:], ALU.mult))
                    step(dve.tensor_tensor(pick[0][:], pick[0][:], view(gate[3][:], [[1, rows], [0, 8]]), ALU.mult))
                    step(dve.tensor_tensor(pick[1][:], pick[1][:], view(gate[2][:], [[1, rows], [0, 8]]), ALU.mult))
                    step(dve.tensor_tensor(gated[:], pick[0][:], pick[1][:], ALU.add))
                    for t in range(NT):
                        ins = dve.tensor_tensor(comb[:, t, :].rearrange("p (g e) -> p g e", e=GE), gated[:, RW * t + 1:RW * t + RW, :],
                                                view(gated[:, RW * t], [[1, G], [0, GE]]), ALU.mult)
                    step(ins)
                step(dve.memset(comb[LAST:128, NT - 1, 0:ne], 0.0))
                dve.tensor_scalar(mask_bf[:, :, 0:ne], comb[:, :, 0:ne], 0.0, None, ALU.is_gt).then_inc(s_mask[l], 1)
                step(dve.tensor_copy(wparts[:, :, 0:ne, 0], comb[:, :, 0:ne]))
                step(dve.tensor_tensor(crest[:, :, 0:ne], comb[:, :, 0:ne], wparts[:, :, 0:ne, 0], ALU.subtract))
                step(dve.tensor_copy(wparts[:, :, 0:ne, 1], crest[:, :, 0:ne]))
                step(dve.tensor_tensor(crest[:, :, 0:ne], crest[:, :, 0:ne], wparts[:, :, 0:ne, 1], ALU.subtract))
                step(dve.tensor_copy(wparts[:, :, 0:ne, 2], crest[:, :, 0:ne]))

            def list_jobs(l):
                ne = E[l]
                dve.wait_ge(s_rank[l], 1)
                step(dve.tensor_tensor(pos[:, :, 0:ne], ps[:, 6, 0:NT * ne].rearrange("p (t e) -> p t e", t=NT), mask_bf[:, :, 0:ne], ALU.mult))
                step(dve.tensor_tensor(over[:, 0:ne, :], view(ps[:, 6, NT * ne:NT * ne + 1], [[1, ne], [0, NCHUNK]]),
                                       view(cst("tile"), [[0, ne], [1, NCHUNK]]), ALU.is_gt))
                step(dve.tensor_reduce(nchunk[:, 0:ne], over[:, 0:ne, :], AX_X, ALU.add))
                step(dve.tensor_tensor_scan(ends[:, 0:ne], cst("ones")[:, 0:ne], nchunk[:, 0:ne], 0.0, ALU.mult, ALU.add))
                step(dve.tensor_scalar(before[:, 0, 0:ne], ends[:, 0:ne], cst("row"), None, ALU.is_le))
                step(dve.tensor_tensor(before[:, 1, 0:ne], before[:, 0, 0:ne], nchunk[:, 0:ne], ALU.mult))
                step(dve.tensor_reduce(job_t[:], before[:, :, 0:ne], AX_X, ALU.add))
                dve.tensor_scalar(job_e[:, 0:1], job_t[:, 0:1], float(ne - 1), None, ALU.min)
                step(dve.tensor_tensor(job_t[:, 1:2], cst("row"), job_t[:, 1:2], ALU.subtract))
                step(dve.scalar_tensor_tensor(out=job_t[:, 1:2], in0=before[:, 0, ne - 1:ne], scalar=float(NCHUNK), in1=job_t[:, 1:2],
                                              op0=ALU.mult, op1=ALU.add))
                dve.tensor_scalar(job_e[:, 1:2], job_t[:, 1:2], float(NCHUNK), 128.0, ALU.min, ALU.mult).then_inc(s_jcol[l], 1)
                dve.wait_ge(s_jrow[l], 1)
                step(dve.tensor_copy(njobs[:], ends[0:1, ne - 1:ne]))
                dve.tensor_copy(jobs[:], ps[0:1, 7, 256:256 + 2 * JOBS]).then_inc(s_jobs[l], 1)

            def experts(l):
                dve.memset(yw[:, 1].bitcast(F32), 0.0).then_inc(s_yw[l], 1)
                dve.wait_ge(s_pad, 17)
                route(l)
                list_jobs(l)
                def select(j, s):
                    e = job_expert(dve, l, j)
                    c = dve.value_load(jobs[0:1, bass.ds(j + JOBS, 1)], min_val=0, max_val=128 * NCHUNK)
                    dve.tensor_copy(info[:, s, :, 2:5], wparts[:, :, bass.ds(e, 1), :].rearrange("p t e w -> p t (e w)"))
                    mine = pos[:, :, bass.ds(e, 1)].rearrange("p t e -> p (t e)")
                    slots = table[:, bass.ds(c + WHERE["count"][0], 128)]
                    dve.tensor_tensor(sel[:, s], view(mine, [[32, NT], [0, 128]]), view(slots, [[0, NT], [1, 128]]),
                                      ALU.is_equal).then_inc(s_sel[l], 1)

                def slots_of(j, s, extra=0):
                    dve.wait_ge(s_inf[l], j + 1)
                    dve.tensor_reduce(nxt[:, s, 1:2], ps[:, 7, 8 * s + 2:8 * s + 5], AX_X, ALU.add)
                    step(dve.tensor_reduce(nxt[:, s, 0:1], ps[:, 7, 8 * s:8 * s + 2], AX_X, ALU.add), extra)
                    dve.tensor_scalar(idx[:, s:s + 1], nxt[:, s, 0:1], -1.0, 0.0, ALU.add, ALU.max).then_inc(s_idx[l], 1)

                dve.wait_ge(s_jobs[l], 1)
                select(0, 0)
                select(1, 1)
                slots_of(0, 0)
                slots_of(1, 1)
                select(2, 0)
                pairs = job_count(dve, l)
                next_stretch()
                per = 2 * 3
                with dve.Fori(0, pairs) as i:
                    for s in range(2):
                        j = i * 2 + s
                        step(dve.tensor_copy(cur[:, s, :], nxt[:, s, :]), i * per)
                        dve.tensor_scalar(selT[:, s, :], cst("count")[:, 0:NP], cur[:, s, 0:1], None, ALU.is_equal)
                        slots_of(j + 2, s, i * per)
                        select(j + 3, 1 - s)
                        dve.wait_ge(s_yp[l], j + 1)
                        y, w = ps[:, 5, D * s:D * s + D], cur[:, s, 1:2]
                        step(dve.tensor_scalar(yw[:, s, 0], y, w, None, ALU.mult), i * per)
                        dve.scalar_tensor_tensor(out=yw[:, s, 1], in0=y, scalar=w, in1=yw[:, s, 0].bitcast(F32),
                                                 op0=ALU.mult, op1=ALU.subtract).then_inc(s_yw[l], 1)
                assert steps == per
                next_stretch()
                dve.wait_ge(s_done[l], 1)
                for b in range(3):
                    tiles = range(2 * b, min(2 * b + 2, NT))
                    dve.tensor_tensor(h[:, tiles[0]:tiles[-1] + 1, :], ps[:, b, 0:len(tiles) * D].rearrange("p (t n) -> p t n", n=D),
                                      h[:, tiles[0]:tiles[-1] + 1, :], ALU.add).then_inc(s_hmoe[l], 1)
                    if l == 0:
                        dve.wait_ge(s_hmoe[l], b + 1)
                        for t in tiles:
                            ins = dve.bn_stats(stats[:, t, :], h[:, t, :])
                if l == 0:
                    step(ins)

            embed()
            norm(0)
            attention(0)
            norm(1)
            experts(0)
            norm(2)
            attention(1)
            norm(3)
            experts(1)

        @block.tensor
        def _(pe):
            def mm(o, a, b, start=True, stop=True):
                return pe.matmul(o, a, b, start=start, stop=stop, skip_group_check=True)

            def norm(k):
                l = k // 2
                nl = G + E[1] if l else E[0]

                def logits(t):
                    pe.wait_ge(s_xt, NT * k + t + 1)
                    for ci in range(CC):
                        ins = mm(ps[:, 5, nl * t:nl * t + nl], xT[:, ci, t * 128:(t + 1) * 128], wr[l][:, ci, :], ci == 0, ci == CC - 1)
                    return ins

                if k % 2:
                    pe.wait_ge(s_rtw[l], 16 * (9 if l else 1))
                for t in range(NT):
                    n = NT * k + t
                    if t and k % 2:
                        logits(t - 1)
                    pe.wait_ge(s_xn, n + 1)
                    if t >= 2:
                        pe.wait_ge(s_xt, n - 1)
                    for c in range(CC):
                        ins = pe.transpose(ps[0:CP, 6 + t % 2, 128 * c:128 * c + 128], xn[:, t, CP * c:CP * c + CP], ident)
                    ins.then_inc(s_xtp, 1)
                if k % 2:
                    logits(NT - 1).then_inc(s_lp[l], 1)
                pe.wait_ge(s_xt, NT * (k + 1))

            def attention(l):
                nu, per = U[l], NPAIR // U[l]
                hk = 6 if l else 3
                pe.wait_ge(s_attw[l], 16 * (14 if l else 6))

                def project(w, bank, co, n):
                    for ci in range(CC):
                        ins = mm(ps[0:CP, bank, 0:HALF], w[l][:, ci, CP * co:CP * co + CP], xT[:, ci, n * HALF:(n + 1) * HALF],
                                 ci == 0, ci == CC - 1)
                    return ins

                for t in range(NT):
                    if t >= 2:
                        pe.wait_ge(s_vtr[l], t - 1)
                    for ci in range(CC):
                        ins = mm(ps[:, 4 + t % 2, 0:D], xT[:, ci, t * 128:(t + 1) * 128], wv[l][:, ci, :], ci == 0, ci == CC - 1)
                    ins.then_inc(s_vtp[l], 1)
                for m in range(4):
                    project(wq, m, m // 2, m % 2).then_inc(s_qp[l], 1)
                if l:
                    pe.wait_ge(s_q[l], 4)
                    pe.wait_ge(s_vtr[l], NT)
                    pe.wait_ge(s_pad, 5)
                    for r in range(CC * NT):
                        t, c = r // CC, r % CC
                        if r >= 2:
                            pe.wait_ge(s_rs, r - 1)
                        mm(ps[:, 4 + r % 2, 0:6 * W_REL], qT[:, c, t * 128:(t + 1) * 128],
                           emb_rev[:].rearrange("p h w -> p (h w)")).then_inc(s_rp, 1)
                for m in range(4):
                    pe.wait_ge(s_q[l], m + 1)
                    project(wk, m, m // 2, m % 2).then_inc(s_kp[l], 1)
                pe.wait_ge(s_kv[l], 2 * hk)
                pe.wait_ge(s_ka[l], 2 * hk)

                def scores(u):
                    if u >= 2:
                        pe.wait_ge(s_sr[l], u - 1)
                    for g in range(per):
                        for i in range(2):
                            b = 2 * (u * per + g) + i
                            for c in range(CC):
                                q = qT[:, c, L * b:L * b + L]
                                k = kblk[:, c, b * hk * L:(b + 1) * hk * L]
                                if l:
                                    ins = mm(ps[64 * i:64 * i + L, u % 2, hk * L * c:hk * L * (c + 1)], q, k)
                                else:
                                    ins = mm(ps[64 * i:64 * i + L, u % 2, TR * g:TR * g + TR], q, k, c == 0, c == CC - 1)
                    ins.then_inc(s_sp[l], 1)

                def turn_probs(u):
                    pe.wait_ge(s_ex[l], u + 1)
                    if u >= 2:
                        pe.wait_ge(s_pt[l], u - 1)
                    for g in range(4):
                        ins = pe.transpose(ps[0:TR, 2 + u % 2, 128 * g:128 * g + 128], prob[:, u % 2, TR * g:TR * g + TR], ident)
                    ins.then_inc(s_ptp[l], 1)

                def context(u):
                    pe.wait_ge(s_pt[l], u + 1)
                    if u == 0:
                        pe.wait_ge(s_vv[l], 1)
                    if u == nu // 2:
                        pe.wait_ge(s_vp[l], 1)
                    if l and u >= 2:
                        pe.wait_ge(s_cn[l], u - 1)
                    if not l and u >= 1:
                        pe.wait_ge(s_cn[l], u)
                    for g in range(4):
                        for i in range(2):
                            p = probT[:, u % 2, 128 * g + 64 * i:128 * g + 64 * i + L]
                            if l:
                                ins = mm(ps[64 * i:64 * i + L, 4 + u % 2, 48 * g:48 * g + 48], p, vblk[:, 2 * u + i, 48 * g:48 * g + 48])
                            else:
                                ins = mm(ps[64 * i:64 * i + L, 4 + g // 2, D * (g % 2):D * (g % 2) + D], p, vblk[:, 2 * (4 * u + g) + i, :])
                    ins.then_inc(s_cp[l], 1)

                def turn_context(u):
                    pe.wait_ge(s_cn[l], u + 1)
                    for p in range(u * per, (u + 1) * per):
                        if p >= 2:
                            pe.wait_ge(s_ct[l], 2 * (p - 1))
                        for c in range(CC):
                            ins = pe.transpose(ps[0:CP, 6 + p % 2, 128 * c:128 * c + 128], ctxr[:, p, CP * c:CP * c + CP], ident)
                        ins.then_inc(s_ctp[l], 1)

                for u in range(nu + 3):
                    if u < nu:
                        scores(u)
                    if 1 <= u <= nu:
                        turn_probs(u - 1)
                    if 2 <= u <= nu + 1:
                        context(u - 2)
                    if u >= 3:
                        turn_context(u - 3)
                if l == 0:
                    for r in range(2):
                        pe.wait_ge(s_gs, 2 * r + 2)
                        same = cst("same", CP).rearrange("p (c d n) -> p c d n", c=CC, d=CC)
                        for d in range(CC):
                            for c in range(CC):
                                ins = mm(ps[0:CP, 7, NI * d:NI * d + NI], same[:, c, d, :], gsum[:, c, :], c == 0, c == CC - 1)
                        ins.then_inc(s_gp, 1)
                    pe.wait_ge(s_gn, CC)
                else:
                    pe.wait_ge(s_ct[l], CC * NPAIR)
                for t in range(NT):
                    if t >= 2:
                        pe.wait_ge(s_or[l], t - 1)
                    for ci in range(CC):
                        ins = mm(ps[:, t % 2, 0:D], ctxT[:, ci, t * 128:(t + 1) * 128], wo[l][:, ci, :], ci == 0, ci == CC - 1)
                    ins.then_inc(s_op[l], 1)

            def experts(l):
                ne = E[l]
                pe.wait_ge(s_pad, 17)
                pe.wait_ge(s_mask[l], 1)
                for t in range(NT):
                    for r in range(t + 1):
                        mm(ps[:, 6, ne * t:ne * t + ne], upto_bf[:] if r == t else ones_bf[:], mask_bf[:, r, 0:ne], r == 0, r == t)
                for r in range(NT):
                    ins = mm(ps[:, 6, NT * ne:(NT + 1) * ne], ones_bf[:], mask_bf[:, r, 0:ne], r == 0, r == NT - 1)
                ins.then_inc(s_rank[l], 1)
                if l:
                    for t in range(NT):
                        ins = pe.transpose(ps[0:32, 5 if t < 4 else 4, 128 * (t % 4):128 * (t % 4) + 128], comb[:, t, :], ident)
                    ins.then_inc(s_cbp[l], 1)
                    pe.wait_ge(s_cbt[l], 2)
                for t in range(NT):
                    o = ps[:, t // 2, D * (t % 2):D * (t % 2) + D]
                    if l:
                        ins = mm(o, combT[:, 128 * t:128 * t + 128], b2all[:], t % 2 == 0, False)
                    else:
                        ins = mm(o, zero_bf[:, 0:128], zero_bf[:, 0:D], t % 2 == 0, False)
                pe.wait_ge(s_jcol[l], 1)
                for c in range(2):
                    ins = mm(ps[0:1, 7, 256 + JOBS * c:256 + JOBS * (c + 1)], job_e[:, c:c + 1], ident_bf[:])
                ins.then_inc(s_jrow[l], 1)

                def slots(j, s):
                    pe.wait_ge(s_sel[l], j + 1)
                    for t in range(NT):
                        ins = mm(ps[:, 7, 8 * s:8 * s + 5], sel[:, s, t, :], info[:, s, t, :], t == 0, t == NT - 1)
                    ins.then_inc(s_inf[l], 1)

                def turn(i, s):
                    pe.wait_ge(s_gat[l][s], i * 16 + 16)
                    for c in range(CC):
                        o = 256 * s + 128 * c
                        ins = pe.transpose(ps[0:CP, 6, o:o + 128], xg[:, s, CP * c:CP * c + CP], ident)
                    ins.then_inc(s_xgp[l], 1)

                def first(i, j, s):
                    pe.wait_ge(s_xg[l], j + 1)
                    pe.wait_ge(s_w1[l][s], i * 16 + 16)
                    for m in range(MC):
                        for ci in range(CC):
                            ins = mm(ps[:, 3 + m // 3, 128 * (m % 3):128 * (m % 3) + 128], w1[:, s, ci, 128 * m:128 * m + 128],
                                     xgT[:, s, ci, :], ci == 0, ci == CC - 1)
                        if m % 3 == 2:
                            ins.then_inc(s_hp[l], 1)

                def second(i, j, s):
                    pe.wait_ge(s_w2[l][s], i * 16 + 16)
                    for m in range(MC):
                        if m % 3 == 0:
                            pe.wait_ge(s_hd[l], j * 2 + 1 + m // 3)
                        ins = mm(ps[:, 5, D * s:D * s + D], hid[:, m, :], w2[:, s, m, :], m == 0, m == MC - 1)
                    ins.then_inc(s_yp[l], 1)

                def scatter(j, s):
                    pe.wait_ge(s_yw[l], j + 2)
                    for t in range(NT):
                        for part in range(2):
                            ins = mm(ps[:, t // 2, D * (t % 2):D * (t % 2) + D], selT[:, s, 128 * t:128 * t + 128],
                                     yw[:, s, part], False, False)
                    return ins

                pe.wait_ge(s_jobs[l], 1)
                slots(0, 0)
                pe.wait_ge(s_idx[l], 1)
                slots(1, 1)
                pairs = job_count(pe, l)
                turn(0, 0)
                with pe.Fori(0, pairs) as i:
                    for s in range(2):
                        j = i * 2 + s
                        first(i, j, s)
                        scatter(j - 1, 1 - s)
                        slots(j + 2, s)
                        turn(i + s, 1 - s)
                        second(i, j, s)
                scatter(pairs * 2 - 1, 1).then_inc(s_done[l], 1)
                pe.wait_ge(s_gat[l][1], pairs * 16 + 16)
                for q in (s_w1[l], s_w2[l]):
                    for s in range(2):
                        pe.wait_ge(q[s], pairs * 16 + 16)

            pe.wait_ge(s_pad, 2)
            pe.wait_ge(s_step[0], 1)
            for k in range(KF):
                pe.wait_ge(s_patch[k], 32)
                for t in range(NT):
                    ins = mm(ps[:, t, 0:D], patches[:, k, t * 128:(t + 1) * 128], tok_w[:, k, :], k == 0, k == KF - 1)
                    if k == KF - 1:
                        ins.then_inc(s_emb, 1)
            pe.wait_ge(s_table, 16)
            norm(0)
            attention(0)
            norm(1)
            experts(0)
            norm(2)
            attention(1)
            norm(3)
            experts(1)


def kernel(**inputs):
    import concourse.bacc as bacc
    from concourse.bass_utils import run_bass_kernel_spmd

    a = {k: np.ascontiguousarray(v) for k, v in inputs.items()}
    n = IMG // PATCH
    x = a.pop("x").reshape(NI, NCH, n, PATCH, n, PATCH)
    a["patchesT"] = x.transpose(1, 3, 5, 0, 2, 4).reshape(FLAT, TOK)
    a["tok_WT"] = a.pop("L0_tok_W").T
    a["pos"] = np.tile(a.pop("L0_tok_pos_emb"), (NI, 1))
    for w in ("Wq", "Wk", "Wv", "Wo"):
        a[w + "T0"] = a.pop("L0_attn_" + w).T
    distance = np.clip(L - 1 - np.arange(W_REL), -MAX_REL, MAX_REL) + MAX_REL
    a["emb_rev"] = a.pop("L1_attn_rel_emb")[distance].T
    a["b1T"] = a.pop("L1_ffn_b1").reshape(E[1], MC, 128).transpose(2, 0, 1)
    for name in ("L0_attn_gn_weight", "L0_attn_gn_bias", "L1_attn_bq", "L1_attn_bk", "L1_attn_bv"):
        a[name] = a[name].reshape(CC, CP).T
    a["table"] = TABLE
    nc = bacc.Bacc("TRN2", target_bir_lowering=False, num_devices=1)
    arrays, aps = {}, {}
    for name, v in a.items():
        arrays["in_" + name] = v = np.ascontiguousarray(v)
        aps[name] = nc.dram_tensor("in_" + name, v.shape, mybir.dt.from_np(v.dtype), kind="ExternalInput").ap()
    out = nc.dram_tensor("tower_out", (TOK, D), F32, kind="ExternalOutput").ap()
    vit_tower(nc, aps, out)
    r = run_bass_kernel_spmd(nc, [arrays], core_ids=[0])
    return r.results[0]["tower_out"].reshape(NI, L, D)
```

```python
from contextlib import ExitStack

import numpy as np

import concourse.bass as bass
from concourse import mybir

F32 = mybir.dt.float32
F32R = mybir.dt.float32r
BF16 = mybir.dt.bfloat16
I32 = mybir.dt.int32
U32 = mybir.dt.uint32
ALU = mybir.AluOpType
ACT = mybir.ActivationFunctionType
AX_X = mybir.AxisListType.X

NI, NCH, IMG, PATCH = 16, 3, 96, 16
L = (IMG // PATCH) ** 2
FLAT = NCH * PATCH * PATCH
KF = FLAT // 128
TOK = NI * L
NT = -(-TOK // 128)
NP = NT * 128
LAST = TOK - (NT - 1) * 128
D = 192
CC, CP = 2, 96
M = 768
MC = M // 128
H = (3, 12)
E = (8, 32)
G, GE = 4, 8
NPAIR = NI // 2
TR = 3 * L
UW = 4 * TR
U = (2, 8)
HALF = TOK // 2
W_REL = 2 * L - 1
MAX_REL = 32
WEIGHT_STEPS = (6, 9)
WARM_NORM, WARM_SOFTMAX, WARM_GROUPS, WARM_RANKS = (16, 10, 10, 10), 12, (4, 12, 12), (5, 20)
WARM_LIST = (0, 10)
OUT_BANK = ((0, 1, 0, 1, 0), (7, 7, 7, 7, 6))
KEY_BANK = (0, 6, 1, 7)
NCHUNK = NT
MOST_JOBS = 50
JOBS = 64
LN_EPS = 1e-5
GN_EPS = 1e-5
LOWEST = -3.0e38


def constants():
    p = np.arange(128)
    parts = {
        "ident": np.eye(128),
        "upto": (p[:, None] <= p[None, :]),
        "ones": np.ones((128, 128)),
        "count": np.broadcast_to(np.arange(1, NP + 129), (128, NP + 128)),
        "row": p[:, None],
        "row1": p[:, None] + 1,
        "eight": np.broadcast_to(np.arange(8), (128, 8)),
        "tile": np.broadcast_to(128 * np.arange(NT), (128, NT)),
    }
    ch = np.arange(CC)[None, :, None] * CP + p[:, None, None]
    parts["khead0"] = (ch // 64 == np.arange(3)).reshape(128, -1)
    parts["khead1"] = (p[:, None, None] // 16 == np.arange(6)) & (np.arange(CC)[None, :, None] >= 0)
    col = np.arange(D)
    parts["vhead0"] = p[:, None] // L == col // 64
    parts["vhead1"] = p[:, None] // L == (col // 16) % 3
    parts["triple"] = p[:, None] // L == np.arange(3)
    to = np.arange(CC)[:, None] * CP + np.arange(CP)[None, :]
    parts["same"] = (ch[:, :, :, None] // 64 == to[None, None] // 64).reshape(128, -1)
    where, cols, at = {}, [], 0
    for name, a in parts.items():
        a = np.asarray(a, np.float32).reshape(128, -1)
        where[name] = (at, a.shape[1])
        cols.append(a)
        at += a.shape[1]
    return where, np.concatenate(cols, 1)


WHERE, TABLE = constants()


def vit_tower(nc, A, out):
    with ExitStack() as ctx:
        def sb(name, shape, dt=F32):
            return ctx.enter_context(nc.sbuf_tensor(name, shape, dt))

        def sem(name):
            return ctx.enter_context(nc.semaphore(name))

        rows_dram = [nc.dram_tensor(f"rows{l}", (NP, D), F32).ap() for l in range(2)]
        rel_dram = nc.dram_tensor("reltab", (NP, H[1] * W_REL), F32)
        value_dram = [nc.dram_tensor(f"values{l}", (NP, D), F32) for l in range(2)]
        decay_dram = nc.dram_tensor("decaytab", (L, H[0] * W_REL), F32)

        table = sb("table", [128, TABLE.shape[1]])
        early = sb("early", [128, KF * (NP + D)])
        patches = early[:, 0:KF * NP].rearrange("p (k n) -> p k n", k=KF)
        tok_w = early[:, KF * NP:].rearrange("p (k n) -> p k n", k=KF)
        qrel = early[:, 0:NT * 12 * W_REL].rearrange("p (t w) -> p t w", t=NT)
        h = sb("h", [128, NT, D])
        stats = sb("stats", [128, NT, 6])
        mv = sb("mv", [128, NT, 2])
        vare = sb("vare", [128, NT])
        std = sb("std", [128, NT])
        rstd = sb("rstd", [128, NT])
        xn = sb("xn", [128, NT, D])
        posb = xn[:]
        xT = sb("xT", [CP, CC, NP])
        wq, wk, wv, wo = [[sb(f"w{n}{l}", [CP, CC, D]) for l in range(2)] for n in "qkvo"]
        bq = sb("bq", [CP, CC])
        bk = sb("bk", [CP, CC])
        bv = sb("bv", [128, D])
        bo = sb("bo", [128, D])
        gnw = sb("gnw", [CP, CC])
        gnb = sb("gnb", [CP, CC])
        zero_col = sb("zero_col", [128, 1])
        spare = sb("spare", [128, 16])
        qT = sb("qT", [CP, CC, NP])
        kblk = sb("kblk", [CP, CC, NI * 6 * L])
        vrow = sb("vrow", [128, NT, D])
        vload = sb("vload", [TR, NI, D])
        vblk = sb("vblk", [TR, NI * (D + 12)])
        score = sb("score", [128, 2, UW])
        prob = sb("prob", [128, 2, UW])
        top = sb("top", [128, 2, 12])
        pinv = sb("pinv", [128, 8, 12])
        probT = sb("probT", [TR, 2, 512])
        ctxr = sb("ctxr", [128, NPAIR, D])
        tok_b = ctxr[:, 0, :]
        ctxT = sb("ctxT", [CP, CC, NP])
        gam = sb("gam", [L, 3])
        powers = sb("powers", [L, 3, W_REL])
        decay = sb("decay", [128, 3, L])
        gsum = sb("gsum", [CP, CC, NI])
        gvar = sb("gvar", [CP, CC, NI])
        gstd = sb("gstd", [CP, CC, NI])
        grs = sb("grs", [CP, CC, NI])
        gscale = sb("gscale", [CP, CC, NI])
        emb_rev = sb("emb_rev", [CP, 6, W_REL])
        rel = sb("rel", [128, NPAIR, UW])
        ones_bf = sb("ones_bf", [128, 128], BF16)
        upto_bf = sb("upto_bf", [128, 128], BF16)
        ident_bf = sb("ident_bf", [128, JOBS], BF16)
        zero_bf = sb("zero_bf", [128, 512], BF16)
        wr = [sb("wr0", [CP, CC, E[0]]), sb("wr1", [CP, CC, G + E[1]])]
        rbias = sb("rbias", [128, G + E[1]])
        RW = 5
        logit = sb("logit", [128, NT * RW, 8])
        pick = [sb(f"pick{n}", [128, NT * RW, 8]) for n in range(2)]
        rank8 = sb("rank8", [128, NT * RW, 8])
        best = [sb(f"best{n}", [128, NT * RW]) for n in range(2)]
        first = sb("first", [128, NT * RW])
        gate = [sb(f"gate{n}", [128, NT * RW]) for n in range(4)]
        gated = sb("gated", [128, NT * RW, 8])
        comb = sb("comb", [128, NT, 32])
        crest = sb("crest", [128, NT, 32])
        mask_bf = sb("mask_bf", [128, NT, 32], BF16)
        wparts = sb("wparts", [128, NT, 32, 3], BF16)
        pos = sb("pos", [128, NT, 32])
        over = sb("over", [128, 32, NCHUNK])
        nchunk = sb("nchunk", [128, 32])
        ends = sb("ends", [128, 32])
        before = sb("before", [128, 2, 32])
        job_e = sb("job_e", [128, 2], BF16)
        job_t = sb("job_t", [128, 2])
        jobs = sb("jobs", [1, 2 * JOBS], I32)
        njobs = sb("njobs", [1, 1], I32)
        combT = sb("combT", [32, NP])
        b1all = sb("b1all", [128, 32, MC])
        b2all = sb("b2all", [32, D])
        w1 = sb("w1", [CP, 2, CC, M])
        w2 = sb("w2", [128, 2, MC, D])
        sel = sb("sel", [128, 2, NT, 128], BF16)
        info = sb("info", [128, 2, NT, 5], BF16)
        nxt = sb("nxt", [128, 2, 2])
        cur = sb("cur", [128, 2, 2])
        idx = sb("idx", [128, 2], U32)
        xg = sb("xg", [128, 2, D])
        xgT = sb("xgT", [CP, 2, CC, 128])
        hid = sb("hid", [128, MC, 128])
        keys_half = hid[0:CP].rearrange("p m n -> p (m n)")[:, 0:CC * HALF].rearrange("p (c n) -> p c n", c=CC)
        yw = sb("yw", [128, 2, 2, D], F32R)
        selT = sb("selT", [128, 2, NP], F32R)

        ps = ctx.enter_context(nc.psum_tensor("ps", [128, 8, 512], F32))

        def cst(name, rows=128):
            at, n = WHERE[name]
            return table[0:rows, at:at + n]

        ident = cst("ident")

        def view(ap, dims, offset=0):
            return bass.AP(ap.tensor, ap.offset + offset, [list(ap.ap[0])] + [list(d) for d in dims])

        s_table = sem("table_loaded")
        s_patch = [sem(f"patches_loaded{k}") for k in range(KF)]
        s_posld = sem("pos_loaded")
        s_attw = [sem("attn0_weights_loaded"), sem("attn1_weights_loaded")]
        s_rtw = [sem("router0_loaded"), sem("router1_loaded")]
        s_pad = sem("pads_zeroed")
        s_posb = sem("pos_plus_bias")
        s_emb = sem("embedding_in_psum")
        s_hemb = sem("embedding_read")
        s_step = [sem(f"vector_step{n}") for n in range(5)]
        s_lnvar = sem("ln_variance")
        s_lnstd = sem("ln_deviation")
        s_xn = sem("normed_rows")
        s_xtp = sem("normed_in_psum")
        s_xt = sem("normed_columns")
        s_gam = sem("gammas_loaded")
        s_pow = sem("powers_ready")
        s_powst = sem("powers_stored")
        s_decay = sem("decay_loaded")
        s_qp, s_q, s_kp, s_kv, s_ka, s_vp, s_vv, s_sp, s_sr, s_sh, s_ex, s_ptp, s_pt, s_cp, s_cn, s_ctp, s_ct, s_op, s_or = [
            [sem(f"{n}{l}") for l in range(2)] for n in (
                "queries_in_psum", "queries_ready", "keys_in_psum", "keys_by_vector", "keys_by_scalar",
                "values_masked_pool", "values_masked", "scores_in_psum", "scores_read", "scores_shifted",
                "exp_ready", "probsT_in_psum", "probsT_ready", "context_in_psum",
                "context_ready", "contextT_in_psum", "contextT_ready", "projected", "projected_read")]
        s_vtp, s_vtr = [[sem(f"{n}{l}") for l in range(2)] for n in ("value_rows_in_psum", "value_rows_ready")]
        s_vst, s_vld = [[sem(f"{n}{l}") for l in range(2)] for n in ("values_stored", "values_loaded")]
        s_gs = sem("group_sums")
        s_gp = sem("group_sums_in_psum")
        s_gc = sem("centred")
        s_gq = sem("squared")
        s_gv = sem("group_variance")
        s_gd = sem("group_deviation")
        s_gn = sem("group_normed")
        s_rp = sem("rel_in_psum")
        s_rs = sem("rel_rows_ready")
        s_rst = [sem(f"rel_rows_stored{t}") for t in range(NT)]
        s_rel = [sem(f"rel_loaded{p}") for p in range(NPAIR // 2)]
        s_kg = sem("keys_by_pool")
        s_hbo = sem("bias_added")
        (s_rows, s_lp, s_rx, s_re, s_mask, s_rank, s_jcol, s_jrow, s_jobs, s_hp, s_hd,
         s_sel, s_inf, s_idx, s_xgp, s_xg, s_yp, s_yw, s_done) = [
            [sem(f"{n}{l}") for l in range(2)] for n in (
                "rows_stored", "logits_in_psum", "router_shifted", "router_exp", "mask_ready",
                "ranks_in_psum", "job_columns", "job_rows_in_psum", "jobs_ready",
                "hidden_in_psum", "hidden_ready", "selection_ready",
                "slots_in_psum", "slots_ready", "gatheredT_in_psum", "gatheredT_ready", "outputs_in_psum",
                "outputs_ready", "sums_complete")]
        s_w1, s_w2, s_gat = [[[sem(f"{n}{l}_{s}") for s in range(2)] for l in range(2)]
                             for n in ("w1_loaded", "w2_loaded", "rows_gathered")]
        s_gate, s_weight = [[sem(f"{n}{l}") for l in range(2)] for n in ("gates_ready", "weight_steps")]
        s_cbp = sem("combineT_in_psum")
        s_cbt = sem("combineT_ready")
        s_asked = [sem(f"gather_asked{l}") for l in range(2)]
        s_hmoe = [sem(f"experts_added{l}") for l in range(2)]
        s_stored = sem("output_stored")

        W1d = [A["L0_ffn_wi"], A["L1_ffn_W1"]]
        W2d = [A["L0_ffn_wo"], A["L1_ffn_W2"]]
        chunked = "(c p) n -> p c n"

        def key_slot(l, co, n, hh):
            hk = 6 if l else 3
            return view(kblk[:, co, 0:1], [[hk * L, NI // 2], [1, L]], (n * NI // 2 * hk + hh) * L)

        def job_count(eng, l):
            eng.wait_ge(s_jobs[l], 1)
            return eng.snap((eng.value_load(njobs[0:1, 0:1], min_val=1, max_val=MOST_JOBS) + 1) // 2)

        def job_expert(eng, l, j):
            return eng.value_load(jobs[0:1, bass.ds(j, 1)], min_val=0, max_val=E[l] - 1)

        def value_block(l, b):
            groups = 4 if l else 1
            return b * (D + 3 * groups), groups, D // groups

        def mask_values(eng, l, half, done):
            eng.wait_ge(s_vld[l], 16 * 3)
            at, groups, n = value_block(l, half * NI // 2)
            wide = n + 3
            into = [[groups * wide, NI // 2], [wide, groups]]
            eng.tensor_tensor(view(vblk[:, 0:1], into + [[1, n]], at),
                              view(vload[:], [[D, NI // 2], [n, groups], [1, n]], half * NI // 2 * D),
                              view(cst(f"vhead{l}", TR), [[0, NI // 2], [n, groups], [1, n]]), ALU.mult)
            eng.tensor_copy(view(vblk[:, 0:1], into + [[1, 3]], at + n),
                            view(cst("triple", TR), [[0, NI // 2], [0, groups], [1, 3]])).then_inc(done[l], 1)

        block = ctx.enter_context(nc.Block())

        @block.sync
        def _(sp):
            for k in range(KF):
                sp.dma_start(patches[:, k, 0:TOK], A["patchesT"][128 * k:128 * k + 128]).then_inc(s_patch[k], 16)
                sp.dma_start(tok_w[:, k, :], A["tok_WT"][128 * k:128 * k + 128]).then_inc(s_patch[k], 16)
            sp.dma_start(posb[:, 0:NT - 1, :], A["pos"][0:(NT - 1) * 128].rearrange("(t p) n -> p t n", p=128)).then_inc(s_posld, 16)
            sp.dma_start(posb[0:LAST, NT - 1, :], A["pos"][(NT - 1) * 128:TOK]).then_inc(s_posld, 16)
            sp.dma_start(tok_b, A["L0_tok_b"].partition_broadcast(128)).then_inc(s_posld, 16)
            sp.dma_start(table[:], A["table"]).then_inc(s_table, 16)
            sp.dma_start(gam[:], A["L0_attn_gammas"].partition_broadcast(L)).then_inc(s_gam, 16)
            for w, n in ((wq, "WqT0"), (wk, "WkT0"), (wv, "WvT0"), (wo, "WoT0")):
                sp.dma_start(w[0][:], A[n].rearrange(chunked, p=CP)).then_inc(s_attw[0], 16)
            for b, n in ((gnw, "L0_attn_gn_weight"), (gnb, "L0_attn_gn_bias")):
                sp.dma_start(b[:], A[n]).then_inc(s_attw[0], 16)
            sp.dma_start(wr[0][:], A["L0_ffn_router_w"].rearrange(chunked, p=CP)).then_inc(s_rtw[0], 16)
            sp.wait_ge(s_pow, 1)
            sp.dma_start(decay_dram.ap(), powers[:].rearrange("q h w -> q (h w)")).then_inc(s_powst, 16)
            sp.wait_ge(s_powst, 16)
            sp.wait_ge(s_pad, 1)
            sheared = bass.AP(decay_dram, L - 1, [[3 * W_REL - 1, L], [W_REL, 3], [1, L]])
            for i in range(2):
                sp.dma_start(decay[64 * i:64 * i + L], sheared).then_inc(s_decay, 16)
            for w, n in ((wq, "Wq"), (wk, "Wk"), (wv, "Wv"), (wo, "Wo")):
                sp.dma_start(w[1][:], A["L1_attn_" + n].rearrange(chunked, p=CP)).then_inc(s_attw[1], 16)
            for b, n in ((bq, "bq"), (bk, "bk")):
                sp.dma_start(b[:], A["L1_attn_" + n]).then_inc(s_attw[1], 16)
            sp.dma_start(bv[:], A["L1_attn_bv"].partition_broadcast(128)).then_inc(s_attw[1], 16)
            sp.dma_start(bo[:], A["L1_attn_bo"].partition_broadcast(128)).then_inc(s_attw[1], 16)
            sp.wait_ge(s_pad, 8)
            for k in range(6):
                sp.dma_start(emb_rev[16 * k:16 * k + 16, k, :], A["emb_rev"]).then_inc(s_attw[1], 16)
            sp.dma_start(wr[1][:, :, 0:G], A["L1_ffn_Wg"].rearrange(chunked, p=CP)).then_inc(s_rtw[1], 16)
            for g in range(G):
                sp.dma_start(wr[1][:, :, G + GE * g:G + GE * (g + 1)], A["L1_ffn_Wge"][g].rearrange(chunked, p=CP)).then_inc(s_rtw[1], 16)
            sp.dma_start(rbias[:, 0:G], A["L1_ffn_bg"].partition_broadcast(128)).then_inc(s_rtw[1], 16)
            sp.dma_start(rbias[:, G:], A["L1_ffn_bge"].rearrange("g e -> (g e)").partition_broadcast(128)).then_inc(s_rtw[1], 16)
            sp.dma_start(b1all[:], A["b1T"]).then_inc(s_rtw[1], 16)
            sp.dma_start(b2all[:], A["L1_ffn_b2"]).then_inc(s_rtw[1], 16)

            def values(l):
                sp.wait_ge(s_vtr[l], NT)
                sp.dma_start(value_dram[l].ap().rearrange("(t p) n -> p t n", p=128), vrow[:]).then_inc(s_vst[l], 16)
                sp.wait_ge(s_vst[l], 16)
                for r in range(3):
                    by_image = bass.AP(value_dram[l], 0, [[D, L], [L * D, NI], [1, D]])
                    sp.dma_start(vload[r * L:(r + 1) * L], by_image).then_inc(s_vld[l], 16)

            def experts(l):
                sp.wait_ge(s_xn, NT * (2 * l + 2))
                sp.dma_start(rows_dram[l].rearrange("(t p) n -> p t n", p=128), xn[:]).then_inc(s_rows[l], 16)

                def load_w1(s, e):
                    sp.dma_start(w1[:, s], W1d[l][bass.ds(e, 1)].rearrange("e (c p) m -> p (e c) m", p=CP)).then_inc(s_w1[l][s], 16)

                def load_w2(s, e):
                    sp.dma_start(w2[:, s], W2d[l][bass.ds(e, 1)].rearrange("e (c p) m -> p (e c) m", p=128)).then_inc(s_w2[l][s], 16)

                def load(j, s, e):
                    sp.wait_ge(s_hp[l], j * 2 - 2)
                    load_w1(s, e)
                    sp.wait_ge(s_yp[l], j - 1)
                    load_w2(s, e)

                sp.wait_ge(s_jobs[l], 1)
                e = job_expert(sp, l, 0)
                load_w1(0, e)
                sp.wait_ge(s_gat[l][0], 16)
                load_w2(0, e)
                e = job_expert(sp, l, 1)
                load_w1(1, e)
                load_w2(1, e)
                pairs = job_count(sp, l)
                with sp.Fori(0, pairs) as i:
                    for s in range(2):
                        load(i * 2 + s + 2, s, job_expert(sp, l, i * 2 + s + 2))

            values(0)
            experts(0)
            values(1)
            for b in range(NI):
                t = (L * b + L - 1) // 128
                sp.wait_ge(s_rst[t], 16)
                sheared = bass.AP(rel_dram, L * b * 12 * W_REL + L - 1, [[12 * W_REL - 1, L], [W_REL, 12], [1, L]])
                sp.dma_start(rel[64 * (b % 2):64 * (b % 2) + L, b // 2, :].rearrange("p (h k) -> p h k", k=L),
                             sheared).then_inc(s_rel[b // 4], 16)
            experts(1)
            sp.wait_ge(s_hmoe[1], 3)
            sp.dma_start(out[0:(NT - 1) * 128].rearrange("(t p) n -> p t n", p=128), h[:, 0:NT - 1, :]).then_inc(s_stored, 16)
            sp.dma_start(out[(NT - 1) * 128:TOK], h[0:LAST, NT - 1, :]).then_inc(s_stored, 16)
            sp.wait_ge(s_stored, 32)
            sp.wait_ge(s_powst, 16)
            for l in range(2):
                sp.wait_ge(s_rows[l], 16)

        @block.gpsimd
        def _(pool):
            for n, pad in enumerate((
                    decay[:],
                    patches[:, :, TOK:NP],
                    posb[64:128, NT - 1, :],
                    zero_col[:],
                    qT[:, :, TOK:NP],
                    ctxT[:, :, TOK:NP],
                    rel[:],
                    emb_rev[:],
                    selT[:].bitcast(F32),
                    zero_bf[:],
            )):
                if n:
                    pool.wait_ge(s_pad, n)
                pool.memset(pad, 0.0).then_inc(s_pad, 1)
            pool.wait_ge(s_pad, 10)
            pool.wait_ge(s_posld, 48)
            pool.tensor_tensor(posb, posb, view(tok_b, [[0, NT], [1, D]]), ALU.add).then_inc(s_posb, 1)
            pool.wait_ge(s_table, 16)
            pool.tensor_copy(ones_bf[:], cst("ones")).then_inc(s_pad, 1)
            pool.tensor_copy(upto_bf[:], cst("upto")).then_inc(s_pad, 1)
            pool.tensor_copy(ident_bf[:], ident[:, 0:JOBS]).then_inc(s_pad, 1)
            for s in range(2):
                pool.tensor_copy(info[:, s, :, 0], view(cst("row1"), [[0, NT]])).then_inc(s_pad, 1)
                pool.tensor_copy(info[:, s, :, 1], cst("tile")).then_inc(s_pad, 1)

            def weights(l):
                ne, rows, steps = E[l], NT * RW, 0

                def step(ins):
                    nonlocal steps
                    steps += 1
                    ins.then_inc(s_weight[l], 1)
                    pool.wait_ge(s_weight[l], steps)

                pool.wait_ge(s_gate[l], 1)
                if l == 0:
                    step(pool.tensor_tensor(comb[:, :, 0:ne], pick[0][:, 0:NT], view(gate[1][:], [[1, NT], [0, 8]]), ALU.mult))
                else:
                    step(pool.tensor_tensor(pick[1][:], pick[1][:], view(gate[1][:], [[1, rows], [0, 8]]), ALU.mult))
                    step(pool.tensor_tensor(pick[1][:], pick[1][:], pick[0][:], ALU.add))
                    step(pool.tensor_tensor(gated[:], pick[1][:], view(gate[3][:], [[1, rows], [0, 8]]), ALU.mult))
                    for t in range(NT):
                        ins = pool.tensor_tensor(comb[:, t, :].rearrange("p (g e) -> p g e", e=GE), gated[:, RW * t + 1:RW * t + RW, :],
                                                 view(gated[:, RW * t], [[1, G], [0, GE]]), ALU.mult)
                    step(ins)
                step(pool.tensor_copy(wparts[:, :, 0:ne, 0], comb[:, :, 0:ne]))
                step(pool.tensor_tensor(crest[:, :, 0:ne], comb[:, :, 0:ne], wparts[:, :, 0:ne, 0], ALU.subtract))
                step(pool.tensor_copy(wparts[:, :, 0:ne, 1], crest[:, :, 0:ne]))
                step(pool.tensor_tensor(crest[:, :, 0:ne], crest[:, :, 0:ne], wparts[:, :, 0:ne, 1], ALU.subtract))
                step(pool.tensor_copy(wparts[:, :, 0:ne, 2], crest[:, :, 0:ne]))
                assert steps == WEIGHT_STEPS[l]

            def gathers(l):
                pool.wait_ge(s_rows[l], 16)
                def gather(j, s):
                    pool.wait_ge(s_idx[l], j + 1)
                    pool.sem_inc(s_asked[l], 1)
                    pool.indirect_dma_start(xg[:, s, :], None, rows_dram[l],
                                            bass.IndirectOffsetOnAxis(idx[:, s:s + 1], 0)).then_inc(s_gat[l][s], 16)

                pairs = job_count(pool, l)
                for s in range(2):
                    gather(s, s)
                with pool.Fori(0, pairs) as i:
                    for s in range(2):
                        gather(i * 2 + s + 2, s)

            pool.wait_ge(s_table, 16)
            mask_values(pool, 0, 1, s_vp)
            weights(0)
            gathers(0)
            pool.wait_ge(s_attw[1], 16 * 14)
            pool.wait_ge(s_xn, NT * 3)
            pool.tensor_tensor(h[:], h[:], view(bo[:], [[0, NT], [1, D]]), ALU.add).then_inc(s_hbo, 1)
            for co in range(CC):
                pool.wait_ge(s_ka[1], co + 1)
                for hh in range(6):
                    mcol = WHERE["khead1"][0] + co * 6 + hh
                    pool.tensor_tensor(key_slot(1, co, 1, hh), keys_half[:, co].rearrange("p (b k) -> p b k", k=L),
                                       view(table[0:CP, mcol:mcol + 1], [[0, NI // 2], [0, L]]), ALU.mult).then_inc(s_kg, 1)
            mask_values(pool, 1, 1, s_vp)
            weights(1)
            gathers(1)

        @block.scalar
        def _(act):
            spares = iter(range(16))

            def table_for(func):
                n = next(spares)
                act.activation(spare[:, n:n + 1], zero_col[:], func)

            def norm(k):
                act.wait_ge(s_lnvar, k + 1)
                act.activation(std[:], vare[:], ACT.Sqrt).then_inc(s_lnstd, 1)
                for t in range(NT):
                    n = NT * k + t
                    act.wait_ge(s_xtp, n + 1)
                    act.activation(xT[:, :, t * 128:(t + 1) * 128],
                                   ps[0:CP, 6 + t % 2, 0:256].rearrange("p (c n) -> p c n", c=CC),
                                   ACT.Identity).then_inc(s_xt, 1)

            def attention(l):
                act.wait_ge(s_pad, 6)
                if l:
                    act.wait_ge(s_attw[1], 16 * 14)
                if l == 0:
                    for t in range(NT):
                        act.wait_ge(s_vtp[0], t + 1)
                        act.activation(vrow[:, t, :], ps[:, 4 + t % 2, 0:D], ACT.Identity).then_inc(s_vtr[0], 1)
                for m in range(4):
                    co, n = m // 2, m % 2
                    act.wait_ge(s_qp[l], m + 1)
                    act.activation(qT[:, co, n * HALF:(n + 1) * HALF], ps[0:CP, m, 0:HALF], ACT.Identity,
                                   bias=bq[:, co:co + 1] if l else zero_col[0:CP]).then_inc(s_q[l], 1)
                if l:
                    for co in range(CC):
                        act.wait_ge(s_kp[1], 3 + co)
                        act.activation(keys_half[:, co], ps[0:CP, KEY_BANK[2 * co + 1], 0:HALF], ACT.Identity,
                                       bias=bk[:, co:co + 1]).then_inc(s_ka[1], 1)
                    for t in range(NT):
                        for c in range(CC):
                            r = 2 * t + c
                            act.wait_ge(s_rp, r + 1)
                            act.activation(qrel[:, t, c * 6 * W_REL:(c + 1) * 6 * W_REL], ps[:, 4 + r % 2, 0:6 * W_REL],
                                           ACT.Identity).then_inc(s_rs, 1)
                        act.wait_ge(s_rs, 2 * t + 2)
                        act.dma_start(rel_dram.ap()[t * 128:(t + 1) * 128], qrel[:, t, :]).then_inc(s_rst[t], 16)
                else:
                    for n in range(2):
                        act.wait_ge(s_kp[0], 2 * n + 2)
                        for hh in range(3):
                            mcol = WHERE["khead0"][0] + 3 + hh
                            act.activation(key_slot(0, 1, n, hh), ps[0:CP, KEY_BANK[2 + n], 0:HALF].rearrange("p (b k) -> p b k", k=L),
                                           ACT.Identity, scale=table[0:CP, mcol:mcol + 1], bias=zero_col[0:CP]).then_inc(s_ka[0], 1)
                table_for(ACT.Exp)
                per = NPAIR // U[l]
                for u in range(U[l] + 3):
                    if u < U[l]:
                        act.wait_ge(s_sh[l], u + 1)
                        if u >= 2:
                            act.wait_ge(s_ptp[l], u - 1)
                        act.activation(prob[:, u % 2], score[:, u % 2], ACT.Exp, scale=0.25 if l else 1.0).then_inc(s_ex[l], 1)
                    if 1 <= u <= U[l]:
                        v = u - 1
                        act.wait_ge(s_ptp[l], v + 1)
                        if v >= 2:
                            act.wait_ge(s_cp[l], v - 1)
                        act.activation(probT[:, v % 2], ps[0:TR, 2 + v % 2, :], ACT.Identity).then_inc(s_pt[l], 1)
                    if u >= 3:
                        for p in range((u - 3) * per, (u - 2) * per):
                            act.wait_ge(s_ctp[l], p + 1)
                            act.activation(ctxT[:, :, 72 * p:72 * p + 72].rearrange("p c (i k) -> p c i k", k=L),
                                           view(ps[0:CP, 6 if l else 6 + p % 2, 0:1], [[128, CC], [64, 2], [1, L]]),
                                           ACT.Identity).then_inc(s_ct[l], 1)
                if l == 0:
                    table_for(ACT.Sqrt)
                    for c in range(CC):
                        act.wait_ge(s_gc, c + 1)
                        act.activation(kblk[:, c, 0:TOK], ctxT[:, c, 0:TOK], ACT.Square).then_inc(s_gq, 1)
                    act.wait_ge(s_gv, 1)
                    act.activation(gstd[:], gvar[:], ACT.Sqrt).then_inc(s_gd, 1)

            def experts(l):
                if l == 0:
                    act.wait_ge(s_rx[0], 1)
                    act.activation(pick[1][:, 0:NT, :], gated[:, 0:NT, :], ACT.Exp).then_inc(s_re[0], 1)
                else:
                    act.wait_ge(s_rx[1], 1)
                    act.activation(gate[1][:], gate[0][:], ACT.Exp).then_inc(s_re[1], 1)
                    act.wait_ge(s_cbp, 1)
                    act.activation(combT[:, 0:512], ps[0:32, 5, :], ACT.Identity).then_inc(s_cbt, 1)
                    act.activation(combT[:, 512:NP], ps[0:32, 4, 0:128], ACT.Identity).then_inc(s_cbt, 1)

                def columns(j, s):
                    act.wait_ge(s_xgp[l], j + 1)
                    act.activation(xgT[:, s], ps[0:CP, 6, 256 * s:256 * s + 256].rearrange("p (c n) -> p c n", c=CC),
                                   ACT.Identity).then_inc(s_xg[l], 1)

                def hidden(j, s):
                    if l:
                        e = job_expert(act, l, j)
                    for b in range(2):
                        act.wait_ge(s_hp[l], j * 2 + b + 1)
                        if l == 0:
                            ins = act.activation(hid[:, 3 * b:3 * b + 3, :].rearrange("p m n -> p (m n)"),
                                                 ps[:, 3 + b, 0:384], ACT.Relu)
                        else:
                            for m in range(3):
                                ins = act.activation(hid[:, 3 * b + m, :], ps[:, 3 + b, 128 * m:128 * m + 128], ACT.Gelu,
                                                     bias=b1all[:, bass.ds(e, 1), 3 * b + m])
                        ins.then_inc(s_hd[l], 1)

                table_for(ACT.Gelu if l else ACT.Relu)
                pairs = job_count(act, l)
                columns(0, 0)
                with act.Fori(0, pairs) as i:
                    for s in range(2):
                        hidden(i * 2 + s, s)
                        columns(i * 2 + s + 1, 1 - s)

            act.wait_ge(s_pad, 4)
            table_for(ACT.Sqrt)
            norm(0)
            attention(0)
            norm(1)
            table_for(ACT.Exp)
            experts(0)
            table_for(ACT.Sqrt)
            norm(2)
            attention(1)
            table_for(ACT.Sqrt)
            norm(3)
            table_for(ACT.Exp)
            experts(1)

        @block.vector
        def _(dve):
            stretch, steps = 0, 0

            def step(ins, before=0):
                nonlocal steps
                steps += 1
                ins.then_inc(s_step[stretch], 1)
                dve.wait_ge(s_step[stretch], before + steps)

            def next_stretch():
                nonlocal stretch, steps
                stretch, steps = stretch + 1, 0

            for bank in (0, 1):
                ins = dve.memset(ps[:, bank, :], 0.0)
            step(ins)

            step(dve.memset(powers[:], 0.0))
            dve.wait_ge(s_gam, 16)
            at = L - 1
            step(dve.memset(powers[:, :, at:at + 1], 1.0))
            step(dve.tensor_copy(powers[:, :, at + 1:at + 2], gam[:].rearrange("p (h o) -> p h o", o=1)))
            n = 1
            while n < L - 1:
                m = min(n, L - 1 - n)
                step(dve.tensor_tensor(powers[:, :, at + n + 1:at + n + m + 1], powers[:, :, at + 1:at + m + 1],
                                       view(powers[:, :, at + n:at + n + 1], [[W_REL, 3], [0, m]]), ALU.mult))
                n += m
            dve.tensor_scalar(powers[:], powers[:], 0.125, None, ALU.mult).then_inc(s_pow, 1)

            dve.wait_ge(s_posb, 1)

            def embed():
                for t in range(NT + 1):
                    if t < NT:
                        dve.wait_ge(s_emb, t + 1)
                        dve.tensor_tensor(h[:, t, :], ps[:, t, 0:D], posb[:, t, :], ALU.add).then_inc(s_hemb, 1)
                    if t:
                        dve.wait_ge(s_hemb, t)
                        ins = dve.bn_stats(stats[:, t - 1, :], h[:, t - 1, :])
                step(ins)

            def norm(k):
                for t in range(NT):
                    ins = dve.bn_aggr(mv[:, t, :], stats[:, t, :])
                step(ins)
                dve.tensor_scalar(vare[:], mv[:, :, 1], LN_EPS, None, ALU.add).then_inc(s_lnvar, 1)
                dve.wait_ge(s_lnstd, k + 1)
                step(dve.reciprocal(rstd[:], std[:]))
                for t in range(NT):
                    dve.tensor_scalar(xn[:, t, :], h[:, t, :], mv[:, t, 0:1], rstd[:, t:t + 1], ALU.subtract, ALU.mult).then_inc(s_xn, 1)

            def attention(l):
                nu, per = U[l], NPAIR // U[l]
                hk = 6 if l else 3
                if l:
                    dve.wait_ge(s_attw[1], 16 * 14)
                    for t in range(NT):
                        dve.wait_ge(s_vtp[1], t + 1)
                        dve.tensor_tensor(vrow[:, t, :], ps[:, 4 + t % 2, 0:D], bv[:], ALU.add).then_inc(s_vtr[1], 1)
                for r in range(2):
                    co, n = (r, 0) if l else (0, r)
                    dve.wait_ge(s_kp[l], 2 * n + co + 1)
                    for hh in range(hk):
                        mcol = WHERE[f"khead{l}"][0] + co * hk + hh
                        src = ps[0:CP, KEY_BANK[2 * co + n], 0:HALF].rearrange("p (b k) -> p b k", k=L)
                        dve.tensor_scalar(key_slot(l, co, n, hh), src, bk[:, co:co + 1] if l else 0.0,
                                          table[0:CP, mcol:mcol + 1], ALU.add, ALU.mult).then_inc(s_kv[l], 1)
                if l:
                    mask_values(dve, 1, 0, s_vv)
                else:
                    dve.wait_ge(s_decay, 32)
                hw = D // H[l]

                def residual(t):
                    dve.wait_ge(s_op[l], t + 1)
                    dve.tensor_tensor(h[:, t, :], ps[:, OUT_BANK[l][t], 0:D], h[:, t, :], ALU.add).then_inc(s_or[l], 1)

                def statistics(t):
                    dve.wait_ge(s_or[l], t + 1)
                    return dve.bn_stats(stats[:, t, :], h[:, t, :])

                for u in range(nu + 2):
                    if u < nu:
                        dve.wait_ge(s_sp[l], u + 1)
                        if u >= 2:
                            dve.wait_ge(s_ex[l], u - 1)
                        if l:
                            dve.wait_ge(s_rel[u // 2], 64)
                            ins = dve.tensor_tensor(score[:, u % 2], ps[:, u % 2, 0:UW], rel[:, u, :], ALU.add)
                        else:
                            ins = dve.tensor_tensor(score[:, u % 2].rearrange("p (g k) -> p g k", g=4),
                                                    ps[:, u % 2, 0:UW].rearrange("p (g k) -> p g k", g=4),
                                                    view(decay[:], [[0, 4], [1, TR]]), ALU.mult)
                        ins.then_inc(s_sr[l], 1)
                        dve.wait_ge(s_sr[l], u + 1)
                        s3 = score[:, u % 2].rearrange("p (h k) -> p h k", k=L)
                        step(dve.tensor_reduce(top[:, u % 2], s3, AX_X, ALU.max))
                        dve.tensor_tensor(s3, s3, view(top[:, u % 2], [[1, 12], [0, L]]), ALU.subtract).then_inc(s_sh[l], 1)
                    if u == 0 and l == 0:
                        mask_values(dve, 0, 0, s_vv)
                    if u >= 2:
                        v = u - 2
                        dve.wait_ge(s_cp[l], v + 1)
                        if l:
                            step(dve.reciprocal(view(pinv[:, v], [[3, 4], [1, 3]]), view(ps[:, 4 + v % 2, 0:1], [[51, 4], [1, 3]], 48)))
                            dve.tensor_tensor(view(ctxr[:, v, :], [[48, 4], [16, 3], [1, 16]]),
                                              view(ps[:, 4 + v % 2, 0:1], [[51, 4], [16, 3], [1, 16]]),
                                              view(pinv[:, v], [[3, 4], [1, 3], [0, 16]]), ALU.mult).then_inc(s_cn[l], 1)
                        else:
                            for b in range(2):
                                ins = dve.reciprocal(view(pinv[:, v], [[3, 2], [1, 3]], 6 * b),
                                                     view(ps[:, 4 + b, 0:1], [[D + 3, 2], [1, 3]], D))
                            step(ins)
                            for b in range(2):
                                ins = dve.tensor_tensor(view(ctxr[:, 4 * v + 2 * b, :], [[D, 2], [hw, 3], [1, hw]]),
                                                        view(ps[:, 4 + b, 0:1], [[D + 3, 2], [hw, 3], [1, hw]]),
                                                        view(pinv[:, v], [[3, 2], [1, 3], [0, hw]], 6 * b), ALU.mult)
                            ins.then_inc(s_cn[l], 1)
                    if l and u in (6, 8):
                        dve.wait_ge(s_hbo, 1)
                        residual((u - 6) // 2)
                        statistics((u - 6) // 2)
                if l == 0:
                    c4 = ctxT[:, :, 0:TOK].rearrange("p c (b k) -> p c b k", k=L)
                    q4 = kblk[:, :, 0:TOK].rearrange("p c (b k) -> p c b k", k=L)
                    spread = [[1, NI], [0, L]]
                    for half in range(2):
                        dve.wait_ge(s_ct[0], NPAIR // 2 * (half + 1))
                        b = slice(half * NI // 2, (half + 1) * NI // 2)
                        dve.tensor_reduce(gsum[:, :, b], c4[:, :, b], AX_X, ALU.add).then_inc(s_gs, 1)
                    dve.wait_ge(s_gp, 1)
                    step(dve.tensor_scalar(gvar[:], ps[0:CP, 7, 0:CC * NI].rearrange("p (c b) -> p c b", c=CC),
                                           1.0 / (64 * L), None, ALU.mult))
                    for c in range(CC):
                        dve.tensor_tensor(c4[:, c], c4[:, c], view(gvar[:, c], spread), ALU.subtract).then_inc(s_gc, 1)
                    for c in range(CC):
                        dve.wait_ge(s_gq, c + 1)
                        dve.tensor_reduce(gsum[:, c], q4[:, c], AX_X, ALU.add).then_inc(s_gs, 1)
                    dve.wait_ge(s_gp, 2)
                    dve.tensor_scalar(gvar[:], ps[0:CP, 7, 0:CC * NI].rearrange("p (c b) -> p c b", c=CC),
                                      1.0 / (64 * L), GN_EPS, ALU.mult, ALU.add).then_inc(s_gv, 1)
                    dve.wait_ge(s_gd, 1)
                    step(dve.reciprocal(grs[:], gstd[:]))
                    step(dve.tensor_tensor(gscale[:], grs[:], view(gnw[:], [[1, CC], [0, NI]]), ALU.mult))
                    for c in range(CC):
                        ins = dve.tensor_tensor(c4[:, c], c4[:, c], view(gscale[:, c], spread), ALU.mult)
                    step(ins)
                    for c in range(CC):
                        dve.tensor_scalar(ctxT[:, c, 0:TOK], ctxT[:, c, 0:TOK], gnb[:, c:c + 1], None, ALU.add).then_inc(s_gn, 1)
                for t in range(2 if l else 0, NT + 1):
                    if t < NT:
                        residual(t)
                    if t and not (l and t < 3):
                        ins = statistics(t - 1)
                step(ins)

            def choose(x, rows, which):
                step(dve.tensor_reduce(best[which][:, 0:rows], x, AX_X, ALU.max))
                b = view(best[which][:], [[1, rows], [0, 8]])
                step(dve.tensor_tensor(rank8[:, 0:rows], x, b, ALU.is_equal))
                first_of_equals(rows, which)

            def first_of_equals(rows, which):
                step(dve.scalar_tensor_tensor(out=rank8[:, 0:rows], in0=rank8[:, 0:rows], scalar=-8.0,
                                              in1=view(cst("eight"), [[0, rows], [1, 8]]), op0=ALU.mult, op1=ALU.add))
                step(dve.tensor_reduce(first[:, 0:rows], rank8[:, 0:rows], AX_X, ALU.min))
                step(dve.tensor_tensor(pick[which][:, 0:rows], rank8[:, 0:rows], view(first[:], [[1, rows], [0, 8]]), ALU.is_equal))

            def route(l):
                ne = E[l]
                dve.memset(mask_bf[LAST:128, NT - 1, 0:ne], 0.0)
                if l:
                    dve.wait_ge(s_rtw[1], 16 * 9)
                    step(dve.memset(logit[:], LOWEST))
                dve.wait_ge(s_lp[l], 1)

                def chosen(experts, group):
                    for t in range(NT):
                        n = min(128, TOK - 128 * t)
                        if l:
                            ins = dve.tensor_tensor(mask_bf[0:n, t, :].rearrange("p (g e) -> p g e", e=GE), experts(t)[0:n], group(t)[0:n], ALU.mult)
                        else:
                            ins = dve.tensor_copy(mask_bf[0:n, t, 0:ne], experts(t)[0:n])
                    ins.then_inc(s_mask[l], 1)

                if l == 0:
                    rows = NT
                    scores = ps[:, 5, 0:8 * NT].rearrange("p (t e) -> p t e", e=8)
                    step(dve.tensor_reduce(best[0][:, 0:rows], scores, AX_X, ALU.max))
                    top1 = view(best[0][:], [[1, rows], [0, 8]])
                    dve.tensor_tensor(gated[:, 0:rows], scores, top1, ALU.subtract).then_inc(s_rx[0], 1)
                    step(dve.tensor_tensor(rank8[:, 0:rows], scores, top1, ALU.is_equal))
                    first_of_equals(rows, 0)
                    chosen(lambda t: pick[0][:, t, :], lambda t: None)
                    dve.wait_ge(s_re[0], 1)
                    step(dve.tensor_reduce(gate[0][:, 0:rows], pick[1][:, 0:rows], AX_X, ALU.add))
                    dve.reciprocal(gate[1][:, 0:rows], gate[0][:, 0:rows]).then_inc(s_gate[0], 1)
                else:
                    rows = NT * RW
                    l4 = logit[:].rearrange("p (t r) e -> p t r e", r=RW)
                    step(dve.tensor_tensor(l4[:, :, 0, 0:G], ps[:, 5, 0:36 * NT].rearrange("p (t e) -> p t e", t=NT)[:, :, 0:G],
                                           view(rbias[:], [[0, NT], [1, G]]), ALU.add))
                    for t in range(NT):
                        ins = dve.tensor_tensor(l4[:, t, 1:RW, :], ps[:, 5, 36 * t + G:36 * t + 36].rearrange("p (g e) -> p g e", e=GE),
                                                rbias[:, G:].rearrange("p (g e) -> p g e", e=GE), ALU.add)
                    step(ins)
                    choose(logit[:], rows, 0)
                    step(dve.scalar_tensor_tensor(out=logit[:].rearrange("p r e -> p (r e)"), in0=pick[0][:].rearrange("p r e -> p (r e)"),
                                                  scalar=LOWEST, in1=logit[:].rearrange("p r e -> p (r e)"), op0=ALU.mult, op1=ALU.add))
                    choose(logit[:], rows, 1)
                    dve.tensor_tensor(gate[0][:], best[1][:], best[0][:], ALU.subtract).then_inc(s_rx[1], 1)
                    step(dve.tensor_tensor(rank8[:], pick[0][:], pick[1][:], ALU.add))
                    chosen(lambda t: rank8[:, RW * t + 1:RW * t + RW, :], lambda t: view(rank8[:, RW * t], [[1, G], [0, GE]]))
                    dve.wait_ge(s_re[1], 1)
                    step(dve.tensor_scalar(gate[2][:], gate[1][:], 1.0, None, ALU.add))
                    dve.reciprocal(gate[3][:], gate[2][:]).then_inc(s_gate[1], 1)

            def list_jobs(l):
                ne = E[l]
                dve.wait_ge(s_rank[l], 1)
                step(dve.tensor_tensor(pos[:, :, 0:ne], ps[:, 6, 0:NT * ne].rearrange("p (t e) -> p t e", t=NT), mask_bf[:, :, 0:ne], ALU.mult))
                step(dve.tensor_tensor(over[:, 0:ne, :], view(ps[:, 6, NT * ne:NT * ne + 1], [[1, ne], [0, NCHUNK]]),
                                       view(cst("tile"), [[0, ne], [1, NCHUNK]]), ALU.is_gt))
                step(dve.tensor_reduce(nchunk[:, 0:ne], over[:, 0:ne, :], AX_X, ALU.add))
                step(dve.tensor_tensor_scan(ends[:, 0:ne], cst("ones")[:, 0:ne], nchunk[:, 0:ne], 0.0, ALU.mult, ALU.add))
                step(dve.tensor_scalar(before[:, 0, 0:ne], ends[:, 0:ne], cst("row"), None, ALU.is_le))
                step(dve.tensor_tensor(before[:, 1, 0:ne], before[:, 0, 0:ne], nchunk[:, 0:ne], ALU.mult))
                step(dve.tensor_reduce(job_t[:], before[:, :, 0:ne], AX_X, ALU.add))
                dve.tensor_scalar(job_e[:, 0:1], job_t[:, 0:1], float(ne - 1), None, ALU.min)
                step(dve.tensor_tensor(job_t[:, 1:2], cst("row"), job_t[:, 1:2], ALU.subtract))
                step(dve.scalar_tensor_tensor(out=job_t[:, 1:2], in0=before[:, 0, ne - 1:ne], scalar=float(NCHUNK), in1=job_t[:, 1:2],
                                              op0=ALU.mult, op1=ALU.add))
                dve.tensor_scalar(job_e[:, 1:2], job_t[:, 1:2], float(NCHUNK), 128.0, ALU.min, ALU.mult).then_inc(s_jcol[l], 1)
                dve.wait_ge(s_jrow[l], 1)
                dve.tensor_copy(njobs[:], ends[0:1, ne - 1:ne])
                dve.tensor_copy(jobs[:], ps[0:1, 7, 256:256 + 2 * JOBS]).then_inc(s_jobs[l], 1)

            def experts(l):
                dve.memset(yw[:, 1].bitcast(F32), 0.0).then_inc(s_yw[l], 1)
                dve.wait_ge(s_pad, 17)
                route(l)
                list_jobs(l)
                def select(j, s, begin=False):
                    e = job_expert(dve, l, j)
                    c = 0 if begin else dve.value_load(jobs[0:1, bass.ds(j + JOBS, 1)], min_val=0, max_val=128 * NCHUNK)
                    mine = pos[:, :, bass.ds(e, 1)].rearrange("p t e -> p (t e)")
                    slots = table[:, bass.ds(c + WHERE["count"][0], 128)]
                    dve.tensor_tensor(sel[:, s], view(mine, [[32, NT], [0, 128]]), view(slots, [[0, NT], [1, 128]]), ALU.is_equal)
                    if begin:
                        dve.wait_ge(s_weight[l], WEIGHT_STEPS[l])
                    dve.tensor_copy(info[:, s, :, 2:5], wparts[:, :, bass.ds(e, 1), :].rearrange("p t e w -> p t (e w)")).then_inc(s_sel[l], 1)

                def slots_of(j, s, extra=0):
                    dve.wait_ge(s_inf[l], j + 1)
                    dve.tensor_reduce(nxt[:, s, 1:2], ps[:, 7, 8 * s + 2:8 * s + 5], AX_X, ALU.add)
                    step(dve.tensor_reduce(nxt[:, s, 0:1], ps[:, 7, 8 * s:8 * s + 2], AX_X, ALU.add), extra)
                    dve.tensor_scalar(idx[:, s:s + 1], nxt[:, s, 0:1], -1.0, 0.0, ALU.add, ALU.max).then_inc(s_idx[l], 1)

                dve.wait_ge(s_jobs[l], 1)
                select(0, 0, begin=True)
                slots_of(0, 0)
                select(1, 1)
                slots_of(1, 1)
                select(2, 0)
                pairs = job_count(dve, l)
                next_stretch()
                per = 2 * 3
                with dve.Fori(0, pairs) as i:
                    for s in range(2):
                        j = i * 2 + s
                        step(dve.tensor_copy(cur[:, s, :], nxt[:, s, :]), i * per)
                        dve.tensor_scalar(selT[:, s, :], cst("count")[:, 0:NP], cur[:, s, 0:1], None, ALU.is_equal)
                        slots_of(j + 2, s, i * per)
                        select(j + 3, 1 - s)
                        dve.wait_ge(s_yp[l], j + 1)
                        y, w = ps[:, 5, D * s:D * s + D], cur[:, s, 1:2]
                        step(dve.tensor_scalar(yw[:, s, 0], y, w, None, ALU.mult), i * per)
                        dve.scalar_tensor_tensor(out=yw[:, s, 1], in0=y, scalar=w, in1=yw[:, s, 0].bitcast(F32),
                                                 op0=ALU.mult, op1=ALU.subtract).then_inc(s_yw[l], 1)
                assert steps == per
                next_stretch()
                dve.wait_ge(s_done[l], 1)
                for b in range(3):
                    tiles = range(2 * b, min(2 * b + 2, NT))
                    dve.tensor_tensor(h[:, tiles[0]:tiles[-1] + 1, :], ps[:, b, 0:len(tiles) * D].rearrange("p (t n) -> p t n", n=D),
                                      h[:, tiles[0]:tiles[-1] + 1, :], ALU.add).then_inc(s_hmoe[l], 1)
                    if l == 0:
                        dve.wait_ge(s_hmoe[l], b + 1)
                        for t in tiles:
                            ins = dve.bn_stats(stats[:, t, :], h[:, t, :])
                if l == 0:
                    step(ins)

            embed()
            norm(0)
            attention(0)
            norm(1)
            experts(0)
            norm(2)
            attention(1)
            norm(3)
            experts(1)

        @block.tensor
        def _(pe):
            def mm(o, a, b, start=True, stop=True):
                return pe.matmul(o, a, b, start=start, stop=stop, skip_group_check=True)

            def keep_warm(bank, n):
                for _ in range(n):
                    mm(ps[:, bank, :], zero_bf[:, 0:128], zero_bf[:])

            def norm(k):
                l = k // 2
                nl = G + E[1] if l else E[0]

                def logits(t):
                    pe.wait_ge(s_xt, NT * k + t + 1)
                    for ci in range(CC):
                        ins = mm(ps[:, 5, nl * t:nl * t + nl], xT[:, ci, t * 128:(t + 1) * 128], wr[l][:, ci, :], ci == 0, ci == CC - 1)
                    return ins

                keep_warm(5, WARM_NORM[k])
                if k % 2:
                    pe.wait_ge(s_rtw[l], 16 * (9 if l else 1))
                for t in range(NT):
                    n = NT * k + t
                    pe.wait_ge(s_xn, n + 1)
                    if t >= 2:
                        pe.wait_ge(s_xt, n - 1)
                    for c in range(CC):
                        ins = pe.transpose(ps[0:CP, 6 + t % 2, 128 * c:128 * c + 128], xn[:, t, CP * c:CP * c + CP], ident)
                    ins.then_inc(s_xtp, 1)
                    if t and k % 2:
                        logits(t - 1)
                if k % 2:
                    logits(NT - 1).then_inc(s_lp[l], 1)
                pe.wait_ge(s_xt, NT * (k + 1))

            def attention(l):
                nu, per = U[l], NPAIR // U[l]
                hk = 6 if l else 3
                pe.wait_ge(s_attw[l], 16 * (14 if l else 6))

                def project(w, bank, co, n):
                    for ci in range(CC):
                        ins = mm(ps[0:CP, bank, 0:HALF], w[l][:, ci, CP * co:CP * co + CP], xT[:, ci, n * HALF:(n + 1) * HALF],
                                 ci == 0, ci == CC - 1)
                    return ins

                for t in range(NT):
                    if t >= 2:
                        pe.wait_ge(s_vtr[l], t - 1)
                    for ci in range(CC):
                        ins = mm(ps[:, 4 + t % 2, 0:D], xT[:, ci, t * 128:(t + 1) * 128], wv[l][:, ci, :], ci == 0, ci == CC - 1)
                    ins.then_inc(s_vtp[l], 1)
                for m in range(4):
                    project(wq, m, m // 2, m % 2).then_inc(s_qp[l], 1)
                pe.wait_ge(s_q[l], 2)
                for n in range(2):
                    for co in range(CC):
                        project(wk, KEY_BANK[2 * co + n], co, n).then_inc(s_kp[l], 1)
                if l:
                    pe.wait_ge(s_q[l], 4)
                    pe.wait_ge(s_pad, 5)
                    pe.wait_ge(s_vtr[l], NT)
                    for r in range(CC * NT):
                        t, c = r // CC, r % CC
                        if r >= 2:
                            pe.wait_ge(s_rs, r - 1)
                        mm(ps[:, 4 + r % 2, 0:6 * W_REL], qT[:, c, t * 128:(t + 1) * 128],
                           emb_rev[:].rearrange("p h w -> p (h w)")).then_inc(s_rp, 1)

                def scores(u):
                    if u == 0:
                        pe.wait_ge(s_kv[l], 2 * hk if l else hk)
                        if l == 0:
                            pe.wait_ge(s_ka[0], hk)
                    if u == nu // 2 and l:
                        pe.wait_ge(s_kg, 2 * hk)
                    if u == nu // 2 and l == 0:
                        pe.wait_ge(s_kv[l], 2 * hk)
                        pe.wait_ge(s_ka[l], 2 * hk)
                    if u >= 2:
                        pe.wait_ge(s_sr[l], u - 1)
                    for g in range(per):
                        for i in range(2):
                            b = 2 * (u * per + g) + i
                            for c in range(CC):
                                q = qT[:, c, L * b:L * b + L]
                                k = kblk[:, c, b * hk * L:(b + 1) * hk * L]
                                if l:
                                    ins = mm(ps[64 * i:64 * i + L, u % 2, hk * L * c:hk * L * (c + 1)], q, k)
                                else:
                                    ins = mm(ps[64 * i:64 * i + L, u % 2, TR * g:TR * g + TR], q, k, c == 0, c == CC - 1)
                    ins.then_inc(s_sp[l], 1)

                def turn_probs(u):
                    pe.wait_ge(s_ex[l], u + 1)
                    if u >= 2:
                        pe.wait_ge(s_pt[l], u - 1)
                    for g in range(4):
                        ins = pe.transpose(ps[0:TR, 2 + u % 2, 128 * g:128 * g + 128], prob[:, u % 2, TR * g:TR * g + TR], ident)
                    ins.then_inc(s_ptp[l], 1)

                def context(u):
                    pe.wait_ge(s_pt[l], u + 1)
                    if u == 0:
                        pe.wait_ge(s_vv[l], 1)
                    if u == nu // 2:
                        pe.wait_ge(s_vp[l], 1)
                    if l and u >= 2:
                        pe.wait_ge(s_cn[l], u - 1)
                    if not l and u >= 1:
                        pe.wait_ge(s_cn[l], u)
                    for g in range(4):
                        for i in range(2):
                            p = probT[:, u % 2, 128 * g + 64 * i:128 * g + 64 * i + 64]
                            at, _, n = value_block(l, 2 * u + i if l else 2 * (4 * u + g) + i)
                            wide = n + 3
                            if l:
                                ins = mm(ps[64 * i:64 * i + 64, 4 + u % 2, wide * g:wide * (g + 1)], p, vblk[:, at + wide * g:at + wide * (g + 1)])
                            else:
                                ins = mm(ps[64 * i:64 * i + 64, 4 + g // 2, wide * (g % 2):wide * (g % 2 + 1)], p, vblk[:, at:at + wide])
                    ins.then_inc(s_cp[l], 1)

                def turn_context(u):
                    pe.wait_ge(s_cn[l], u + 1)
                    for p in range(u * per, (u + 1) * per):
                        if l:
                            pe.wait_ge(s_ka[1], CC)
                            if p:
                                pe.wait_ge(s_ct[l], p)
                        elif p >= 2:
                            pe.wait_ge(s_ct[l], p - 1)
                        for c in range(CC):
                            ins = pe.transpose(ps[0:CP, 6 if l else 6 + p % 2, 128 * c:128 * c + 128], ctxr[:, p, CP * c:CP * c + CP], ident)
                        ins.then_inc(s_ctp[l], 1)

                def output(t):
                    if l and t:
                        pe.wait_ge(s_or[l], min(t, NT - 2))
                    elif t >= 2:
                        pe.wait_ge(s_or[l], t - 1)
                    for ci in range(CC):
                        ins = mm(ps[:, OUT_BANK[l][t], 0:D], ctxT[:, ci, t * 128:(t + 1) * 128], wo[l][:, ci, :], ci == 0, ci == CC - 1)
                    ins.then_inc(s_op[l], 1)

                for u in range(nu + 3):
                    if u < nu:
                        scores(u)
                    if u == 1:
                        keep_warm(3, WARM_SOFTMAX)
                    if 1 <= u <= nu:
                        turn_probs(u - 1)
                    if 2 <= u <= nu + 1:
                        context(u - 2)
                    if u >= 3:
                        turn_context(u - 3)
                    if l and u >= 5 and u % 2:
                        pe.wait_ge(s_ct[l], u - 3)
                        output((u - 5) // 2)
                if l == 0:
                    keep_warm(5, WARM_GROUPS[0])
                    for r in range(2):
                        pe.wait_ge(s_gs, 2 * r + 2)
                        same = cst("same", CP).rearrange("p (c d n) -> p c d n", c=CC, d=CC)
                        for d in range(CC):
                            for c in range(CC):
                                ins = mm(ps[0:CP, 7, NI * d:NI * d + NI], same[:, c, d, :], gsum[:, c, :], c == 0, c == CC - 1)
                        ins.then_inc(s_gp, 1)
                        keep_warm(6, WARM_GROUPS[1 + r])
                    pe.wait_ge(s_gn, CC)
                else:
                    pe.wait_ge(s_ct[l], NPAIR)
                for t in range(3 if l else 0, NT):
                    output(t)

            def experts(l):
                ne = E[l]
                pe.wait_ge(s_pad, 17)
                keep_warm(3, WARM_RANKS[l])
                pe.wait_ge(s_mask[l], 1)
                for t in range(NT):
                    for r in range(t + 1):
                        mm(ps[:, 6, ne * t:ne * t + ne], upto_bf[:] if r == t else ones_bf[:], mask_bf[:, r, 0:ne], r == 0, r == t)
                for r in range(NT):
                    ins = mm(ps[:, 6, NT * ne:(NT + 1) * ne], ones_bf[:], mask_bf[:, r, 0:ne], r == 0, r == NT - 1)
                ins.then_inc(s_rank[l], 1)
                keep_warm(3, WARM_LIST[l])
                pe.wait_ge(s_jcol[l], 1)
                for c in range(2):
                    ins = mm(ps[0:1, 7, 256 + JOBS * c:256 + JOBS * (c + 1)], job_e[:, c:c + 1], ident_bf[:])
                ins.then_inc(s_jrow[l], 1)
                if l:
                    pe.wait_ge(s_weight[1], 4)
                    for t in range(NT):
                        ins = pe.transpose(ps[0:32, 5 if t < 4 else 4, 128 * (t % 4):128 * (t % 4) + 128], comb[:, t, :], ident)
                    ins.then_inc(s_cbp, 1)

                if l:
                    pe.wait_ge(s_cbt, 2)
                for t in range(NT):
                    o = ps[:, t // 2, D * (t % 2):D * (t % 2) + D]
                    if l:
                        mm(o, combT[:, 128 * t:128 * t + 128], b2all[:], t % 2 == 0, False)
                    else:
                        mm(o, zero_bf[:, 0:128], zero_bf[:, 0:D], t % 2 == 0, False)

                def slots(j, s):
                    pe.wait_ge(s_sel[l], j + 1)
                    for t in range(NT):
                        ins = mm(ps[:, 7, 8 * s:8 * s + 5], sel[:, s, t, :], info[:, s, t, :], t == 0, t == NT - 1)
                    ins.then_inc(s_inf[l], 1)

                def turn(i, s):
                    pe.wait_ge(s_gat[l][s], i * 16 + 16)
                    for c in range(CC):
                        o = 256 * s + 128 * c
                        ins = pe.transpose(ps[0:CP, 6, o:o + 128], xg[:, s, CP * c:CP * c + CP], ident)
                    ins.then_inc(s_xgp[l], 1)

                def first(i, j, s):
                    pe.wait_ge(s_xg[l], j + 1)
                    pe.wait_ge(s_w1[l][s], i * 16 + 16)
                    for m in range(MC):
                        for ci in range(CC):
                            ins = mm(ps[:, 3 + m // 3, 128 * (m % 3):128 * (m % 3) + 128], w1[:, s, ci, 128 * m:128 * m + 128],
                                     xgT[:, s, ci, :], ci == 0, ci == CC - 1)
                        if m % 3 == 2:
                            ins.then_inc(s_hp[l], 1)

                def second(i, j, s):
                    pe.wait_ge(s_w2[l][s], i * 16 + 16)
                    for m in range(MC):
                        if m % 3 == 0:
                            pe.wait_ge(s_hd[l], j * 2 + 1 + m // 3)
                        ins = mm(ps[:, 5, D * s:D * s + D], hid[:, m, :], w2[:, s, m, :], m == 0, m == MC - 1)
                    ins.then_inc(s_yp[l], 1)

                def scatter(j, s):
                    pe.wait_ge(s_yw[l], j + 2)
                    for t in range(NT):
                        n = min(128, TOK - 128 * t)
                        for part in range(2):
                            ins = mm(ps[0:n, t // 2, D * (t % 2):D * (t % 2) + D], selT[:, s, 128 * t:128 * t + n],
                                     yw[:, s, part], False, False)
                    return ins

                pe.wait_ge(s_jobs[l], 1)
                slots(0, 0)
                pe.wait_ge(s_idx[l], 1)
                slots(1, 1)
                pairs = job_count(pe, l)
                turn(0, 0)
                with pe.Fori(0, pairs) as i:
                    for s in range(2):
                        j = i * 2 + s
                        first(i, j, s)
                        scatter(j - 1, 1 - s)
                        slots(j + 2, s)
                        turn(i + s, 1 - s)
                        second(i, j, s)
                scatter(pairs * 2 - 1, 1).then_inc(s_done[l], 1)
                pe.wait_ge(s_gat[l][1], pairs * 16 + 16)
                for q in (s_w1[l], s_w2[l]):
                    for s in range(2):
                        pe.wait_ge(q[s], pairs * 16 + 16)

            pe.wait_ge(s_pad, 2)
            pe.wait_ge(s_step[0], 1)
            for k in range(KF):
                pe.wait_ge(s_patch[k], 32)
                for t in range(NT):
                    ins = mm(ps[:, t, 0:D], patches[:, k, t * 128:(t + 1) * 128], tok_w[:, k, :], k == 0, k == KF - 1)
                    if k == KF - 1:
                        ins.then_inc(s_emb, 1)
            pe.wait_ge(s_table, 16)
            pe.wait_ge(s_pad, 10)
            norm(0)
            attention(0)
            norm(1)
            experts(0)
            norm(2)
            attention(1)
            norm(3)
            experts(1)


def kernel(**inputs):
    import concourse.bacc as bacc
    from concourse.bass_utils import run_bass_kernel_spmd

    a = {k: np.ascontiguousarray(v) for k, v in inputs.items()}
    n = IMG // PATCH
    x = a.pop("x").reshape(NI, NCH, n, PATCH, n, PATCH)
    a["patchesT"] = x.transpose(1, 3, 5, 0, 2, 4).reshape(FLAT, TOK)
    a["tok_WT"] = a.pop("L0_tok_W").T
    a["pos"] = np.tile(a.pop("L0_tok_pos_emb"), (NI, 1))
    for w in ("Wq", "Wk", "Wv", "Wo"):
        a[w + "T0"] = a.pop("L0_attn_" + w).T
    distance = np.clip(L - 1 - np.arange(W_REL), -MAX_REL, MAX_REL) + MAX_REL
    a["emb_rev"] = a.pop("L1_attn_rel_emb")[distance].T
    a["b1T"] = a.pop("L1_ffn_b1").reshape(E[1], MC, 128).transpose(2, 0, 1)
    for name in ("L0_attn_gn_weight", "L0_attn_gn_bias", "L1_attn_bq", "L1_attn_bk"):
        a[name] = a[name].reshape(CC, CP).T
    a["table"] = TABLE
    nc = bacc.Bacc("TRN2", target_bir_lowering=False, num_devices=1)
    arrays, aps = {}, {}
    for name, v in a.items():
        arrays["in_" + name] = v = np.ascontiguousarray(v)
        aps[name] = nc.dram_tensor("in_" + name, v.shape, mybir.dt.from_np(v.dtype), kind="ExternalInput").ap()
    out = nc.dram_tensor("tower_out", (TOK, D), F32, kind="ExternalOutput").ap()
    vit_tower(nc, aps, out)
    r = run_bass_kernel_spmd(nc, [arrays], core_ids=[0])
    return r.results[0]["tower_out"].reshape(NI, L, D)
```
